# Optimizing a Trainium2 kernel written in Bass

```python
import numpy as np
import jax
import jax.numpy as jnp

def _softmax(x, axis=-1):
    return jax.nn.softmax(x, axis=axis)

def _gelu(x):
    return jax.nn.gelu(x, approximate=True)

def _silu(x):
    return jax.nn.silu(x)

def _sigmoid(x):
    return jax.nn.sigmoid(x)

def _layernorm(x, axis=-1, eps=1e-05):
    m = jnp.mean(x, axis=axis, keepdims=True)
    v = jnp.var(x, axis=axis, keepdims=True)
    return (x - m) / jnp.sqrt(v + eps)

def _scatter_add(tgt, idx, src, axis=0):
    return tgt.at[idx].add(src)

def _segment_sum(src, seg, n):
    return jax.ops.segment_sum(src, seg, n)
kernel_name = 'mk_flamingo_gated_d2_seqx_r8_cc55f9'

def setup_inputs(seed: int=0):
    np.random.seed(seed)
    _w = jnp.asarray

    def _rec_inputs():
        import jax
        import jax.numpy as jnp
        _rk = jax.random.key(seed)
        x = -0.0002928 + 1 * jax.random.normal(jax.random.fold_in(_rk, 1), (16, 128, 128), jnp.float32)
        _lenS = 128 - jax.random.randint(jax.random.fold_in(_rk, 7), (16,), 0, max(1, 128 // 4) + 1, jnp.int32)
        _lenS2 = 128 - jax.random.randint(jax.random.fold_in(_rk, 8), (16,), 0, max(1, 128 // 4) + 1, jnp.int32)
        _ctx_1024P = jax.random.normal(jax.random.fold_in(_rk, 11), (16, 16, 128), jnp.float32)
        _ctx_1024c = jax.random.dirichlet(jax.random.fold_in(_rk, 511), 0.3 * jnp.ones((16,), jnp.float32), (16, 128))
        _ctx_1024t = jnp.einsum('bsk,bkd->bsd', _ctx_1024c, _ctx_1024P)
        _ctx_1024t = _ctx_1024t * jax.lax.rsqrt(jnp.mean(jnp.square(_ctx_1024t)) + 1e-12) * 0.953939
        ctx_1024 = -1.39393e-06 + 0.999914 * (_ctx_1024t + 0.3 * jax.random.normal(jax.random.fold_in(_rk, 611), (16, 128, 128), jnp.float32))
        _validS = jnp.arange(128)[None, :] < _lenS[:, None]
        _validS2 = jnp.arange(128)[None, :] < _lenS2[:, None]
        _causal = jnp.tril(jnp.ones((128, 128), dtype=bool))
        mask_BxS2_bf0 = jnp.logical_not(jnp.ones((16, 128), dtype=bool))
        _g = jax.random.normal(jax.random.fold_in(_rk, 9001), (2, 2), jnp.float32)
        _g = jnp.sign(_g) * jnp.maximum(jnp.abs(_g), 1.0) + (_g == 0) * 1.0
        g_xattn = _g[0]
        g_ffn = _g[1]
        return (x, ctx_1024, mask_BxS2_bf0, g_xattn, g_ffn)
    x, ctx_1024, mask_BxS2_bf0, g_xattn, g_ffn = _rec_inputs()

    def _L0_xattn_setup():
        import jax, jax.numpy as jnp
        import numpy as np
        D_MODEL = 128
        NUM_HEADS = 16
        D_K = D_MODEL // NUM_HEADS
        key = jax.random.key(seed)
        ks = jax.random.split(key, 11)
        B, S, D = (2, 256, D_MODEL)
        scale = 1.0 / np.sqrt(D)
        inp = {'query': jax.random.normal(ks[0], (B, S, D), jnp.float32), 'key': jax.random.normal(ks[1], (B, S, D), jnp.float32), 'value': jax.random.normal(ks[2], (B, S, D), jnp.float32), 'Wq': jax.random.normal(ks[3], (D, D), jnp.float32) * scale, 'bq': jnp.zeros((D,), jnp.float32), 'Wk': jax.random.normal(ks[4], (D, D), jnp.float32) * scale, 'bk': jnp.zeros((D,), jnp.float32), 'Wv': jax.random.normal(ks[5], (D, D), jnp.float32) * scale, 'bv': jnp.zeros((D,), jnp.float32), 'Wo': jax.random.normal(ks[6], (D, D), jnp.float32) * scale, 'bo': jnp.zeros((D,), jnp.float32)}
        return inp
    _L0_xattn_all = _L0_xattn_setup()
    _L0_xattn_in = {k: v for k, v in _L0_xattn_all.items() if k in ('Wq', 'bq', 'Wk', 'bk', 'Wv', 'bv', 'Wo', 'bo')}
    del _L0_xattn_all

    def _L0_ffn_setup():
        import jax, jax.numpy as jnp
        import numpy as np
        H, F, E_SHARED, E_ROUTED, K = (128, 512, 1, 8, 2)

        def _expert(x, w_up, w_down):
            h = jax.nn.gelu(jnp.einsum('bsh,hf->bsf', x, w_up), approximate=False)
            return jnp.einsum('bsf,fh->bsh', h, w_down)
        key = jax.random.key(seed)
        ks = jax.random.split(key, 6)
        x = jax.random.normal(ks[0], (4, 256, H), dtype=jnp.float32)
        s = 0.02
        shared_up = jax.random.normal(ks[1], (E_SHARED, H, F), dtype=jnp.float32) * s
        shared_down = jax.random.normal(ks[2], (E_SHARED, F, H), dtype=jnp.float32) * s
        routed_up = jax.random.normal(ks[3], (E_ROUTED, H, F), dtype=jnp.float32) * s
        routed_down = jax.random.normal(ks[4], (E_ROUTED, F, H), dtype=jnp.float32) * s
        router_w = jax.random.normal(ks[5], (H, E_ROUTED), dtype=jnp.float32) * s
        return {'x': x, 'shared_up': shared_up, 'shared_down': shared_down, 'routed_up': routed_up, 'routed_down': routed_down, 'router_w': router_w}
    _L0_ffn_all = _L0_ffn_setup()
    _L0_ffn_in = {k: v for k, v in _L0_ffn_all.items() if k in ('shared_up', 'shared_down', 'routed_up', 'routed_down', 'router_w')}
    del _L0_ffn_all

    def _L1_xattn_setup():
        import jax, jax.numpy as jnp
        import numpy as np
        DIM = 128
        HEADS = 16
        DIM_HEAD = 64
        INNER = HEADS * DIM_HEAD
        B, N = (2, 256)
        SCALE = DIM_HEAD ** (-0.5)
        key = jax.random.key(seed)
        ks = jax.random.split(key, 9)
        s_in = 1.0 / np.sqrt(DIM)
        s_inner = 1.0 / np.sqrt(INNER)
        return {'q': jax.random.normal(ks[0], (B, N, DIM), jnp.float32), 'k': jax.random.normal(ks[1], (B, N, DIM), jnp.float32), 'v': jax.random.normal(ks[2], (B, N, DIM), jnp.float32), 'Wq': jax.random.normal(ks[3], (DIM, INNER), jnp.float32) * s_in, 'Wk': jax.random.normal(ks[4], (DIM, INNER), jnp.float32) * s_in, 'Wv': jax.random.normal(ks[5], (DIM, INNER), jnp.float32) * s_in, 'Wo': jax.random.normal(ks[6], (INNER, DIM), jnp.float32) * s_inner, 'bo': jax.random.normal(ks[7], (DIM,), jnp.float32) * s_inner, 'mask': jnp.zeros((B, N), dtype=bool)}
    _L1_xattn_all = _L1_xattn_setup()
    _L1_xattn_in = {k: v for k, v in _L1_xattn_all.items() if k in ('Wq', 'Wk', 'Wv', 'Wo', 'bo')}
    del _L1_xattn_all

    def _L1_ffn_setup():
        import jax, jax.numpy as jnp
        import numpy as np
        TOP_K = 2
        key = jax.random.key(seed)
        ks = jax.random.split(key, 5)
        B, S, D, E = (4, 256, 128, 8)
        H = 4 * D
        scale = 0.02
        return {'x': jax.random.normal(ks[0], (B, S, D), dtype=jnp.float32), 'gate_w': jax.random.normal(ks[1], (E, D), dtype=jnp.float32) * scale, 'gate_b': jnp.zeros((E,), dtype=jnp.float32), 'w1': jax.random.normal(ks[2], (E, H, D), dtype=jnp.float32) * scale, 'b1': jnp.zeros((E, H), dtype=jnp.float32), 'w2': jax.random.normal(ks[3], (E, D, H), dtype=jnp.float32) * scale, 'b2': jnp.zeros((E, D), dtype=jnp.float32)}
    _L1_ffn_all = _L1_ffn_setup()
    _L1_ffn_in = {k: v for k, v in _L1_ffn_all.items() if k in ('gate_w', 'gate_b', 'w1', 'b1', 'w2', 'b2')}
    del _L1_ffn_all
    return {'x': x, 'ctx_1024': ctx_1024, 'mask_BxS2_bf0': mask_BxS2_bf0, 'g_xattn': g_xattn, 'g_ffn': g_ffn, 'L0_xattn_Wq': _L0_xattn_in['Wq'], 'L0_xattn_bq': _L0_xattn_in['bq'], 'L0_xattn_Wk': _L0_xattn_in['Wk'], 'L0_xattn_bk': _L0_xattn_in['bk'], 'L0_xattn_Wv': _L0_xattn_in['Wv'], 'L0_xattn_bv': _L0_xattn_in['bv'], 'L0_xattn_Wo': _L0_xattn_in['Wo'], 'L0_xattn_bo': _L0_xattn_in['bo'], 'L0_ffn_shared_up': _L0_ffn_in['shared_up'], 'L0_ffn_shared_down': _L0_ffn_in['shared_down'], 'L0_ffn_routed_up': _L0_ffn_in['routed_up'], 'L0_ffn_routed_down': _L0_ffn_in['routed_down'], 'L0_ffn_router_w': _L0_ffn_in['router_w'], 'L1_xattn_Wq': _L1_xattn_in['Wq'], 'L1_xattn_Wk': _L1_xattn_in['Wk'], 'L1_xattn_Wv': _L1_xattn_in['Wv'], 'L1_xattn_Wo': _L1_xattn_in['Wo'], 'L1_xattn_bo': _L1_xattn_in['bo'], 'L1_ffn_gate_w': _L1_ffn_in['gate_w'], 'L1_ffn_gate_b': _L1_ffn_in['gate_b'], 'L1_ffn_w1': _L1_ffn_in['w1'], 'L1_ffn_b1': _L1_ffn_in['b1'], 'L1_ffn_w2': _L1_ffn_in['w2'], 'L1_ffn_b2': _L1_ffn_in['b2']}

def reference(x, ctx_1024, mask_BxS2_bf0, g_xattn, g_ffn, L0_xattn_Wq, L0_xattn_bq, L0_xattn_Wk, L0_xattn_bk, L0_xattn_Wv, L0_xattn_bv, L0_xattn_Wo, L0_xattn_bo, L0_ffn_shared_up, L0_ffn_shared_down, L0_ffn_routed_up, L0_ffn_routed_down, L0_ffn_router_w, L1_xattn_Wq, L1_xattn_Wk, L1_xattn_Wv, L1_xattn_Wo, L1_xattn_bo, L1_ffn_gate_w, L1_ffn_gate_b, L1_ffn_w1, L1_ffn_b1, L1_ffn_w2, L1_ffn_b2):
    import jax
    import jax.numpy as jnp

    def _L0_xattn_ref(query, key, value, Wq, bq, Wk, bk, Wv, bv, Wo, bo):
        import jax, jax.numpy as jnp
        import numpy as np
        D_MODEL = 128
        NUM_HEADS = 16
        D_K = D_MODEL // NUM_HEADS
        B, S, D = query.shape
        H, dk = (NUM_HEADS, D_K)
        Q = (query @ Wq.T + bq).reshape(B, S, H, dk).transpose(0, 2, 1, 3)
        K = (key @ Wk.T + bk).reshape(B, S, H, dk).transpose(0, 2, 1, 3)
        V = (value @ Wv.T + bv).reshape(B, S, H, dk).transpose(0, 2, 1, 3)
        scores = jnp.einsum('bhqd,bhkd->bhqk', Q, K) / jnp.sqrt(jnp.float32(dk))
        attn = jax.nn.softmax(scores, axis=-1)
        out = jnp.einsum('bhqk,bhkd->bhqd', attn, V)
        out = out.transpose(0, 2, 1, 3).reshape(B, S, D)
        return out @ Wo.T + bo

    def _L0_ffn_ref(x, shared_up, shared_down, routed_up, routed_down, router_w):
        import jax, jax.numpy as jnp
        import numpy as np
        H, F, E_SHARED, E_ROUTED, K = (128, 512, 1, 8, 2)

        def _expert(x, w_up, w_down):
            h = jax.nn.gelu(jnp.einsum('bsh,hf->bsf', x, w_up), approximate=False)
            return jnp.einsum('bsf,fh->bsh', h, w_down)
        shared_out = jnp.zeros_like(x)
        for i in range(E_SHARED):
            shared_out = shared_out + _expert(x, shared_up[i], shared_down[i])
        probs = jax.nn.softmax(jnp.einsum('bsh,he->bse', x, router_w), axis=-1)
        top_k_prob, top_k_idx = jax.lax.top_k(probs, K)
        onehot = jax.nn.one_hot(top_k_idx, E_ROUTED, dtype=x.dtype)
        gates = jnp.einsum('bsk,bske->bse', top_k_prob, onehot)
        routed_out = jnp.zeros_like(x)
        for e in range(E_ROUTED):
            y = _expert(x, routed_up[e], routed_down[e])
            routed_out = routed_out + gates[..., e:e + 1] * y
        return shared_out + routed_out + x

    def _L1_xattn_ref(q, k, v, Wq, Wk, Wv, Wo, bo, mask):
        import jax, jax.numpy as jnp
        import numpy as np
        DIM = 128
        HEADS = 16
        DIM_HEAD = 64
        INNER = HEADS * DIM_HEAD
        B, N = (2, 256)
        SCALE = DIM_HEAD ** (-0.5)
        b, n, _ = q.shape
        h, d = (HEADS, DIM_HEAD)

        def split_heads(x):
            return x.reshape(b, n, h, d).transpose(0, 2, 1, 3)
        qh = split_heads(q @ Wq)
        kh = split_heads(k @ Wk)
        vh = split_heads(v @ Wv)
        dots = jnp.einsum('bhid,bhjd->bhij', qh, kh) * SCALE
        mask_value = -jnp.finfo(dots.dtype).max
        dots = jnp.where(mask[:, None, None, :], mask_value, dots)
        causal = jnp.triu(jnp.ones((n, n), dtype=bool), k=1)
        dots = jnp.where(causal[None, None, :, :], mask_value, dots)
        attn = jax.nn.softmax(dots, axis=-1)
        out = jnp.einsum('bhij,bhjd->bhid', attn, vh)
        out = out.transpose(0, 2, 1, 3).reshape(b, n, h * d)
        return out @ Wo + bo

    def _L1_ffn_ref(x, gate_w, gate_b, w1, b1, w2, b2):
        import jax, jax.numpy as jnp
        import numpy as np
        TOP_K = 2
        B, S, D = x.shape
        E = gate_w.shape[0]
        logits = jnp.einsum('bsd,ed->bse', x, gate_w) + gate_b
        scores = jax.nn.softmax(logits, axis=-1)
        topk_scores, topk_idx = jax.lax.top_k(scores, TOP_K)
        onehot = jax.nn.one_hot(topk_idx, E, dtype=scores.dtype)
        dispatch = jnp.einsum('bsk,bske->bse', topk_scores, onehot)
        x_flat = x.reshape(B * S, D)
        w_flat = dispatch.reshape(B * S, E)
        out = jnp.zeros_like(x_flat)
        for i in range(E):
            wi = w_flat[:, i:i + 1]
            h = jax.nn.relu(jnp.einsum('nd,hd->nh', x_flat * wi, w1[i]) + b1[i])
            y = jnp.einsum('nh,dh->nd', h, w2[i]) + b2[i]
            out = jnp.where(wi > 0, y, out)
        return out.reshape(B, S, D)
    x = x + jnp.tanh(g_xattn[0]) * _L0_xattn_ref(_layernorm(x, axis=-1), ctx_1024, ctx_1024, L0_xattn_Wq, L0_xattn_bq, L0_xattn_Wk, L0_xattn_bk, L0_xattn_Wv, L0_xattn_bv, L0_xattn_Wo, L0_xattn_bo)
    x = x + jnp.tanh(g_ffn[0]) * _L0_ffn_ref(_layernorm(x, axis=-1), L0_ffn_shared_up, L0_ffn_shared_down, L0_ffn_routed_up, L0_ffn_routed_down, L0_ffn_router_w)
    x = x + jnp.tanh(g_xattn[1]) * _L1_xattn_ref(_layernorm(x, axis=-1), ctx_1024, ctx_1024, L1_xattn_Wq, L1_xattn_Wk, L1_xattn_Wv, L1_xattn_Wo, L1_xattn_bo, mask_BxS2_bf0)
    x = x + jnp.tanh(g_ffn[1]) * _L1_ffn_ref(_layernorm(x, axis=-1), L1_ffn_gate_w, L1_ffn_gate_b, L1_ffn_w1, L1_ffn_b1, L1_ffn_w2, L1_ffn_b2)
    return x

_drawn_inputs = setup_inputs


def setup_inputs(seed=0):
    import zlib

    import numpy as np

    out = dict(_drawn_inputs(seed))
    spreads = {'g_ffn': (-1.0, 0.6),
     'L0_xattn_bq': (0.0, 0.401),
     'L0_xattn_bk': (0.0, 0.8),
     'L0_xattn_bv': (0.0, 0.1),
     'L0_xattn_bo': (0.0, 0.1),
     'L1_ffn_gate_b': (0.0, 0.1),
     'L1_ffn_b1': (0.0, 0.1),
     'L1_ffn_b2': (0.0, 0.1)}
    factors = {'L1_ffn_w1': 4.036}
    for name, (base, spread) in spreads.items():
        noise = np.random.default_rng([zlib.crc32(name.encode()), seed]).standard_normal(out[name].shape)
        drawn = base * np.exp(spread * noise) if base else spread * noise
        out[name] = jnp.asarray(drawn.astype(out[name].dtype))
    for name, factor in factors.items():
        out[name] = (out[name] * factor).astype(out[name].dtype)
    return out
```

```python
from contextlib import ExitStack

import numpy as np

import concourse.bass as bass
from concourse import mybir

F32 = mybir.dt.float32
U8 = mybir.dt.uint8
ALU = mybir.AluOpType
ACT = mybir.ActivationFunctionType
AX = mybir.AxisListType.X

B, S, D = 16, 128, 128
HEADS = 16
DK = D // HEADS
DH = 64
INNER = HEADS * DH
F = 512
FC = F // 128
E = 8
G = 4
U = HEADS // G
PAIRS = B // 2
GROUPS = 4
GB = B // GROUPS
GT = GB * S
EPS = 1e-5
FMAX = float(np.finfo(np.float32).max)


class Tools:

    def __init__(self, nc, ctx, tag):
        self.nc, self.ctx, self.tag = nc, ctx, tag

    def sb(self, name, shape, dt=F32):
        return self.ctx.enter_context(self.nc.sbuf_tensor(f"{self.tag}_{name}", shape, dt))

    def ps(self, name, shape, dt=F32):
        return self.ctx.enter_context(self.nc.psum_tensor(f"{self.tag}_{name}", shape, dt))

    def sem(self, name):
        return self.ctx.enter_context(self.nc.semaphore(f"{self.tag}_{name}"))


def wide(ap, n):
    return ap.unsqueeze(2).to_broadcast([ap.shape[0], ap.shape[1], n])


def rows(ap, m):
    return ap.unsqueeze(1).to_broadcast([ap.shape[0], m, ap.shape[1]])


def start_phase(nc, k, w):
    with ExitStack() as ctx:
        t = Tools(nc, ctx, "start")
        loaded = t.sem("loaded")
        x_loaded = t.sem("x_loaded")
        tanh_done = t.sem("tanh_done")
        block = ctx.enter_context(nc.Block())

        @block.sync
        def _(sp):
            sp.dma_start(k.x[:, :, :], w["xr"]).then_inc(x_loaded, 16)
            sp.dma_start(k.graw[:, 0:2], w["g_xattn"].partition_broadcast(128)).then_inc(loaded, 16)
            sp.dma_start(k.graw[:, 2:4], w["g_ffn"].partition_broadcast(128)).then_inc(loaded, 16)
            sp.dma_start(k.ident[:, :], w["ident"]).then_inc(loaded, 16)

        @block.scalar
        def _(act):
            act.wait_ge(loaded, 48)
            nc.scalar.activation(k.tg[:, :], k.graw[:, :], ACT.Tanh).then_inc(tanh_done, 1)
            act.wait_ge(tanh_done, 1)

        @block.vector
        def _(dve):
            nc.vector.memset(k.half[:, :], -0.5)
            dve.wait_ge(x_loaded, 16)
            with dve.Fori(0, B) as b:
                nc.vector.bn_stats(k.stats[:, b, :], k.x[:, b, :])


def norm_stats(nc, dve, k, own, ready):
    m0, m1 = k.stats[:, :, 1], k.stats[:, :, 4]
    v0, v1 = k.stats[:, :, 2], k.stats[:, :, 5]
    nc.vector.tensor_tensor(k.mean[:, :], m0, m1, ALU.add).then_inc(own, 1)
    nc.vector.tensor_tensor(k.diff[:, :], m0, m1, ALU.subtract).then_inc(own, 1)
    nc.vector.tensor_tensor(k.var[:, :], v0, v1, ALU.add).then_inc(own, 1)
    dve.wait_ge(own, 3)
    nc.vector.tensor_scalar(k.mean[:, :], k.mean[:, :], 0.5, None, ALU.mult).then_inc(own, 1)
    nc.vector.tensor_tensor(k.diff[:, :], k.diff[:, :], k.diff[:, :], ALU.mult).then_inc(own, 1)
    nc.vector.tensor_scalar(k.var[:, :], k.var[:, :], 1.0 / D, EPS, ALU.mult, ALU.add).then_inc(own, 1)
    dve.wait_ge(own, 6)
    nc.vector.scalar_tensor_tensor(out=k.var[:, :], in0=k.diff[:, :], scalar=0.25, in1=k.var[:, :],
                                   op0=ALU.mult, op1=ALU.add).then_inc(ready, 1)


def attention_phase(nc, k, w, layer):
    first = layer == 0
    scale = float(np.float32(1.0) / np.sqrt(np.float32(DK if first else DH)))
    OC = 1 if first else HEADS * DH // 128
    gate = 2 * 0 + layer

    with ExitStack() as ctx:
        t = Tools(nc, ctx, f"att{layer}")
        wo = t.sb("wo", [128, OC, D])
        bo = t.sb("bo", [128, D])
        if first:
            wq, wk, wv = t.sb("wq", [128, D]), t.sb("wk", [128, D]), t.sb("wv", [128, D])
            bqkv = t.sb("bqkv", [128, 3])
            headmask = t.sb("headmask", [128, G])
            ones = t.sb("ones", [128, G, U, G, DK])
            bv = t.sb("bv", [128, S])
            oinv = [t.sb(f"oinv{i}", [128, S]) for i in range(2)]
        else:
            wqT, wkT = t.sb("wqT", [DH, HEADS, D]), t.sb("wkT", [DH, HEADS, D])
            wv = t.sb("wv", [128, INNER])
            wqk = t.sb("wqk", [128, HEADS, D])
            causal = t.sb("causal", [128, S])
            hidden = t.sb("hidden", [128, B, S], U8)
        ctxT = [t.sb(f"ctxT{i}", [128, S]) for i in range(2)]
        xn = [t.sb(f"xn{i}", [128, D]) for i in range(2)]
        xnT = [t.sb(f"xnT{i}", [128, S]) for i in range(2)]
        if first:
            qT = [t.sb(f"qT{i}", [128, U, S]) for i in range(2)]
            kraw = [t.sb(f"kraw{i}", [128, S]) for i in range(2)]
            kT = [t.sb(f"kT{i}", [128, G, S]) for i in range(2)]
            v = [t.sb(f"v{i}", [128, G, U, G, DK]) for i in range(2)]
        else:
            qT = [t.sb(f"qT{i}", [128, HEADS, S]) for i in range(2)]
            v = [t.sb(f"v{i}", [128, INNER]) for i in range(2)]
            bias = [t.sb(f"bias{i}", [128, S]) for i in range(2)]
        oT = [t.sb(f"oT{i}", [128, OC, S]) for i in range(2)]
        probs = [t.sb(f"probs{i}", [128, G, S]) for i in range(2 * U)]
        top = [t.sb(f"top{i}", [128, G]) for i in range(2 * U)]
        total = [t.sb(f"total{i}", [128, G]) for i in range(2 * U)]
        inv = [t.sb(f"inv{i}", [128, G]) for i in range(2 * U)]
        pT = [t.sb(f"pT{i}", [128, G, S]) for i in range(2)]
        sc_ps = [t.ps(f"sc_ps{i}", [128, G, S]) for i in range(2)]
        t_ps = [t.ps(f"t_ps{i}", [128, G, S]) for i in range(2)]
        q_ps = t.ps("q_ps", [128, G, S])
        kv_ps = t.ps("kv_ps", [128, G, S])
        o_ps = t.ps("o_ps", [128, G, S])
        y_ps = t.ps("y_ps", [128, G, S])

        weights = t.sem("weights")
        ctx_in = [t.sem(f"ctx_in{i}") for i in range(2)]
        norm_own = t.sem("norm_own")
        var_ready = t.sem("var_ready")
        rstd_ready = t.sem("rstd_ready")
        base_own = t.sem("base_own")
        base_ready = t.sem("base_ready")
        zeros_set, ones_set = t.sem("zeros_set"), t.sem("ones_set")
        wqk_made, wqk_ready = t.sem("wqk_made"), t.sem("wqk_ready")
        xn_ready, xnT_made, xnT_ready = t.sem("xn_ready"), t.sem("xnT_made"), t.sem("xnT_ready")
        q_made, q_ready = t.sem("q_made"), t.sem("q_ready")
        k_made, kraw_ready, k_ready = t.sem("k_made"), t.sem("kraw_ready"), t.sem("k_ready")
        v_made, v_ready = t.sem("v_made"), t.sem("v_ready")
        bias_ready = t.sem("bias_ready")
        sc_made, masked, top_ready, shifted = t.sem("sc_made"), t.sem("masked"), t.sem("top_ready"), t.sem("shifted")
        exp_done, total_ready, inv_ready = t.sem("exp_done"), t.sem("total_ready"), t.sem("inv_ready")
        probs_ready, pT_made, pT_ready = t.sem("probs_ready"), t.sem("pT_made"), t.sem("pT_ready")
        o_made, o_ready, oinv_ready = t.sem("o_made"), t.sem("o_ready"), t.sem("oinv_ready")
        bv_ready, bv_made, bo_full = t.sem("bv_ready"), t.sem("bv_made"), t.sem("bo_full")
        y_made, x_ready, stats_ready = t.sem("y_made"), t.sem("x_ready"), t.sem("stats_ready")
        block = ctx.enter_context(nc.Block())

        QE = 1 if first else U
        VE = 1 if first else 2

        def batch(i, par, ahead=0):
            return 2 * i + par + ahead, (par + ahead) % 2

        def turns(i, par, ahead):
            return i + (par + ahead) // 2

        @block.sync
        def _(sp):
            loads = [(wo[:, :, :], w[f"wo{layer}"]), (bo[:, :], w[f"bo{layer}"].partition_broadcast(128))]
            if first:
                loads += [(wq[:, :], w["wq0"]), (wk[:, :], w["wk0"]), (wv[:, :], w["wv0"]),
                          (bqkv[:, :], w["bqkv0"]), (headmask[:, :], w["headmask"])]
            else:
                loads += [(wqT[:, :, :], w["wqT1"]), (wkT[:, :, :], w["wkT1"]), (wv[:, :], w["wv1"]),
                          (causal[:, :], w["causal"]), (hidden[:, :, :], w["mask"].partition_broadcast(128))]
            for dst, src in loads:
                sp.dma_start(dst, src).then_inc(weights, 16)
            for par in range(2):
                sp.dma_start(ctxT[par][:, :], w["ctxT"][par]).then_inc(ctx_in[par], 16)
            with sp.Fori(1, PAIRS) as i:
                for par in range(2):
                    b, _p = batch(i, par)
                    if first:
                        sp.wait_ge(v_made, b - 1)
                    else:
                        sp.wait_ge(sc_made, U * (b - 1))
                    sp.dma_start(ctxT[par][:, :], w["ctxT"][b]).then_inc(ctx_in[par], 16)

        NW = 7 if first else 7

        @block.tensor
        def _(pe):
            def x_transpose(i, par, ahead):
                b, q = batch(i, par, ahead)
                pe.wait_ge(xn_ready, b + 1)
                if not (isinstance(b, int) and b == 0):
                    pe.wait_ge(q_ready, QE * b)
                nc.tensor.transpose(q_ps[:, 0, :], xn[q][:, :], k.ident[:, :]).then_inc(xnT_made, 1)

            def project_q(i, par, ahead, g):
                b, q = batch(i, par, ahead)
                pe.wait_ge(xnT_ready, b + 1)
                if first:
                    nc.tensor.matmul(q_ps[:, 0, :], wq[:, :], xnT[q][:, :], start=True, stop=True).then_inc(q_made, 1)
                    return
                if g or not (isinstance(b, int) and b == 0):
                    pe.wait_ge(q_ready, QE * b + g)
                for hh in range(G):
                    mm = nc.tensor.matmul(q_ps[:, hh, :], wqk[:, G * g + hh, :], xnT[q][:, :], start=True, stop=True)
                mm.then_inc(q_made, 1)

            def project_k(i, par, ahead):
                b, q = batch(i, par, ahead)
                pe.wait_ge(ctx_in[q], 16 * (turns(i, par, ahead) + 1))
                if not (isinstance(b, int) and b == 0):
                    pe.wait_ge(v_ready, b)
                nc.tensor.matmul(kv_ps[:, 0, :], wk[:, :], ctxT[q][:, :], start=True, stop=True).then_inc(k_made, 1)

            def project_v(i, par, ahead, half):
                b, q = batch(i, par, ahead)
                if first:
                    pe.wait_ge(kraw_ready, b + 1)
                    nc.tensor.matmul(kv_ps[:, 0, :], ctxT[q][:, :], wv[:, :], start=True, stop=True).then_inc(v_made, 1)
                    return
                pe.wait_ge(ctx_in[q], 16 * (turns(i, par, ahead) + 1))
                if half or not (isinstance(b, int) and b == 0):
                    pe.wait_ge(v_ready, VE * b + half)
                nc.tensor.matmul(kv_ps[:, :, :].rearrange("p a b -> p (a b)"), ctxT[q][:, :],
                                 wv[:, half * 512:half * 512 + 512], start=True, stop=True).then_inc(v_made, 1)

            def scores(i, par, ahead, g):
                b, q = batch(i, par, ahead)
                if first:
                    pe.wait_ge(q_ready, b + 1)
                    pe.wait_ge(k_ready, b + 1)
                else:
                    pe.wait_ge(q_ready, QE * b + g + 1)
                    pe.wait_ge(ctx_in[q], 16 * (turns(i, par, ahead) + 1))
                if g >= 2 or not (isinstance(b, int) and b == 0):
                    pe.wait_ge(shifted if first else masked, U * b + g - 1)
                if first:
                    nc.tensor.matmul(sc_ps[g % 2][:, :, :].rearrange("p a b -> p (a b)"), qT[q][:, g, :],
                                     kT[q][:, :, :].rearrange("p a b -> p (a b)"), start=True, stop=True).then_inc(sc_made, 1)
                    return
                for hh in range(G):
                    mm = nc.tensor.matmul(sc_ps[g % 2][:, hh, :], qT[q][:, G * g + hh, :], ctxT[q][:, :],
                                          start=True, stop=True)
                mm.then_inc(sc_made, 1)

            def turn_probs(i, par, g):
                b, q = batch(i, par)
                pe.wait_ge(exp_done if first else probs_ready, U * b + g + 1)
                if g >= 2 or not (isinstance(b, int) and b == 0):
                    pe.wait_ge(pT_ready, U * b + g - 1)
                for hh in range(G):
                    mm = nc.tensor.transpose(t_ps[g % 2][:, hh, :], probs[U * q + g][:, hh, :], k.ident[:, :])
                mm.then_inc(pT_made, 1)

            def values(i, par, ahead, g):
                b, q = batch(i, par, ahead)
                pe.wait_ge(pT_ready, U * b + g + 1)
                pe.wait_ge(v_ready, VE * b + VE)
                if first:
                    if g == 0 and not (isinstance(b, int) and b == 0):
                        pe.wait_ge(o_ready, b)
                    elif g == 0:
                        pe.wait_ge(ones_set, G)
                    for hh in range(G):
                        mm = nc.tensor.matmul(o_ps[32 * g:32 * g + 32, 0, :],
                                              v[q][:, hh, g, :, :].rearrange("p a b -> p (a b)"),
                                              pT[g % 2][:, hh, :], start=(hh == 0), stop=(hh == G - 1))
                    for hh in range(G):
                        mm = nc.tensor.matmul(o_ps[32 * g:32 * g + 32, 1, :],
                                              ones[:, hh, g, :, :].rearrange("p a b -> p (a b)"),
                                              pT[g % 2][:, hh, :], start=(hh == 0), stop=(hh == G - 1))
                else:
                    if g or not (isinstance(b, int) and b == 0):
                        pe.wait_ge(o_ready, U * b + g)
                    for hh in range(G):
                        h = G * g + hh
                        r = 64 * (hh % 2)
                        mm = nc.tensor.matmul(o_ps[r:r + 64, hh // 2, :], v[q][:, DH * h:DH * h + DH],
                                              pT[g % 2][:, hh, :], start=True, stop=True)
                mm.then_inc(o_made, 1)

            def project_out(i, par, ahead):
                b, q = batch(i, par, ahead)
                pe.wait_ge(o_ready, (b + 1) if first else U * (b + 1))
                if not (isinstance(b, int) and b == 0):
                    pe.wait_ge(x_ready, b)
                elif first:
                    pe.wait_ge(bo_full, 1)
                for c in range(OC):
                    mm = nc.tensor.matmul(y_ps[:, 0, :], oT[q][:, c, :], wo[:, c, :], start=(c == 0), stop=(c == OC - 1))
                mm.then_inc(y_made, 1)

            def pair(i, is_first, is_last):
                for par in range(2):
                    has_before = not (is_first and par == 0)
                    has_next = not (is_last and par == 1)
                    for g in range(U):
                        turn_probs(i, par, g)
                        if g:
                            values(i, par, 0, g - 1)
                        elif has_before:
                            values(i, par, -1, U - 1)
                        if g == 0 and not is_last:
                            x_transpose(i, par, 2)
                        if g == 1 and has_before:
                            project_out(i, par, -1)
                        if g == 1 and has_next:
                            project_v(i, par, 1, 0)
                        if g == 2 and has_next and not first:
                            project_v(i, par, 1, 1)
                        if not is_last:
                            if first:
                                if g == 1:
                                    project_q(i, par, 2, 0)
                                if g == 2:
                                    project_k(i, par, 2)
                            else:
                                if g:
                                    project_q(i, par, 2, g - 1)
                                if g == 3:
                                    project_q(i, par, 2, 3)
                        if g < U - 1:
                            if has_next:
                                scores(i, par, 1, g + 1)
                        elif not is_last:
                            scores(i, par, 2, 0)

            pe.wait_ge(weights, 16 * NW)
            if not first:
                for g in range(U):
                    if g >= 2:
                        pe.wait_ge(wqk_ready, g - 1)
                    for hh in range(G):
                        h = G * g + hh
                        mm = nc.tensor.matmul(sc_ps[g % 2][:, hh, :], wqT[:, h, :], wkT[:, h, :], start=True, stop=True)
                    mm.then_inc(wqk_made, 1)
                pe.wait_ge(wqk_ready, U)
            else:
                pe.wait_ge(bv_ready, 1)
                nc.tensor.matmul(y_ps[:, 0, :], bv[:, :], wo[:, 0, :], start=True, stop=True).then_inc(bv_made, 1)
                pe.wait_ge(zeros_set, 3)
            for par in range(2):
                x_transpose(0, par, 0)
                for g in range(QE):
                    project_q(0, par, 0, g)
                if first:
                    project_k(0, par, 0)
                if par == 0:
                    for half in range(VE):
                        project_v(0, par, 0, half)
            for g in range(U):
                scores(0, 0, 0, g)
            scores(0, 1, 0, 0)
            pair(0, True, False)
            with pe.Fori(1, PAIRS - 1) as i:
                pair(i, False, False)
            pair(PAIRS - 1, False, True)
            values(PAIRS, 0, -1, U - 1)
            project_out(PAIRS, 0, -1)

        @block.scalar
        def _(act):
            def take_xnT(i, par, ahead):
                b, q = batch(i, par, ahead)
                act.wait_ge(xnT_made, b + 1)
                if not (isinstance(i, int) and i == 0 and ahead == 0):
                    act.wait_ge(q_made, QE * (b - 1))
                nc.scalar.activation(xnT[q][:, :], q_ps[:, 0, :], ACT.Copy).then_inc(xnT_ready, 1)

            def take_k(i, par, ahead):
                b, q = batch(i, par, ahead)
                act.wait_ge(k_made, b + 1)
                if not (isinstance(i, int) and i == 0 and ahead == 0):
                    act.wait_ge(k_ready, b - 1)
                nc.scalar.activation(kraw[q][:, :], kv_ps[:, 0, :], ACT.Identity, bias=bqkv[:, 1:2]).then_inc(kraw_ready, 1)

            def take_v(i, par, ahead, half):
                b, q = batch(i, par, ahead)
                act.wait_ge(v_made, VE * b + half + 1)
                if not (isinstance(i, int) and i == 0 and par + ahead < 2):
                    act.wait_ge(o_made, U * (b - 1))
                if first:
                    dst = v[q][:, :, :, :, :].rearrange("p h u c d -> p (h u c d)")
                    out = bass.AP(tensor=dst.tensor, offset=dst.offset,
                                  ap=[dst.ap[0], [D + DK, G], [G * DK, U], [1, DK]])
                    src = kv_ps[:, 0, :].rearrange("p (u h d) -> p h u d", u=U, h=G)
                    nc.scalar.activation(out, src, ACT.Copy).then_inc(v_ready, 1)
                else:
                    nc.scalar.activation(v[q][:, half * 512:half * 512 + 512],
                                         kv_ps[:, :, :].rearrange("p a b -> p (a b)"), ACT.Copy).then_inc(v_ready, 1)

            def take_q(i, par, ahead, g):
                b, q = batch(i, par, ahead)
                act.wait_ge(q_made, QE * b + g + 1)
                if first:
                    if not (isinstance(i, int) and i == 0 and ahead == 0):
                        act.wait_ge(sc_made, U * (b - 1))
                    for u in range(U):
                        r = 32 * u
                        last = nc.scalar.activation(qT[q][r:r + 32, u, :], q_ps[r:r + 32, 0, :], ACT.Identity,
                                                    bias=bqkv[r:r + 32, 0:1])
                    last.then_inc(q_ready, 1)
                    return
                if not (isinstance(i, int) and i == 0 and ahead == 0):
                    act.wait_ge(sc_made, U * (b - 2) + g + 1)
                nc.scalar.activation(qT[q][:, G * g:G * g + G, :], q_ps[:, :, :], ACT.Copy).then_inc(q_ready, 1)

            def exponentials(i, par, ahead, g):
                b, q = batch(i, par, ahead)
                act.wait_ge(shifted, U * b + g + 1)
                p = probs[U * q + g][:, :, :]
                nc.scalar.activation(p, p, ACT.Exp, scale=scale).then_inc(exp_done, 1)

            def take_pT(i, par, g):
                b, q = batch(i, par)
                act.wait_ge(pT_made, U * b + g + 1)
                if g >= 2 or not (isinstance(b, int) and b == 0):
                    act.wait_ge(o_made, U * b + g - 1)
                nc.scalar.activation(pT[g % 2][:, :, :], t_ps[g % 2][:, :, :], ACT.Copy).then_inc(pT_ready, 1)

            def pair(i, is_first, is_last):
                for par in range(2):
                    has_next = not (is_last and par == 1)
                    for g in range(U):
                        take_pT(i, par, g)
                        if g == 0 and not is_last:
                            take_xnT(i, par, 2)
                        if g == 1 and has_next:
                            take_v(i, par, 1, 0)
                        if g == 2 and has_next and not first:
                            take_v(i, par, 1, 1)
                        if not is_last:
                            if first:
                                if g == 1:
                                    take_q(i, par, 2, 0)
                                if g == 2:
                                    take_k(i, par, 2)
                            else:
                                if g:
                                    take_q(i, par, 2, g - 1)
                                if g == 3:
                                    take_q(i, par, 2, 3)
                        if has_next:
                            exponentials(i, par, 1, g)

            if not first:
                for g in range(U):
                    act.wait_ge(wqk_made, g + 1)
                    nc.scalar.activation(wqk[:, G * g:G * g + G, :], sc_ps[g % 2][:, :, :], ACT.Copy).then_inc(wqk_ready, 1)
            else:
                act.wait_ge(weights, 16 * NW)
                act.wait_ge(zeros_set, 3)
            for par in range(2):
                take_xnT(0, par, 0)
                for g in range(QE):
                    take_q(0, par, 0, g)
                if first:
                    take_k(0, par, 0)
                if par == 0:
                    for half in range(VE):
                        take_v(0, par, 0, half)
            for g in range(U):
                exponentials(0, 0, 0, g)
            pair(0, True, False)
            with act.Fori(1, PAIRS - 1) as i:
                pair(i, False, False)
            pair(PAIRS - 1, False, True)

        @block.gpsimd
        def _(pool):
            if first:
                for q in range(2):
                    nc.gpsimd.memset(v[q][:, :, :, :, :], 0.0).then_inc(zeros_set, 1)
            pool.wait_ge(var_ready, 1)
            nc.gpsimd.tensor_tensor(k.rstd[:, :], k.var[:, :], k.half[:, :], ALU.pow).then_inc(rstd_ready, 1)
            pool.wait_ge(weights, 16 * NW)
            if first:
                pool.wait_ge(bo_full, 1)
                nc.gpsimd.memset(ones[:, :, :, :, :], 0.0).then_inc(base_own, 1)
                pool.wait_ge(base_own, 1)
                for hh in range(G):
                    nc.gpsimd.memset(ones[:, hh, :, hh, :], 1.0).then_inc(ones_set, 1)
            nc.gpsimd.tensor_scalar(bo[:, :], bo[:, :], k.tg[:, gate:gate + 1], None, ALU.mult).then_inc(base_own, 1)
            pool.wait_ge(base_own, 2 if first else 1)
            nc.gpsimd.tensor_tensor(k.base[:, :, :], k.x[:, :, :], rows(bo[:, :], B), ALU.add).then_inc(base_ready, 1)

            def mask_k(i, par, ahead):
                b, q = batch(i, par, ahead)
                pool.wait_ge(kraw_ready, b + 1)
                if not (isinstance(i, int) and i == 0 and ahead == 0):
                    pool.wait_ge(sc_made, U * (b - 1))
                nc.gpsimd.tensor_tensor(kT[q][:, :, :], rows(kraw[q][:, :], G), wide(headmask[:, :], S),
                                        ALU.mult).then_inc(k_ready, 1)

            def normalize(i, par, ahead, g):
                b, q = batch(i, par, ahead)
                pool.wait_ge(inv_ready, U * b + g + 1)
                p = probs[U * q + g][:, :, :]
                nc.gpsimd.tensor_tensor(p, p, wide(inv[U * q + g][:, :], S), ALU.mult).then_inc(probs_ready, 1)

            def pair(i, is_last):
                for par in range(2):
                    has_next = not (is_last and par == 1)
                    for g in range(U):
                        if first:
                            pass
                        elif g == 0:
                            normalize(i, par, 0, U - 1)
                        elif has_next:
                            normalize(i, par, 1, g - 1)
                        if g == 2 and first and not is_last:
                            mask_k(i, par, 2)

            if first:
                mask_k(0, 0, 0)
                mask_k(0, 1, 0)
            for g in range(0 if first else U - 1):
                normalize(0, 0, 0, g)
            pair(0, False)
            with pool.Fori(1, PAIRS - 1) as i:
                pair(i, False)
            pair(PAIRS - 1, True)

        @block.vector
        def _(dve):
            def norm(i, par, ahead):
                b, q = batch(i, par, ahead)
                if not (isinstance(i, int) and i == 0 and ahead == 0):
                    dve.wait_ge(xnT_made, b - 1)
                if isinstance(b, int):
                    mean, rstd, x = k.mean[:, b:b + 1], k.rstd[:, b:b + 1], k.x[:, b, :]
                else:
                    mean, rstd, x = k.mean[:, bass.ds(b, 1)], k.rstd[:, bass.ds(b, 1)], k.x[:, b, :]
                nc.vector.tensor_scalar(xn[q][:, :], x, mean, rstd, ALU.subtract, ALU.mult).then_inc(xn_ready, 1)

            def make_bias(i, par, ahead):
                b, q = batch(i, par, ahead)
                if not (isinstance(i, int) and i == 0 and ahead == 0):
                    dve.wait_ge(masked, U * (b - 1))
                nc.vector.scalar_tensor_tensor(out=bias[q][:, :], in0=hidden[:, b, :], scalar=-FMAX,
                                               in1=causal[:, :], op0=ALU.mult, op1=ALU.min).then_inc(bias_ready, 1)

            def find_top(i, par, ahead, g):
                b, q = batch(i, par, ahead)
                n = U * b + g
                p = probs[U * q + g][:, :, :]
                dve.wait_ge(sc_made, n + 1)
                if not (isinstance(i, int) and i == 0 and par + ahead < 2):
                    dve.wait_ge(pT_made, n - 2 * U + 1)
                if first:
                    nc.vector.tensor_reduce(top[U * q + g][:, :], sc_ps[g % 2][:, :, :], AX, ALU.max).then_inc(top_ready, 1)
                else:
                    dve.wait_ge(bias_ready, b + 1)
                    nc.vector.tensor_tensor(p, sc_ps[g % 2][:, :, :], rows(bias[q][:, :], G), ALU.add).then_inc(masked, 1)
                    dve.wait_ge(masked, n + 1)
                    nc.vector.tensor_reduce(top[U * q + g][:, :], p, AX, ALU.max).then_inc(top_ready, 1)

            def shift(i, par, ahead, g):
                b, q = batch(i, par, ahead)
                p = probs[U * q + g][:, :, :]
                dve.wait_ge(top_ready, U * b + g + 1)
                src = sc_ps[g % 2][:, :, :] if first else p
                nc.vector.tensor_tensor(p, src, wide(top[U * q + g][:, :], S), ALU.subtract).then_inc(shifted, 1)

            def add_up(i, par, ahead, g):
                b, q = batch(i, par, ahead)
                dve.wait_ge(exp_done, U * b + g + 1)
                nc.vector.tensor_reduce(total[U * q + g][:, :], probs[U * q + g][:, :, :], AX, ALU.add).then_inc(total_ready, 1)

            def invert(i, par, ahead, g):
                b, q = batch(i, par, ahead)
                dve.wait_ge(total_ready, U * b + g + 1)
                nc.vector.reciprocal(inv[U * q + g][:, :], total[U * q + g][:, :]).then_inc(inv_ready, 1)

            def take_o(i, par, ahead, g):
                b, q = batch(i, par, ahead)
                dve.wait_ge(o_made, U * b + g + 1)
                if not (isinstance(i, int) and i == 0 and par + ahead < 2):
                    dve.wait_ge(y_made, b - 1)
                if first:
                    nc.vector.reciprocal(oinv[q][:, :], o_ps[:, 1, :]).then_inc(oinv_ready, 1)
                    dve.wait_ge(oinv_ready, b + 1)
                    nc.vector.tensor_tensor(oT[q][:, 0, :], o_ps[:, 0, :], oinv[q][:, :], ALU.mult).then_inc(o_ready, 1)
                else:
                    nc.vector.tensor_copy(oT[q][:, 2 * g:2 * g + 2, :], o_ps[:, 0:2, :]).then_inc(o_ready, 1)

            def finish(i, par, ahead):
                b, q = batch(i, par, ahead)
                dve.wait_ge(y_made, b + 1)
                nc.vector.scalar_tensor_tensor(out=k.x[:, b, :], in0=y_ps[:, 0, :], scalar=k.tg[:, gate:gate + 1],
                                               in1=k.base[:, b, :], op0=ALU.mult, op1=ALU.add).then_inc(x_ready, 1)

            def row_stats(i, par, ahead):
                b, q = batch(i, par, ahead)
                dve.wait_ge(x_ready, b + 1)
                nc.vector.bn_stats(k.stats[:, b, :], k.x[:, b, :]).then_inc(stats_ready, 1)

            def pair(i, is_first, is_last):
                for par in range(2):
                    has_before = not (is_first and par == 0)
                    has_next = not (is_last and par == 1)
                    for g in range(U):
                        if g == 0 and not is_last:
                            norm(i, par, 2)
                        if has_next:
                            find_top(i, par, 1, g)
                        if first:
                            pass
                        elif g == 0:
                            add_up(i, par, 0, U - 1)
                        elif has_next:
                            add_up(i, par, 1, g - 1)
                        if has_next:
                            shift(i, par, 1, g)
                        if first:
                            pass
                        elif g == 0:
                            invert(i, par, 0, U - 1)
                        elif has_next:
                            invert(i, par, 1, g - 1)
                        if first:
                            if g == 0 and has_before:
                                take_o(i, par, -1, U - 1)
                        else:
                            if g:
                                take_o(i, par, 0, g - 1)
                            elif has_before:
                                take_o(i, par, -1, U - 1)
                            if g == 3 and not is_last:
                                make_bias(i, par, 2)
                        if g == 1 and has_before:
                            finish(i, par, -1)
                        if g == 2 and has_before:
                            row_stats(i, par, -1)

            norm_stats(nc, dve, k, norm_own, var_ready)
            if first:
                for q in range(2):
                    last = nc.vector.memset(qT[q][:, :, :], 0.0)
                last.then_inc(zeros_set, 1)
                dve.wait_ge(weights, 16 * NW)
                nc.vector.tensor_scalar(bv[:, :], k.ident[:, :], 0.0, bqkv[:, 2:3], ALU.mult, ALU.add).then_inc(bv_ready, 1)
                dve.wait_ge(bv_made, 1)
                nc.vector.tensor_tensor(bo[:, :], y_ps[:, 0, :], bo[:, :], ALU.add).then_inc(bo_full, 1)
            dve.wait_ge(weights, 16 * NW)
            if first:
                dve.wait_ge(zeros_set, 3)
            dve.wait_ge(rstd_ready, 1)
            for par in range(2):
                norm(0, par, 0)
                if not first:
                    make_bias(0, par, 0)
            for g in range(U):
                find_top(0, 0, 0, g)
                shift(0, 0, 0, g)
                if g and not first:
                    add_up(0, 0, 0, g - 1)
                    invert(0, 0, 0, g - 1)
            dve.wait_ge(base_ready, 1)
            pair(0, True, False)
            with dve.Fori(1, PAIRS - 1) as i:
                pair(i, False, False)
            pair(PAIRS - 1, False, True)
            take_o(PAIRS, 0, -1, U - 1)
            finish(PAIRS, 0, -1)
            row_stats(PAIRS, 0, -1)
            dve.wait_ge(stats_ready, B)


def experts_phase(nc, k, w, layer):
    first = layer == 0
    gate = 2 + layer
    NE = E + 1 if first else E
    act_fn = ACT.Gelu if first else ACT.Relu

    with ExitStack() as ctx:
        t = Tools(nc, ctx, f"ffn{layer}")
        router = t.sb("router", [128, E])
        iota = t.sb("iota", [128, E])
        up = [t.sb(f"up{i}", [128, F]) for i in range(2)]
        down = [t.sb(f"down{i}", [128, FC, D]) for i in range(2)]
        if not first:
            router_b = t.sb("router_b", [128, E])
            b1 = [t.sb(f"b1_{i}", [128, FC]) for i in range(2)]
            b2 = t.sb("b2", [E, D])
            weight = t.sb("weight", [128, B])
            pickT = [t.sb(f"pickT{i}", [E, S]) for i in range(2)]
        xn = [t.sb(f"xn{i}", [128, D]) for i in range(2)]
        xrT = [t.sb(f"xrT{i}", [128, S]) for i in range(2)]
        xT = t.sb("xT", [128, B, S])
        hT = [t.sb(f"hT{i}", [128, FC, GT]) for i in range(2)]
        pr, o1, o2, tmp = (t.sb(n, [128, B, E]) for n in ("pr", "o1", "o2", "tmp"))
        top, total, m1, i1, m2, i2 = (t.sb(n, [128, B]) for n in ("top", "total", "m1", "i1", "m2", "i2"))
        gates = t.sb("gates", [128, NE, B])

        up_ps = [t.ps(f"up_ps{i}", [128, GT]) for i in range(FC)]
        dn_ps = [t.ps(f"dn_ps{i}", [128, GB, D]) for i in range(2)]
        tr_ps = t.ps("tr_ps", [128, GB, S])
        lg_ps = t.ps("lg_ps", [128, B * 2, E])

        consts = t.sem("consts")
        w_in = [t.sem(f"w_in{i}") for i in range(2)]
        norm_own, var_ready, rstd_ready = t.sem("norm_own"), t.sem("var_ready"), t.sem("rstd_ready")
        xn_ready, xnT_made, xr_ready = t.sem("xn_ready"), t.sem("xnT_made"), t.sem("xr_ready")
        lg_made, e_ready, own = t.sem("lg_made"), t.sem("e_ready"), t.sem("own")
        shifted, picked, pickT_made, pickT_ready, b2_made, b2_added = (
            t.sem(n) for n in ("shifted", "picked", "pickT_made", "pickT_ready", "b2_made", "b2_added"))
        xs_ready, xsT_made, xsr_ready, xT_ready = (t.sem(n) for n in ("xs_ready", "xsT_made", "xsr_ready", "xT_ready"))
        up_made, h_ready, dn_made, dn_taken = t.sem("up_made"), t.sem("h_ready"), t.sem("dn_made"), t.sem("dn_taken")
        stats_ready = t.sem("stats_ready")
        block = ctx.enter_context(nc.Block())
        NC = 2 if first else 4
        WL = 2 if first else 3

        @block.sync
        def _(sp):
            loads = [(router[:, :], w[f"router{layer}"]), (iota[:, :], w["iota"].partition_broadcast(128))]
            if not first:
                loads += [(router_b[:, :], w["router_b1"].partition_broadcast(128)), (b2[:, :], w["b2"])]
            for dst, src in loads:
                sp.dma_start(dst, src).then_inc(consts, 16)

            def load(e, par):
                sp.dma_start(up[par][:, :], w[f"up{layer}"][e]).then_inc(w_in[par], 16)
                sp.dma_start(down[par][:, :, :], w[f"down{layer}"][e]).then_inc(w_in[par], 16)
                if not first:
                    sp.dma_start(b1[par][:, :], w["b1"][e]).then_inc(w_in[par], 16)

            load(0, 0)
            load(1, 1)
            with sp.Fori(1, E // 2) as i:
                for par in range(2):
                    before = sp.snap(GROUPS * (2 * i + par - 1))
                    sp.wait_ge(dn_made, before)
                    load(2 * i + par, par)
            if first:
                sp.wait_ge(dn_made, GROUPS * (E - 1))
                load(E, 0)

        @block.tensor
        def _(pe):
            def turn(b, par, made, ready, is_first):
                pe.wait_ge(ready, b + 1)
                if not (is_first and par == 0):
                    pe.wait_ge(xr_ready, b)
                nc.tensor.transpose(tr_ps[:, 0, :], xn[par][:, :], k.ident[:, :]).then_inc(made, 1)

            def logits(b, par):
                pe.wait_ge(xr_ready, b + 1)
                out = lg_ps[:, b, :] if isinstance(b, int) else lg_ps[:, b, :]
                nc.tensor.matmul(out, xrT[par][:, :], router[:, :], start=True, stop=True).then_inc(lg_made, 1)

            def turn_pair(i, is_first):
                for par in range(2):
                    turn(2 * i + par, par, xnT_made, xn_ready, is_first)
                    logits(2 * i + par, par)

            pe.wait_ge(consts, 16 * NC)
            turn_pair(0, True)
            with pe.Fori(1, PAIRS) as i:
                turn_pair(i, False)
            if not first:
                def scaled_pair(i, is_first):
                    for par in range(2):
                        b = 2 * i + par
                        pe.wait_ge(xs_ready, b + 1)
                        if not (is_first and par == 0):
                            pe.wait_ge(xsr_ready, b)
                        nc.tensor.transpose(tr_ps[:, 0, :], xn[par][:, :], k.ident[:, :]).then_inc(xsT_made, 1)
                scaled_pair(0, True)
                with pe.Fori(1, PAIRS) as i:
                    scaled_pair(i, False)
                pe.wait_ge(picked, 1)
                for b in range(B):
                    if b:
                        pe.wait_ge(pickT_ready, b)
                    else:
                        pe.wait_ge(xT_ready, B)
                    nc.tensor.transpose(tr_ps[0:E, 0, :], o1[:, b, :], k.ident[:, :]).then_inc(pickT_made, 1)
                    pe.wait_ge(pickT_ready, b + 1)
                    if b >= 2:
                        pe.wait_ge(b2_added, b - 1)
                    nc.tensor.matmul(dn_ps[b % 2][:, 0, :], pickT[b % 2][:, :], b2[:, :], start=True, stop=True).then_inc(b2_made, 1)
                pe.wait_ge(b2_added, B)

            def go_up(n, e, par, turns, g, is_first):
                pe.wait_ge(w_in[par], 16 * WL * (turns + 1))
                pe.wait_ge(xT_ready, B if not first else (GB * (g + 1) if is_first else B))
                for c in range(FC):
                    if not (is_first and g == 0):
                        pe.wait_ge(h_ready, FC * (n - 1) + c + 1)
                    nc.tensor.matmul(up_ps[c][:, :], up[par][:, 128 * c:128 * c + 128],
                                     xT[:, GB * g:GB * g + GB, :].rearrange("p a b -> p (a b)"),
                                     start=True, stop=True).then_inc(up_made, 1)

            def go_down(n, par, g, is_first):
                pe.wait_ge(h_ready, FC * (n + 1))
                if not (is_first and g < 2):
                    pe.wait_ge(dn_taken, n - 1)
                for s in range(GB):
                    for c in range(FC):
                        mm = nc.tensor.matmul(dn_ps[g % 2][:, s, :], hT[g % 2][:, c, S * s:S * s + S], down[par][:, c, :],
                                              start=(c == 0), stop=(c == FC - 1))
                mm.then_inc(dn_made, 1)

            def expert(i, par, is_first, is_last):
                e = 2 * i + par
                for g in range(GROUPS):
                    n = GROUPS * e + g
                    if g < GROUPS - 1:
                        go_up(n + 1, e, par, i, g + 1, is_first)
                    elif not is_last:
                        go_up(n + 1, e + 1, (par + 1) % 2, i + (par + 1) // 2, 0, False)
                    go_down(n, par, g, is_first)

            go_up(0, 0, 0, 0, 0, True)
            expert(0, 0, True, False)
            expert(0, 1, False, False)
            with pe.Fori(1, E // 2 - 1) as i:
                for par in range(2):
                    expert(i, par, False, False)
            expert(E // 2 - 1, 0, False, False)
            expert(E // 2 - 1, 1, False, not first)
            if first:
                expert(E // 2, 0, False, True)

        @block.scalar
        def _(act):
            def take(b, par, is_first):
                act.wait_ge(xnT_made, b + 1)
                if not is_first:
                    act.wait_ge(lg_made, b - 1)
                    if first:
                        act.wait_ge(xT_ready, b - 1)
                nc.scalar.activation(xrT[par][:, :], tr_ps[:, 0, :], ACT.Copy).then_inc(xr_ready, 1)

            for par in range(2):
                take(par, par, True)
            with act.Fori(1, PAIRS) as i:
                for par in range(2):
                    take(2 * i + par, par, False)
            act.wait_ge(shifted, 1)
            nc.scalar.activation(pr[:, :, :], pr[:, :, :], ACT.Exp).then_inc(e_ready, 1)
            if not first:
                def take_scaled(i):
                    for par in range(2):
                        b = 2 * i + par
                        act.wait_ge(xsT_made, b + 1)
                        if not isinstance(i, int):
                            act.wait_ge(xT_ready, b - 1)
                        nc.scalar.activation(xrT[par][:, :], tr_ps[:, 0, :], ACT.Copy).then_inc(xsr_ready, 1)

                take_scaled(0)
                with act.Fori(1, PAIRS) as i:
                    take_scaled(i)
                for b in range(B):
                    act.wait_ge(pickT_made, b + 1)
                    if b >= 2:
                        act.wait_ge(b2_made, b - 1)
                    nc.scalar.activation(pickT[b % 2][:, :], tr_ps[0:E, 0, :], ACT.Copy).then_inc(pickT_ready, 1)

            def hidden(n, i, par, g, is_first):
                if not first and g == 0:
                    act.wait_ge(w_in[par], 16 * WL * (i + 1))
                if not (is_first and g < 2):
                    act.wait_ge(dn_made, n - 1)
                for c in range(FC):
                    act.wait_ge(up_made, FC * n + c + 1)
                    bias = 0.0 if first else b1[par][:, c:c + 1]
                    nc.scalar.activation(hT[g % 2][:, c, :], up_ps[c][:, :], act_fn, bias=bias).then_inc(h_ready, 1)

            def expert(i, par, is_first):
                for g in range(GROUPS):
                    hidden(GROUPS * (2 * i + par) + g, i, par, g, is_first)

            expert(0, 0, True)
            expert(0, 1, False)
            with act.Fori(1, E // 2) as i:
                for par in range(2):
                    expert(i, par, False)
            if first:
                expert(E // 2, 0, False)

        @block.gpsimd
        def _(pool):
            pool.wait_ge(var_ready, 1)
            nc.gpsimd.tensor_tensor(k.rstd[:, :], k.var[:, :], k.half[:, :], ALU.pow).then_inc(rstd_ready, 1)
            source = xr_ready if first else xsr_ready
            if True:
                with pool.Fori(0, PAIRS) as i:
                    for par in range(2):
                        pool.wait_ge(source, 2 * i + par + 1)
                        nc.gpsimd.tensor_copy(xT[:, 2 * i + par, :], xrT[par][:, :]).then_inc(xT_ready, 1)

        @block.vector
        def _(dve):
            norm_stats(nc, dve, k, norm_own, var_ready)
            dve.wait_ge(rstd_ready, 1)

            def norm(i, is_first):
                for par in range(2):
                    b = 2 * i + par
                    if not is_first:
                        dve.wait_ge(xnT_made, b - 1)
                    mean = k.mean[:, b:b + 1] if isinstance(b, int) else k.mean[:, bass.ds(b, 1)]
                    rstd = k.rstd[:, b:b + 1] if isinstance(b, int) else k.rstd[:, bass.ds(b, 1)]
                    nc.vector.tensor_scalar(xn[par][:, :], k.x[:, b, :], mean, rstd, ALU.subtract, ALU.mult).then_inc(xn_ready, 1)
                    if first:
                        dve.wait_ge(xn_ready, b + 1)
                        nc.vector.scalar_tensor_tensor(out=k.x[:, b, :], in0=xn[par][:, :], scalar=k.tg[:, gate:gate + 1],
                                                       in1=k.x[:, b, :], op0=ALU.mult, op1=ALU.add)
                    else:
                        nc.vector.tensor_scalar(k.base[:, b, :], k.x[:, b, :], mean, rstd, ALU.subtract, ALU.mult)

            norm(0, True)
            with dve.Fori(1, PAIRS) as i:
                norm(i, False)

            count = [0]

            def step(ins):
                count[0] += 1
                ins.then_inc(own, 1)
                dve.wait_ge(own, count[0])

            V = nc.vector
            lg = lg_ps[:, 0:B, :]
            dve.wait_ge(lg_made, B)
            dve.wait_ge(consts, 16 * NC)
            it = rows(iota[:, :], B)
            if first:
                step(V.tensor_copy(pr[:, :, :], lg))
            else:
                step(V.tensor_tensor(pr[:, :, :], lg, rows(router_b[:, :], B), ALU.add))
            step(V.tensor_reduce(top[:, :], pr[:, :, :], AX, ALU.max))
            V.tensor_tensor(pr[:, :, :], pr[:, :, :], wide(top[:, :], E), ALU.subtract).then_inc(shifted, 1)
            dve.wait_ge(e_ready, 1)
            step(V.tensor_reduce(total[:, :], pr[:, :, :], AX, ALU.add))
            step(V.reciprocal(total[:, :], total[:, :]))
            step(V.tensor_tensor(pr[:, :, :], pr[:, :, :], wide(total[:, :], E), ALU.mult))

            def pick(prob, m, idx, onehot):
                step(V.tensor_reduce(m[:, :], prob, AX, ALU.max))
                step(V.tensor_tensor(tmp[:, :, :], prob, wide(m[:, :], E), ALU.is_lt))
                step(V.scalar_tensor_tensor(out=tmp[:, :, :], in0=tmp[:, :, :], scalar=float(E), in1=it, op0=ALU.mult, op1=ALU.add))
                step(V.tensor_reduce(idx[:, :], tmp[:, :, :], AX, ALU.min))
                step(V.tensor_tensor(onehot, it, wide(idx[:, :], E), ALU.is_equal))

            pick(pr[:, :, :], m1, i1, o1[:, :, :])
            step(V.scalar_tensor_tensor(out=o2[:, :, :], in0=o1[:, :, :], scalar=-2.0, in1=pr[:, :, :], op0=ALU.mult, op1=ALU.add))
            pick(o2[:, :, :], m2, i2, o2[:, :, :])
            tg = k.tg[:, gate:gate + 1]
            if first:
                step(V.tensor_tensor(o1[:, :, :], o1[:, :, :], wide(m1[:, :], E), ALU.mult))
                step(V.tensor_tensor(o2[:, :, :], o2[:, :, :], wide(m2[:, :], E), ALU.mult))
                step(V.tensor_tensor(o1[:, :, :], o1[:, :, :], o2[:, :, :], ALU.add))
                V.memset(gates[:, 0, :], 1.0).then_inc(own, 1)
                V.tensor_copy(gates[:, 1:NE, :], o1[:, :, :].rearrange("p b e -> p e b")).then_inc(own, 1)
                count[0] += 2
                dve.wait_ge(own, count[0])
                step(V.tensor_scalar(gates[:, :, :], gates[:, :, :], tg, None, ALU.mult))
            else:
                step(V.tensor_scalar(i2[:, :], i2[:, :], 1.0, None, ALU.add))
                step(V.tensor_scalar(top[:, :], m2[:, :], 0.0, None, ALU.is_gt))
                step(V.tensor_tensor(i2[:, :], i2[:, :], top[:, :], ALU.mult))
                step(V.scalar_tensor_tensor(out=i1[:, :], in0=i2[:, :], scalar=-1.0, in1=i1[:, :], op0=ALU.add, op1=ALU.max))
                step(V.tensor_tensor(o1[:, :, :], it, wide(i1[:, :], E), ALU.is_equal))
                step(V.tensor_tensor(o2[:, :, :], o1[:, :, :], pr[:, :, :], ALU.mult))
                step(V.tensor_reduce(weight[:, :], o2[:, :, :], AX, ALU.add))
                V.tensor_scalar(gates[:, :, :], o1[:, :, :].rearrange("p b e -> p e b"), tg, None, ALU.mult).then_inc(picked, 1)

                def scaled(i):
                    for par in range(2):
                        b = 2 * i + par
                        if isinstance(i, int):
                            dve.wait_ge(xnT_made, B)
                        else:
                            dve.wait_ge(xsT_made, b - 1)
                        wt = weight[:, b:b + 1] if isinstance(b, int) else weight[:, bass.ds(b, 1)]
                        V.tensor_scalar(xn[par][:, :], k.base[:, b, :], wt, None, ALU.mult).then_inc(xs_ready, 1)

                scaled(0)
                with dve.Fori(1, PAIRS) as i:
                    scaled(i)
                for b in range(B):
                    dve.wait_ge(b2_made, b + 1)
                    V.scalar_tensor_tensor(out=k.x[:, b, :], in0=dn_ps[b % 2][:, 0, :], scalar=tg, in1=k.x[:, b, :],
                                           op0=ALU.mult, op1=ALU.add).then_inc(b2_added, 1)
                dve.wait_ge(picked, 1)
                dve.wait_ge(b2_added, B)

            def collect(e, is_first):
                for g in range(GROUPS):
                    n = GROUPS * e + g
                    dve.wait_ge(dn_made, n + 1)
                    if not is_first:
                        dve.wait_ge(dn_taken, n - GROUPS + 1)
                    for s in range(GB):
                        b = GB * g + s
                        gt = gates[:, e, b:b + 1]
                        ins = V.scalar_tensor_tensor(out=k.x[:, b, :], in0=dn_ps[g % 2][:, s, :], scalar=gt,
                                                     in1=k.x[:, b, :], op0=ALU.mult, op1=ALU.add)
                    ins.then_inc(dn_taken, 1)

            collect(0, True)
            with dve.Fori(1, NE) as e:
                collect(e, False)
            dve.wait_ge(dn_taken, GROUPS * NE)
            if first:
                with dve.Fori(0, B) as b:
                    V.bn_stats(k.stats[:, b, :], k.x[:, b, :]).then_inc(stats_ready, 1)
                dve.wait_ge(stats_ready, B)


def store_phase(nc, k, w):
    with ExitStack() as ctx:
        stored = ctx.enter_context(nc.semaphore("stored"))
        block = ctx.enter_context(nc.Block())

        @block.sync
        def _(sp):
            sp.dma_start(w["out"], k.x[:, :, :]).then_inc(stored, 16)
            sp.wait_ge(stored, 16)


class Kept:
    pass


def flamingo(nc, w):
    with ExitStack() as ctx:
        t = Tools(nc, ctx, "kept")
        k = Kept()
        k.x = t.sb("x", [128, B, D])
        k.base = t.sb("base", [128, B, D])
        k.ident = t.sb("ident", [128, 128])
        k.graw = t.sb("graw", [128, 4])
        k.tg = t.sb("tg", [128, 4])
        k.half = t.sb("half", [128, B])
        k.stats = t.sb("stats", [128, B, 6])
        k.mean, k.diff, k.var, k.rstd = (t.sb(n, [128, B]) for n in ("mean", "diff", "var", "rstd"))
        start_phase(nc, k, w)
        for layer in range(2):
            attention_phase(nc, k, w, layer)
            experts_phase(nc, k, w, layer)
        store_phase(nc, k, w)


def kernel(x, ctx_1024, mask_BxS2_bf0, g_xattn, g_ffn, L0_xattn_Wq, L0_xattn_bq, L0_xattn_Wk, L0_xattn_bk,
           L0_xattn_Wv, L0_xattn_bv, L0_xattn_Wo, L0_xattn_bo, L0_ffn_shared_up, L0_ffn_shared_down,
           L0_ffn_routed_up, L0_ffn_routed_down, L0_ffn_router_w, L1_xattn_Wq, L1_xattn_Wk, L1_xattn_Wv,
           L1_xattn_Wo, L1_xattn_bo, L1_ffn_gate_w, L1_ffn_gate_b, L1_ffn_w1, L1_ffn_b1, L1_ffn_w2, L1_ffn_b2):
    import concourse.bacc as bacc
    from concourse.bass_utils import run_bass_kernel_spmd

    def a(v):
        return np.asarray(v)

    head = np.arange(128) // DK % G
    data = {
        "xr": a(x).transpose(1, 0, 2),
        "ctxT": a(ctx_1024).transpose(0, 2, 1),
        "mask": a(mask_BxS2_bf0),
        "g_xattn": a(g_xattn), "g_ffn": a(g_ffn),
        "ident": np.eye(128, dtype=np.float32),
        "headmask": (head[:, None] == np.arange(G)[None]).astype(np.float32),
        "causal": np.where(np.arange(S)[None] > np.arange(S)[:, None], np.float32(-FMAX), np.float32(0)),
        "iota": np.arange(E, dtype=np.float32),
        "wq0": a(L0_xattn_Wq).T, "wk0": a(L0_xattn_Wk).T, "wv0": a(L0_xattn_Wv).T,
        "bqkv0": np.stack([a(L0_xattn_bq), a(L0_xattn_bk), a(L0_xattn_bv)], 1),
        "wo0": a(L0_xattn_Wo).T[:, None], "bo0": a(L0_xattn_bo),
        "wqT1": a(L1_xattn_Wq).reshape(D, HEADS, DH).transpose(2, 1, 0),
        "wkT1": a(L1_xattn_Wk).reshape(D, HEADS, DH).transpose(2, 1, 0),
        "wv1": a(L1_xattn_Wv),
        "wo1": a(L1_xattn_Wo).reshape(INNER // 128, 128, D).transpose(1, 0, 2), "bo1": a(L1_xattn_bo),
        "router0": a(L0_ffn_router_w), "router1": a(L1_ffn_gate_w).T, "router_b1": a(L1_ffn_gate_b),
        "up0": np.concatenate([a(L0_ffn_shared_up), a(L0_ffn_routed_up)]),
        "down0": np.concatenate([a(L0_ffn_shared_down), a(L0_ffn_routed_down)]).reshape(E + 1, FC, 128, D).transpose(0, 2, 1, 3),
        "up1": a(L1_ffn_w1).transpose(0, 2, 1),
        "down1": a(L1_ffn_w2).transpose(0, 2, 1).reshape(E, FC, 128, D).transpose(0, 2, 1, 3),
        "b1": a(L1_ffn_b1).reshape(E, FC, 128).transpose(0, 2, 1), "b2": a(L1_ffn_b2),
    }
    nc = bacc.Bacc("TRN2", target_bir_lowering=False, num_devices=1)
    arrays, w = {}, {}
    for name, v in data.items():
        v = np.ascontiguousarray(v)
        arrays[f"in_{name}"] = v
        w[name] = nc.dram_tensor(f"in_{name}", v.shape, mybir.dt.from_np(v.dtype), kind="ExternalInput").ap()
    w["out"] = nc.dram_tensor("out", (S, B, D), F32, kind="ExternalOutput").ap()
    flamingo(nc, w)
    r = run_bass_kernel_spmd(nc, [arrays], core_ids=[0])
    return np.ascontiguousarray(r.results[0]["out"].transpose(1, 0, 2))
```

```python
from contextlib import ExitStack

import numpy as np

import concourse.bass as bass
from concourse import mybir

F32 = mybir.dt.float32
U8 = mybir.dt.uint8
I32 = mybir.dt.int32
ALU = mybir.AluOpType
ACT = mybir.ActivationFunctionType
AX = mybir.AxisListType.X

B, S, D = 16, 128, 128
HEADS = 16
DK = D // HEADS
DH = 64
INNER = HEADS * DH
F = 512
FC = F // 128
E = 8
G = 4
U = HEADS // G
PAIRS = B // 2
GROUPS = 4
GB = B // GROUPS
GT = GB * S
R = 8
ROW = D + 2
NTILES = [(uses * B * S + E * 127) // 128 for uses in (2, 1)]
EPS = 1e-5
FMAX = float(np.finfo(np.float32).max)


class Tools:

    def __init__(self, nc, ctx, tag, used):
        self.nc, self.ctx, self.tag, self.used = nc, ctx, tag, used

    def sb(self, name, shape, dt=F32):
        return self.ctx.enter_context(self.nc.sbuf_tensor(f"{self.tag}_{name}", shape, dt))

    def ps(self, name, shape, dt=F32):
        return self.ctx.enter_context(self.nc.psum_tensor(f"{self.tag}_{name}", shape, dt))

    def sem(self, name):
        self.used.append(self.nc.alloc_semaphore(f"{self.tag}_{name}"))
        return self.used[-1]


def wide(ap, n):
    return ap.unsqueeze(2).to_broadcast([ap.shape[0], ap.shape[1], n])


def rows(ap, m):
    return ap.unsqueeze(1).to_broadcast([ap.shape[0], m, ap.shape[1]])


def start_phase(nc, k, w):
    with ExitStack() as ctx:
        t = Tools(nc, ctx, "start", k.used)
        loaded = t.sem("loaded")
        x_loaded = t.sem("x_loaded")
        tanh_done = t.sem("tanh_done")
        block = ctx.enter_context(nc.Block())

        @block.sync
        def _(sp):
            sp.dma_start(k.x[:, :, :], w["xr"]).then_inc(x_loaded, 16)
            sp.dma_start(k.graw[:, 0:2], w["g_xattn"].partition_broadcast(128)).then_inc(loaded, 16)
            sp.dma_start(k.graw[:, 2:4], w["g_ffn"].partition_broadcast(128)).then_inc(loaded, 16)
            sp.dma_start(k.ident[:, :], w["ident"]).then_inc(loaded, 16)
            for layer, slots in enumerate(k.slots):
                sp.dma_start(slots.bitcast(I32), w[f"padding{layer}"]).then_inc(k.slots_set, 16)

        @block.scalar
        def _(act):
            act.wait_ge(loaded, 48)
            nc.scalar.activation(k.tg[:, :], k.graw[:, :], ACT.Tanh).then_inc(tanh_done, 1)
            act.wait_ge(tanh_done, 1)

        @block.vector
        def _(dve):
            nc.vector.memset(k.half[:, :], -0.5)
            dve.wait_ge(x_loaded, 16)
            with dve.Fori(0, B) as b:
                nc.vector.bn_stats(k.stats[:, b, :], k.x[:, b, :])


def norm_stats(nc, dve, k, own, ready):
    m0, m1 = k.stats[:, :, 1], k.stats[:, :, 4]
    v0, v1 = k.stats[:, :, 2], k.stats[:, :, 5]
    nc.vector.tensor_tensor(k.mean[:, :], m0, m1, ALU.add).then_inc(own, 1)
    nc.vector.tensor_tensor(k.diff[:, :], m0, m1, ALU.subtract).then_inc(own, 1)
    nc.vector.tensor_tensor(k.var[:, :], v0, v1, ALU.add).then_inc(own, 1)
    dve.wait_ge(own, 3)
    nc.vector.tensor_scalar(k.mean[:, :], k.mean[:, :], 0.5, None, ALU.mult).then_inc(own, 1)
    nc.vector.tensor_tensor(k.diff[:, :], k.diff[:, :], k.diff[:, :], ALU.mult).then_inc(own, 1)
    nc.vector.tensor_scalar(k.var[:, :], k.var[:, :], 1.0 / D, EPS, ALU.mult, ALU.add).then_inc(own, 1)
    dve.wait_ge(own, 6)
    nc.vector.scalar_tensor_tensor(out=k.var[:, :], in0=k.diff[:, :], scalar=0.25, in1=k.var[:, :],
                                   op0=ALU.mult, op1=ALU.add).then_inc(ready, 1)


def attention_phase(nc, k, w, layer):
    first = layer == 0
    scale = float(np.float32(1.0) / np.sqrt(np.float32(DK if first else DH)))
    earlier = list(k.used)
    OC = 1 if first else HEADS * DH // 128
    gate = 2 * 0 + layer

    with ExitStack() as ctx:
        t = Tools(nc, ctx, f"att{layer}", k.used)
        if first:
            wo = t.sb("wo", [128, OC, D])
            bo = t.sb("bo", [128, D])
            wq, wk, wv = t.sb("wq", [128, D]), t.sb("wk", [128, D]), t.sb("wv", [128, D])
            bqkv = t.sb("bqkv", [128, 3])
            headmask = t.sb("headmask", [128, G])
            ones = t.sb("ones", [128, G, U, G, DK])
            bv = t.sb("bv", [128, S])
            oinv = [t.sb(f"oinv{i}", [128, S]) for i in range(2)]
        else:
            wo, bo, wv, wqk, causal, hidden = k.wo1, k.bo1, k.wv1, k.wqk, k.causal, k.hidden
        ctxT = [t.sb(f"ctxT{i}", [128, S]) for i in range(2)]
        xn = [t.sb(f"xn{i}", [128, D]) for i in range(2)]
        xnT = [t.sb(f"xnT{i}", [128, S]) for i in range(2)]
        if first:
            qT = [t.sb(f"qT{i}", [128, U, S]) for i in range(2)]
            kraw = [t.sb(f"kraw{i}", [128, S]) for i in range(2)]
            kT = [t.sb(f"kT{i}", [128, G, S]) for i in range(2)]
            v = [t.sb(f"v{i}", [128, G, U, G, DK]) for i in range(2)]
        else:
            qT = [t.sb(f"qT{i}", [128, HEADS, S]) for i in range(2)]
            v = [t.sb(f"v{i}", [128, INNER]) for i in range(2)]
            bias = [t.sb(f"bias{i}", [128, S]) for i in range(2)]
        oT = [t.sb(f"oT{i}", [128, OC, S]) for i in range(2)]
        probs = [t.sb(f"probs{i}", [128, G, S]) for i in range(2 * U)]
        top = [t.sb(f"top{i}", [128, G]) for i in range(2 * U)]
        total = [t.sb(f"total{i}", [128, G]) for i in range(2 * U)]
        inv = [t.sb(f"inv{i}", [128, G]) for i in range(2 * U)]
        pT = [t.sb(f"pT{i}", [128, G, S]) for i in range(2)]
        sc_ps = [t.ps(f"sc_ps{i}", [128, G, S]) for i in range(2)]
        t_ps = [t.ps(f"t_ps{i}", [128, G, S]) for i in range(2)]
        q_ps = t.ps("q_ps", [128, G, S])
        kv_ps = t.ps("kv_ps", [128, G, S])
        o_ps = t.ps("o_ps", [128, G, S])
        y_ps = t.ps("y_ps", [128, G, S])

        weights = t.sem("weights") if first else k.att1_in
        ctx_in = [t.sem(f"ctx_in{i}") for i in range(2)]
        norm_own = t.sem("norm_own")
        var_ready = t.sem("var_ready")
        rstd_ready = t.sem("rstd_ready")
        base_own = t.sem("base_own")
        base_ready = t.sem("base_ready")
        xn_ready, xnT_made, xnT_ready = t.sem("xn_ready"), t.sem("xnT_made"), t.sem("xnT_ready")
        q_made, q_ready = t.sem("q_made"), t.sem("q_ready")
        v_made, v_ready = t.sem("v_made"), t.sem("v_ready")
        sc_made, top_ready, shifted = t.sem("sc_made"), t.sem("top_ready"), t.sem("shifted")
        exp_done, pT_made, pT_ready = t.sem("exp_done"), t.sem("pT_made"), t.sem("pT_ready")
        o_made, o_ready = t.sem("o_made"), t.sem("o_ready")
        y_made, x_ready, stats_ready = t.sem("y_made"), t.sem("x_ready"), t.sem("stats_ready")
        if first:
            zeros_set, ones_set = t.sem("zeros_set"), t.sem("ones_set")
            k_made, kraw_ready, k_ready = t.sem("k_made"), t.sem("kraw_ready"), t.sem("k_ready")
            oinv_ready = t.sem("oinv_ready")
            bv_ready, bv_made, bo_full = t.sem("bv_ready"), t.sem("bv_made"), t.sem("bo_full")
        else:
            bias_ready, masked = t.sem("bias_ready"), t.sem("masked")
            total_ready, inv_ready, probs_ready = t.sem("total_ready"), t.sem("inv_ready"), t.sem("probs_ready")
        if not first:
            nc.clear_and_free_semaphores(earlier)
        block = ctx.enter_context(nc.Block())

        spread = [q_ps, kv_ps, o_ps, y_ps]
        QE = 1 if first else U
        VE = 1 if first else 2

        def batch(i, par, ahead=0):
            return 2 * i + par + ahead, (par + ahead) % 2

        def turns(i, par, ahead):
            return i + (par + ahead) // 2

        @block.sync
        def _(sp):
            if first:
                for dst, src in [(wq[:, :], w["wq0"]), (wk[:, :], w["wk0"]), (wv[:, :], w["wv0"]), (bqkv[:, :], w["bqkv0"]),
                                 (headmask[:, :], w["headmask"]), (wo[:, :, :], w["wo0"]),
                                 (bo[:, :], w["bo0"].partition_broadcast(128))]:
                    sp.dma_start(dst, src).then_inc(weights, 16)
            experts = [(k.wup[:, :, :], w[f"up{layer}"]), (k.wdn[:, :, :, :], w[f"down{layer}"])]
            biases = [] if first else [(k.b1[:, :, :], w["b1"].partition_broadcast(128)), (k.b2[:, :, :], w["b2"].partition_broadcast(128))]
            for par in range(2):
                sp.dma_start(ctxT[par][:, :], w["ctxT"][par]).then_inc(ctx_in[par], 16)
            for dst, src in experts:
                sp.dma_start(dst, src).then_inc(k.w_in[layer], 16)
            for dst, src in biases:
                sp.dma_start(dst, src).then_inc(k.bias_in, 16)
            with sp.Fori(1, PAIRS) as i:
                for par in range(2):
                    b, _p = batch(i, par)
                    if first:
                        sp.wait_ge(v_made, b - 1)
                    else:
                        sp.wait_ge(sc_made, U * (b - 1))
                    sp.dma_start(ctxT[par][:, :], w["ctxT"][b]).then_inc(ctx_in[par], 16)

        NW = 7 if first else 5

        @block.tensor
        def _(pe):
            def x_transpose(i, par, ahead):
                b, q = batch(i, par, ahead)
                pe.wait_ge(xn_ready, b + 1)
                if not (isinstance(b, int) and b == 0):
                    pe.wait_ge(q_ready, QE * b)
                nc.tensor.transpose(q_ps[:, 0, :], xn[q][:, :], k.ident[:, :]).then_inc(xnT_made, 1)

            def project_q(i, par, ahead, g):
                b, q = batch(i, par, ahead)
                pe.wait_ge(xnT_ready, b + 1)
                if first:
                    nc.tensor.matmul(q_ps[:, 0, :], wq[:, :], xnT[q][:, :], start=True, stop=True).then_inc(q_made, 1)
                    return
                if g or not (isinstance(b, int) and b == 0):
                    pe.wait_ge(q_ready, QE * b + g)
                for hh in range(G):
                    mm = nc.tensor.matmul(q_ps[:, hh, :], wqk[:, G * g + hh, :], xnT[q][:, :], start=True, stop=True)
                mm.then_inc(q_made, 1)

            def project_k(i, par, ahead):
                b, q = batch(i, par, ahead)
                pe.wait_ge(ctx_in[q], 16 * (turns(i, par, ahead) + 1))
                if not (isinstance(b, int) and b == 0):
                    pe.wait_ge(v_ready, b)
                nc.tensor.matmul(kv_ps[:, 0, :], wk[:, :], ctxT[q][:, :], start=True, stop=True).then_inc(k_made, 1)

            def project_v(i, par, ahead, half):
                b, q = batch(i, par, ahead)
                if first:
                    pe.wait_ge(kraw_ready, b + 1)
                    nc.tensor.matmul(kv_ps[:, 0, :], ctxT[q][:, :], wv[:, :], start=True, stop=True).then_inc(v_made, 1)
                    return
                pe.wait_ge(ctx_in[q], 16 * (turns(i, par, ahead) + 1))
                if half or not (isinstance(b, int) and b == 0):
                    pe.wait_ge(v_ready, VE * b + half)
                nc.tensor.matmul(kv_ps[:, :, :].rearrange("p a b -> p (a b)"), ctxT[q][:, :],
                                 wv[:, half * 512:half * 512 + 512], start=True, stop=True).then_inc(v_made, 1)

            def scores(i, par, ahead, g):
                b, q = batch(i, par, ahead)
                if first:
                    pe.wait_ge(q_ready, b + 1)
                    pe.wait_ge(k_ready, b + 1)
                else:
                    pe.wait_ge(q_ready, QE * b + g + 1)
                    pe.wait_ge(ctx_in[q], 16 * (turns(i, par, ahead) + 1))
                if g >= 2 or not (isinstance(b, int) and b == 0):
                    pe.wait_ge(shifted if first else masked, U * b + g - 1)
                if first:
                    nc.tensor.matmul(sc_ps[g % 2][:, :, :].rearrange("p a b -> p (a b)"), qT[q][:, g, :],
                                     kT[q][:, :, :].rearrange("p a b -> p (a b)"), start=True, stop=True).then_inc(sc_made, 1)
                    return
                for hh in range(G):
                    mm = nc.tensor.matmul(sc_ps[g % 2][:, hh, :], qT[q][:, G * g + hh, :], ctxT[q][:, :],
                                          start=True, stop=True)
                mm.then_inc(sc_made, 1)

            def turn_probs(i, par, g):
                b, q = batch(i, par)
                pe.wait_ge(exp_done if first else probs_ready, U * b + g + 1)
                if g >= 2 or not (isinstance(b, int) and b == 0):
                    pe.wait_ge(pT_ready, U * b + g - 1)
                for hh in range(G):
                    mm = nc.tensor.transpose(t_ps[g % 2][:, hh, :], probs[U * q + g][:, hh, :], k.ident[:, :])
                mm.then_inc(pT_made, 1)

            def values(i, par, ahead, g):
                b, q = batch(i, par, ahead)
                pe.wait_ge(pT_ready, U * b + g + 1)
                pe.wait_ge(v_ready, VE * b + VE)
                if first:
                    if g == 0 and not (isinstance(b, int) and b == 0):
                        pe.wait_ge(o_ready, b)
                    elif g == 0:
                        pe.wait_ge(ones_set, G)
                    for hh in range(G):
                        mm = nc.tensor.matmul(o_ps[32 * g:32 * g + 32, 0, :],
                                              v[q][:, hh, g, :, :].rearrange("p a b -> p (a b)"),
                                              pT[g % 2][:, hh, :], start=(hh == 0), stop=(hh == G - 1))
                    for hh in range(G):
                        mm = nc.tensor.matmul(o_ps[32 * g:32 * g + 32, 1, :],
                                              ones[:, hh, g, :, :].rearrange("p a b -> p (a b)"),
                                              pT[g % 2][:, hh, :], start=(hh == 0), stop=(hh == G - 1))
                else:
                    if g or not (isinstance(b, int) and b == 0):
                        pe.wait_ge(o_ready, U * b + g)
                    for hh in range(G):
                        h = G * g + hh
                        r = 64 * (hh % 2)
                        mm = nc.tensor.matmul(o_ps[r:r + 64, hh // 2, :], v[q][:, DH * h:DH * h + DH],
                                              pT[g % 2][:, hh, :], start=True, stop=True)
                mm.then_inc(o_made, 1)

            def project_out(i, par, ahead):
                b, q = batch(i, par, ahead)
                pe.wait_ge(o_ready, (b + 1) if first else U * (b + 1))
                if not (isinstance(b, int) and b == 0):
                    pe.wait_ge(x_ready, b)
                elif first:
                    pe.wait_ge(bo_full, 1)
                for c in range(OC):
                    mm = nc.tensor.matmul(y_ps[:, 0, :], oT[q][:, c, :], wo[:, c, :], start=(c == 0), stop=(c == OC - 1))
                mm.then_inc(y_made, 1)

            def pair(i, is_first, is_last):
                for par in range(2):
                    has_before = not (is_first and par == 0)
                    has_next = not (is_last and par == 1)
                    for g in range(U):
                        turn_probs(i, par, g)
                        if g:
                            values(i, par, 0, g - 1)
                        elif has_before:
                            values(i, par, -1, U - 1)
                        if g == 0 and not is_last:
                            x_transpose(i, par, 2)
                        if g == 1 and has_before:
                            project_out(i, par, -1)
                        if g == 1 and has_next:
                            project_v(i, par, 1, 0)
                        if g == 2 and has_next and not first:
                            project_v(i, par, 1, 1)
                        if not is_last:
                            if first:
                                if g == 1:
                                    project_q(i, par, 2, 0)
                                if g == 2:
                                    project_k(i, par, 2)
                            else:
                                if g:
                                    project_q(i, par, 2, g - 1)
                                if g == 3:
                                    project_q(i, par, 2, 3)
                        if g < U - 1:
                            if has_next:
                                scores(i, par, 1, g + 1)
                        elif not is_last:
                            scores(i, par, 2, 0)

            pe.wait_ge(weights, 16 * NW)
            if first:
                pe.wait_ge(bv_ready, 1)
                nc.tensor.matmul(y_ps[:, 0, :], bv[:, :], wo[:, 0, :], start=True, stop=True).then_inc(bv_made, 1)
                pe.wait_ge(zeros_set, 3)
                for par in range(2):
                    x_transpose(0, par, 0)
                    project_q(0, par, 0, 0)
                    project_k(0, par, 0)
                    if par == 0:
                        project_v(0, par, 0, 0)
                for g in range(U):
                    scores(0, 0, 0, g)
            else:
                pe.wait_ge(k.wqk_ready, U)
                for par in range(2):
                    pe.wait_ge(xn_ready, par + 1)
                    nc.tensor.transpose(t_ps[par][:, 0, :], xn[par][:, :], k.ident[:, :]).then_inc(xnT_made, 1)

                def first_q(b, g):
                    pe.wait_ge(xnT_ready, b + 1)
                    if b and g in (1, 2):
                        pe.wait_ge(v_ready, g)
                    elif b:
                        pe.wait_ge(q_ready, g + 1)
                    for hh in range(G):
                        mm = nc.tensor.matmul(spread[g][:, hh, :], wqk[:, G * g + hh, :], xnT[b][:, :], start=True, stop=True)
                    mm.then_inc(q_made, 1)

                def first_v(half):
                    pe.wait_ge(ctx_in[0], 16)
                    pe.wait_ge(q_ready, half + 2)
                    nc.tensor.matmul(spread[1 + half][:, :, :].rearrange("p a b -> p (a b)"), ctxT[0][:, :],
                                     wv[:, half * 512:half * 512 + 512], start=True, stop=True).then_inc(v_made, 1)

                for g in range(U):
                    first_q(0, g)
                for half in range(VE):
                    scores(0, 0, 0, half)
                    first_v(half)
                for g in range(U):
                    first_q(1, g)
                    if g < 2:
                        scores(0, 0, 0, g + 2)
            scores(0, 1, 0, 0)
            pair(0, True, False)
            with pe.Fori(1, PAIRS - 1) as i:
                pair(i, False, False)
            pair(PAIRS - 1, False, True)
            values(PAIRS, 0, -1, U - 1)
            project_out(PAIRS, 0, -1)

        @block.scalar
        def _(act):
            def take_xnT(i, par, ahead, src=q_ps[:, 0, :]):
                b, q = batch(i, par, ahead)
                act.wait_ge(xnT_made, b + 1)
                if not (isinstance(i, int) and i == 0 and ahead == 0):
                    act.wait_ge(q_made, QE * (b - 1))
                nc.scalar.activation(xnT[q][:, :], src, ACT.Copy).then_inc(xnT_ready, 1)

            def take_k(i, par, ahead):
                b, q = batch(i, par, ahead)
                act.wait_ge(k_made, b + 1)
                if not (isinstance(i, int) and i == 0 and ahead == 0):
                    act.wait_ge(k_ready, b - 1)
                nc.scalar.activation(kraw[q][:, :], kv_ps[:, 0, :], ACT.Identity, bias=bqkv[:, 1:2]).then_inc(kraw_ready, 1)

            def take_v(i, par, ahead, half, bank=kv_ps):
                b, q = batch(i, par, ahead)
                act.wait_ge(v_made, VE * b + half + 1)
                if not (isinstance(i, int) and i == 0 and par + ahead < 2):
                    act.wait_ge(o_made, U * (b - 1))
                if first:
                    dst = v[q][:, :, :, :, :].rearrange("p h u c d -> p (h u c d)")
                    out = bass.AP(tensor=dst.tensor, offset=dst.offset,
                                  ap=[dst.ap[0], [D + DK, G], [G * DK, U], [1, DK]])
                    src = kv_ps[:, 0, :].rearrange("p (u h d) -> p h u d", u=U, h=G)
                    nc.scalar.activation(out, src, ACT.Copy).then_inc(v_ready, 1)
                else:
                    nc.scalar.activation(v[q][:, half * 512:half * 512 + 512],
                                         bank[:, :, :].rearrange("p a b -> p (a b)"), ACT.Copy).then_inc(v_ready, 1)

            def take_q(i, par, ahead, g, bank=q_ps):
                b, q = batch(i, par, ahead)
                act.wait_ge(q_made, QE * b + g + 1)
                if first:
                    if not (isinstance(i, int) and i == 0 and ahead == 0):
                        act.wait_ge(sc_made, U * (b - 1))
                    for u in range(U):
                        r = 32 * u
                        last = nc.scalar.activation(qT[q][r:r + 32, u, :], q_ps[r:r + 32, 0, :], ACT.Identity,
                                                    bias=bqkv[r:r + 32, 0:1])
                    last.then_inc(q_ready, 1)
                    return
                if not (isinstance(i, int) and i == 0 and ahead == 0):
                    act.wait_ge(sc_made, U * (b - 2) + g + 1)
                nc.scalar.activation(qT[q][:, G * g:G * g + G, :], bank[:, :, :], ACT.Copy).then_inc(q_ready, 1)

            def exponentials(i, par, ahead, g):
                b, q = batch(i, par, ahead)
                act.wait_ge(shifted, U * b + g + 1)
                p = probs[U * q + g][:, :, :]
                nc.scalar.activation(p, p, ACT.Exp, scale=scale).then_inc(exp_done, 1)

            def take_pT(i, par, g):
                b, q = batch(i, par)
                act.wait_ge(pT_made, U * b + g + 1)
                if g >= 2 or not (isinstance(b, int) and b == 0):
                    act.wait_ge(o_made, U * b + g - 1)
                nc.scalar.activation(pT[g % 2][:, :, :], t_ps[g % 2][:, :, :], ACT.Copy).then_inc(pT_ready, 1)

            def pair(i, is_first, is_last):
                for par in range(2):
                    has_next = not (is_last and par == 1)
                    for g in range(U):
                        take_pT(i, par, g)
                        if g == 0 and not is_last:
                            take_xnT(i, par, 2)
                        if g == 1 and has_next:
                            take_v(i, par, 1, 0)
                        if g == 2 and has_next and not first:
                            take_v(i, par, 1, 1)
                        if not is_last:
                            if first:
                                if g == 1:
                                    take_q(i, par, 2, 0)
                                if g == 2:
                                    take_k(i, par, 2)
                            else:
                                if g:
                                    take_q(i, par, 2, g - 1)
                                if g == 3:
                                    take_q(i, par, 2, 3)
                        if has_next:
                            exponentials(i, par, 1, g)

            if first:
                act.wait_ge(weights, 16 * NW)
                act.wait_ge(zeros_set, 3)
                for par in range(2):
                    take_xnT(0, par, 0)
                    take_q(0, par, 0, 0)
                    take_k(0, par, 0)
                    if par == 0:
                        take_v(0, par, 0, 0)
                for g in range(U):
                    exponentials(0, 0, 0, g)
            else:
                for par in range(2):
                    take_xnT(0, par, 0, t_ps[par][:, 0, :])
                for g in range(U):
                    take_q(0, 0, 0, g, spread[g])
                for half in range(VE):
                    take_v(0, 0, 0, half, spread[1 + half])
                for g in range(U):
                    take_q(0, 1, 0, g, spread[g])
                    exponentials(0, 0, 0, g)
            pair(0, True, False)
            with act.Fori(1, PAIRS - 1) as i:
                pair(i, False, False)
            pair(PAIRS - 1, False, True)

        @block.gpsimd
        def _(pool):
            if first:
                for q in range(2):
                    nc.gpsimd.memset(v[q][:, :, :, :, :], 0.0).then_inc(zeros_set, 1)
            pool.wait_ge(var_ready, 1)
            nc.gpsimd.tensor_tensor(k.rstd[:, :], k.var[:, :], k.half[:, :], ALU.pow).then_inc(rstd_ready, 1)
            pool.wait_ge(weights, 16 * NW)
            if first:
                pool.wait_ge(bo_full, 1)
                nc.gpsimd.memset(ones[:, :, :, :, :], 0.0).then_inc(base_own, 1)
                pool.wait_ge(base_own, 1)
                for hh in range(G):
                    nc.gpsimd.memset(ones[:, hh, :, hh, :], 1.0).then_inc(ones_set, 1)
            nc.gpsimd.tensor_scalar(bo[:, :], bo[:, :], k.tg[:, gate:gate + 1], None, ALU.mult).then_inc(base_own, 1)
            pool.wait_ge(base_own, 2 if first else 1)
            nc.gpsimd.tensor_tensor(k.base[:, :, :], k.x[:, :, :], rows(bo[:, :], B), ALU.add).then_inc(base_ready, 1)

            def mask_k(i, par, ahead):
                b, q = batch(i, par, ahead)
                pool.wait_ge(kraw_ready, b + 1)
                if not (isinstance(i, int) and i == 0 and ahead == 0):
                    pool.wait_ge(sc_made, U * (b - 1))
                nc.gpsimd.tensor_tensor(kT[q][:, :, :], rows(kraw[q][:, :], G), wide(headmask[:, :], S),
                                        ALU.mult).then_inc(k_ready, 1)

            def normalize(i, par, ahead, g):
                b, q = batch(i, par, ahead)
                pool.wait_ge(inv_ready, U * b + g + 1)
                p = probs[U * q + g][:, :, :]
                nc.gpsimd.tensor_tensor(p, p, wide(inv[U * q + g][:, :], S), ALU.mult).then_inc(probs_ready, 1)

            def pair(i, is_last):
                for par in range(2):
                    has_next = not (is_last and par == 1)
                    for g in range(U):
                        if first:
                            pass
                        elif g == 0:
                            normalize(i, par, 0, U - 1)
                        elif has_next:
                            normalize(i, par, 1, g - 1)
                        if g == 2 and first and not is_last:
                            mask_k(i, par, 2)

            if first:
                mask_k(0, 0, 0)
                mask_k(0, 1, 0)
            for g in range(0 if first else U - 1):
                normalize(0, 0, 0, g)
            pair(0, False)
            with pool.Fori(1, PAIRS - 1) as i:
                pair(i, False)
            pair(PAIRS - 1, True)

        @block.vector
        def _(dve):
            def norm(i, par, ahead):
                b, q = batch(i, par, ahead)
                if not (isinstance(i, int) and i == 0 and ahead == 0):
                    dve.wait_ge(xnT_made, b - 1)
                if isinstance(b, int):
                    mean, rstd, x = k.mean[:, b:b + 1], k.rstd[:, b:b + 1], k.x[:, b, :]
                else:
                    mean, rstd, x = k.mean[:, bass.ds(b, 1)], k.rstd[:, bass.ds(b, 1)], k.x[:, b, :]
                nc.vector.tensor_scalar(xn[q][:, :], x, mean, rstd, ALU.subtract, ALU.mult).then_inc(xn_ready, 1)

            def make_bias(i, par, ahead):
                b, q = batch(i, par, ahead)
                if not (isinstance(i, int) and i == 0 and ahead == 0):
                    dve.wait_ge(masked, U * (b - 1))
                nc.vector.scalar_tensor_tensor(out=bias[q][:, :], in0=hidden[:, b, :], scalar=-FMAX,
                                               in1=causal[:, :], op0=ALU.mult, op1=ALU.min).then_inc(bias_ready, 1)

            def find_top(i, par, ahead, g):
                b, q = batch(i, par, ahead)
                n = U * b + g
                p = probs[U * q + g][:, :, :]
                dve.wait_ge(sc_made, n + 1)
                if not (isinstance(i, int) and i == 0 and par + ahead < 2):
                    dve.wait_ge(pT_made, n - 2 * U + 1)
                if first:
                    nc.vector.tensor_reduce(top[U * q + g][:, :], sc_ps[g % 2][:, :, :], AX, ALU.max).then_inc(top_ready, 1)
                else:
                    dve.wait_ge(bias_ready, b + 1)
                    nc.vector.tensor_tensor(p, sc_ps[g % 2][:, :, :], rows(bias[q][:, :], G), ALU.add).then_inc(masked, 1)
                    dve.wait_ge(masked, n + 1)
                    nc.vector.tensor_reduce(top[U * q + g][:, :], p, AX, ALU.max).then_inc(top_ready, 1)

            def shift(i, par, ahead, g):
                b, q = batch(i, par, ahead)
                p = probs[U * q + g][:, :, :]
                dve.wait_ge(top_ready, U * b + g + 1)
                src = sc_ps[g % 2][:, :, :] if first else p
                nc.vector.tensor_tensor(p, src, wide(top[U * q + g][:, :], S), ALU.subtract).then_inc(shifted, 1)

            def add_up(i, par, ahead, g):
                b, q = batch(i, par, ahead)
                dve.wait_ge(exp_done, U * b + g + 1)
                nc.vector.tensor_reduce(total[U * q + g][:, :], probs[U * q + g][:, :, :], AX, ALU.add).then_inc(total_ready, 1)

            def invert(i, par, ahead, g):
                b, q = batch(i, par, ahead)
                dve.wait_ge(total_ready, U * b + g + 1)
                nc.vector.reciprocal(inv[U * q + g][:, :], total[U * q + g][:, :]).then_inc(inv_ready, 1)

            def take_o(i, par, ahead, g):
                b, q = batch(i, par, ahead)
                dve.wait_ge(o_made, U * b + g + 1)
                if not (isinstance(i, int) and i == 0 and par + ahead < 2):
                    dve.wait_ge(y_made, b - 1)
                if first:
                    nc.vector.reciprocal(oinv[q][:, :], o_ps[:, 1, :]).then_inc(oinv_ready, 1)
                    dve.wait_ge(oinv_ready, b + 1)
                    nc.vector.tensor_tensor(oT[q][:, 0, :], o_ps[:, 0, :], oinv[q][:, :], ALU.mult).then_inc(o_ready, 1)
                else:
                    nc.vector.tensor_copy(oT[q][:, 2 * g:2 * g + 2, :], o_ps[:, 0:2, :]).then_inc(o_ready, 1)

            def finish(i, par, ahead):
                b, q = batch(i, par, ahead)
                dve.wait_ge(y_made, b + 1)
                nc.vector.scalar_tensor_tensor(out=k.x[:, b, :], in0=y_ps[:, 0, :], scalar=k.tg[:, gate:gate + 1],
                                               in1=k.base[:, b, :], op0=ALU.mult, op1=ALU.add).then_inc(x_ready, 1)

            def row_stats(i, par, ahead):
                b, q = batch(i, par, ahead)
                dve.wait_ge(x_ready, b + 1)
                nc.vector.bn_stats(k.stats[:, b, :], k.x[:, b, :]).then_inc(stats_ready, 1)

            def pair(i, is_first, is_last):
                for par in range(2):
                    has_before = not (is_first and par == 0)
                    has_next = not (is_last and par == 1)
                    for g in range(U):
                        if g == 0 and not is_last:
                            norm(i, par, 2)
                        if has_next:
                            find_top(i, par, 1, g)
                        if first:
                            pass
                        elif g == 0:
                            add_up(i, par, 0, U - 1)
                        elif has_next:
                            add_up(i, par, 1, g - 1)
                        if has_next:
                            shift(i, par, 1, g)
                        if first:
                            pass
                        elif g == 0:
                            invert(i, par, 0, U - 1)
                        elif has_next:
                            invert(i, par, 1, g - 1)
                        if first:
                            if g == 0 and has_before:
                                take_o(i, par, -1, U - 1)
                        else:
                            if g:
                                take_o(i, par, 0, g - 1)
                            elif has_before:
                                take_o(i, par, -1, U - 1)
                            if g == 3 and not is_last:
                                make_bias(i, par, 2)
                        if g == 1 and has_before:
                            finish(i, par, -1)
                        if g == 2 and has_before:
                            row_stats(i, par, -1)

            norm_stats(nc, dve, k, norm_own, var_ready)
            if first:
                for q in range(2):
                    last = nc.vector.memset(qT[q][:, :, :], 0.0)
                last.then_inc(zeros_set, 1)
                dve.wait_ge(weights, 16 * NW)
                nc.vector.tensor_scalar(bv[:, :], k.ident[:, :], 0.0, bqkv[:, 2:3], ALU.mult, ALU.add).then_inc(bv_ready, 1)
                dve.wait_ge(bv_made, 1)
                nc.vector.tensor_tensor(bo[:, :], y_ps[:, 0, :], bo[:, :], ALU.add).then_inc(bo_full, 1)
            dve.wait_ge(weights, 16 * NW)
            if first:
                dve.wait_ge(zeros_set, 3)
            dve.wait_ge(rstd_ready, 1)
            for par in range(2):
                norm(0, par, 0)
                if not first:
                    make_bias(0, par, 0)
            for g in range(U):
                find_top(0, 0, 0, g)
                shift(0, 0, 0, g)
                if g and not first:
                    add_up(0, 0, 0, g - 1)
                    invert(0, 0, 0, g - 1)
            dve.wait_ge(base_ready, 1)
            pair(0, True, False)
            with dve.Fori(1, PAIRS - 1) as i:
                pair(i, False, False)
            pair(PAIRS - 1, False, True)
            take_o(PAIRS, 0, -1, U - 1)
            finish(PAIRS, 0, -1)
            row_stats(PAIRS, 0, -1)
            dve.wait_ge(stats_ready, B)


def experts_phase(nc, k, w, layer):
    first = layer == 0
    gate = 2 + layer
    PICKS = 2 if first else 1
    NT = NTILES[layer]
    tg = k.tg[:, gate:gate + 1]
    slots_dram, out_dram = k.slots[layer], k.outs[layer]

    with ExitStack() as ctx:
        t = Tools(nc, ctx, f"ffn{layer}", k.used)
        router = t.sb("router", [128, E])
        iota = t.sb("iota", [128, E])
        iota_tile = t.sb("iota_tile", [128, NT])
        edges = t.sb("edges", [128, B])
        before = t.sb("before", [128, 128])
        ones = t.sb("ones", [128, 128])
        ids = t.sb("ids", [128, PICKS, B], I32)
        rowbuf = [t.sb(f"rowbuf{p}", [128, B, ROW]) for p in range(PICKS)]
        xn = [t.sb(f"xn{i}", [128, D]) for i in range(2)]
        xrT = [t.sb(f"xrT{i}", [128, S]) for i in range(2)]
        if first:
            xT = t.sb("xT", [128, B, S])
            sup, sdown = t.sb("sup", [128, F]), t.sb("sdown", [128, FC, D])
            shT = [t.sb(f"shT{i}", [128, FC, GT]) for i in range(2)]
            wqT, wkT = t.sb("wqT", [DH, HEADS, D]), t.sb("wkT", [DH, HEADS, D])
        else:
            router_b = t.sb("router_b", [128, E])
            weight = t.sb("weight", [128, B])
        pr, o1, o2, tmp = (t.sb(n, [128, B, E]) for n in ("pr", "o1", "o2", "tmp"))
        top, total, m1, i1, m2, i2 = (t.sb(n, [128, B]) for n in ("top", "total", "m1", "i1", "m2", "i2"))
        uses = t.sb("uses", [128, B, E])
        count = t.sb("count", [128, E, B])
        upto = [t.sb(f"upto{i}", [128, E, B]) for i in range(2)]
        tiles = t.sb("tiles", [128, E])
        tupto = [t.sb(f"tupto{i}", [128, E]) for i in range(2)]
        slot = [t.sb(f"slot{p}", [128, B], I32) for p in range(PICKS)]
        at = t.sb("at", [128, NT, E])
        tile_e = t.sb("tile_e", [128, NT])
        tile_i = t.sb("tile_i", [128, NT], I32)
        xin = [t.sb(f"xin{i}", [128, ROW]) for i in range(R)]
        xt = [t.sb(f"xt{i}", [128, 128]) for i in range(2)]
        h = [t.sb(f"h{i}", [128, F]) for i in range(2)]
        hT = [t.sb(f"hT{i}", [128, FC, 128]) for i in range(2)]
        y = [t.sb(f"y{i}", [128, D]) for i in range(R)]
        z = t.sb("z", [128, PICKS, B, D])

        bank = [t.ps(f"bank{i}", [128, 512]) for i in range(8)]
        tr_ps = bank[6][:, 0:128]
        lg_ps = bank[7][:, 0:B * E].rearrange("p (b e) -> p b e", e=E)
        rank_ps = bank[5][:, 0:B * E]
        count_ps = bank[5][:, 128:128 + B * E]
        sup_ps, sdn_ps = bank[0:4], bank[4:6]
        up_ps, turn_ps, y_ps = bank[0:2], bank[2:4], bank[4:6]

        consts, shared_in = t.sem("consts"), t.sem("shared_in")
        norm_own, var_ready, rstd_ready = t.sem("norm_own"), t.sem("var_ready"), t.sem("rstd_ready")
        xn_ready, xnT_made, xr_ready = t.sem("xn_ready"), t.sem("xnT_made"), t.sem("xr_ready")
        rows_ready, lg_made, shifted, e_ready, own = (t.sem(n) for n in ("rows_ready", "lg_made", "shifted", "e_ready", "own"))
        uses_ready, rank_made, slots_ready, ids_set, scattered, plan_ready = (
            t.sem(n) for n in ("uses_ready", "rank_made", "slots_ready", "ids_set", "scattered", "plan_ready"))
        if first:
            qk_in, wqk_made = t.sem("qk_in"), t.sem("wqk_made")
            xT_ready, sup_made, sh_ready, sdn_made, sdn_taken = (
                t.sem(n) for n in ("xT_ready", "sup_made", "sh_ready", "sdn_made", "sdn_taken"))
        tile_in = [t.sem(f"tile_in{i}") for i in range(R)]
        puts_begun = t.sem("puts_begun")
        tile_out = [t.sem(f"tile_out{i}") for i in range(R)]
        xt_made, xt_ready, up_made, h_ready, turned, hT_ready, y_made, y_ready = (
            t.sem(n) for n in ("xt_made", "xt_ready", "up_made", "h_ready", "turned", "hT_ready", "y_made", "y_ready"))
        z_in = [t.sem(f"z_in{g}") for g in range(GROUPS)]
        z1_added, z_added, stats_ready, stored = t.sem("z1_added"), t.sem("z_added"), t.sem("stats_ready"), t.sem("stored")
        block = ctx.enter_context(nc.Block())
        NC = 7 if first else 8

        def all_tiles(step, engine):
            for r in range(R):
                step(r, 0, r, True)
            with engine.Fori(1, NT // R) as i:
                for r in range(R):
                    step(R * i + r, i, r, False)
            for r in range(NT % R):
                step(NT - NT % R + r, NT // R, r, False)

        def left(tile):
            return NT - 1 - tile if isinstance(tile, int) else 3

        @block.sync
        def _(sp):
            loads = [(router[:, :], w[f"router{layer}"]), (iota[:, :], w["iota"].partition_broadcast(128)),
                     (iota_tile[:, :], w["iota_tile"][0:NT].partition_broadcast(128)),
                     (edges[:, :], w["edges"].partition_broadcast(128)), (before[:, :], w["before"]),
                     (ones[:, :], w["ones"]), (ids[:, :, :], w["ids"][:, 0:PICKS, :])]
            if not first:
                loads += [(router_b[:, :], w["router_b1"].partition_broadcast(128))]
            for dst, src in loads:
                sp.dma_start(dst, src).then_inc(consts, 16)
            if first:
                sp.dma_start(sup[:, :], w["shared_up"]).then_inc(shared_in, 16)
                sp.dma_start(sdown[:, :, :], w["shared_down"]).then_inc(shared_in, 16)
                for dst, src in [(wqT[:, :, :], w["wqT1"]), (wkT[:, :, :], w["wkT1"])]:
                    sp.dma_start(dst, src).then_inc(qk_in, 16)
                for dst, src in [(k.wv1[:, :], w["wv1"]), (k.wo1[:, :, :], w["wo1"]),
                                 (k.bo1[:, :], w["bo1"].partition_broadcast(128)), (k.causal[:, :], w["causal"]),
                                 (k.hidden[:, :, :], w["mask"].partition_broadcast(128))]:
                    sp.dma_start(dst, src).then_inc(k.att1_in, 16)
            sp.wait_ge(scattered, 16 * PICKS * B)

            def load(tile, i, r, is_first):
                if not is_first:
                    sp.wait_ge(tile_out[r], 16 * i)
                sp.dma_start(xin[r][:, :], slots_dram[tile]).then_inc(tile_in[r], 16)

            all_tiles(load, sp)
            for r in range(R):
                sp.wait_ge(tile_out[r], 16 * len(range(r, NT, R)))
            for g in range(GROUPS):
                for p in range(PICKS):
                    src = out_dram[p * B + GB * g:p * B + GB * g + GB].rearrange("b s d -> s b d")
                    sp.dma_start(z[:, p, GB * g:GB * g + GB, :], src).then_inc(z_in[g], 16)
            if not first:
                for g in range(GROUPS):
                    sp.wait_ge(z_added, g + 1)
                    sp.dma_start(w["out"][:, GB * g:GB * g + GB, :], k.x[:, GB * g:GB * g + GB, :]).then_inc(stored, 16)
                sp.wait_ge(stored, 16 * GROUPS)

        @block.tensor
        def _(pe):
            def turn_pair(i, is_first):
                for par in range(2):
                    b = 2 * i + par
                    pe.wait_ge(xn_ready, b + 1)
                    if not (is_first and par == 0):
                        pe.wait_ge(xr_ready, b)
                    nc.tensor.transpose(tr_ps, xn[par][:, :], k.ident[:, :]).then_inc(xnT_made, 1)
                    pe.wait_ge(xr_ready, b + 1)
                    nc.tensor.matmul(lg_ps[:, b, :], xrT[par][:, :], router[:, :], start=True, stop=True).then_inc(lg_made, 1)

            pe.wait_ge(consts, 16 * NC)
            turn_pair(0, True)
            with pe.Fori(1, PAIRS) as i:
                turn_pair(i, False)

            def shared_up(g):
                pe.wait_ge(xT_ready, GB * (g + 1))
                for c in range(FC):
                    if g:
                        pe.wait_ge(sh_ready, FC * (g - 1) + c + 1)
                    nc.tensor.matmul(sup_ps[c][:, :], sup[:, 128 * c:128 * c + 128],
                                     xT[:, GB * g:GB * g + GB, :].rearrange("p a b -> p (a b)"),
                                     start=True, stop=True).then_inc(sup_made, 1)

            def shared_down(g):
                pe.wait_ge(sh_ready, FC * (g + 1))
                if g >= 2:
                    pe.wait_ge(sdn_taken, g - 1)
                for s in range(GB):
                    for c in range(FC):
                        mm = nc.tensor.matmul(sdn_ps[g % 2][:, 128 * s:128 * s + 128], shT[g % 2][:, c, S * s:S * s + S],
                                              sdown[:, c, :], start=(c == 0), stop=(c == FC - 1))
                mm.then_inc(sdn_made, 1)

            def ranks():
                pe.wait_ge(uses_ready, 1)
                u = uses[:, :, :].rearrange("p b e -> p (b e)")
                nc.tensor.matmul(rank_ps, before[:, :], u, start=True, stop=True)
                nc.tensor.matmul(count_ps, ones[:, :], u, start=True, stop=True).then_inc(rank_made, 1)

            if first:
                pe.wait_ge(shared_in, 32)
                shared_up(0)
                shared_up(1)
                ranks()
                shared_down(0)
                pe.wait_ge(slots_ready, PICKS)
                for g in range(1, GROUPS):
                    if g + 1 < GROUPS:
                        shared_up(g + 1)
                    shared_down(g)
                pe.wait_ge(qk_in, 32)
                for u in range(U):
                    for hh in range(G):
                        mm = nc.tensor.matmul(sup_ps[u][:, D * hh:D * hh + D], wqT[:, G * u + hh, :], wkT[:, G * u + hh, :],
                                              start=True, stop=True)
                    mm.then_inc(wqk_made, 1)
                pe.wait_ge(k.wqk_ready, U)
                pe.wait_ge(sdn_taken, GROUPS)
            else:
                ranks()
            pe.wait_ge(plan_ready, 1)
            pe.wait_ge(k.w_in[layer], 32)

            def turn_x(tile, i, r):
                pe.wait_ge(tile_in[r], 16 * (i + 1))
                if not (isinstance(tile, int) and tile == 0):
                    pe.wait_ge(xt_ready, tile)
                nc.tensor.transpose(tr_ps, xin[r][:, 0:D], k.ident[:, :]).then_inc(xt_made, 1)

            def expert_of(tile):
                at = tile_i[0:1, tile:tile + 1] if isinstance(tile, int) else tile_i[0:1, bass.ds(tile, 1)]
                return pe.value_load(at, min_val=0, max_val=E - 1)

            def up(tile, r):
                e = expert_of(tile)
                pe.wait_ge(xt_ready, tile + 1)
                if not (isinstance(tile, int) and tile < 2):
                    pe.wait_ge(h_ready, tile - 1)
                nc.tensor.matmul(up_ps[r % 2][:, :], xt[r % 2][:, :], k.wup[:, e, :], start=True, stop=True).then_inc(up_made, 1)

            def turn_h(tile, r):
                pe.wait_ge(h_ready, tile + 1)
                if not (isinstance(tile, int) and tile < 2):
                    pe.wait_ge(hT_ready, tile - 1)
                for c in range(FC):
                    mm = nc.tensor.transpose(turn_ps[r % 2][:, 128 * c:128 * c + 128], h[r % 2][:, 128 * c:128 * c + 128], k.ident[:, :])
                mm.then_inc(turned, 1)

            def down(tile, r):
                e = expert_of(tile)
                pe.wait_ge(hT_ready, tile + 1)
                if not (isinstance(tile, int) and tile < 2):
                    pe.wait_ge(y_ready, tile - 1)
                for c in range(FC):
                    mm = nc.tensor.matmul(y_ps[r % 2][:, 0:D], hT[r % 2][:, c, :], k.wdn[:, e, c, :], start=(c == 0), stop=(c == FC - 1))
                mm.then_inc(y_made, 1)

            def step(tile, i, r, is_first):
                if left(tile) >= 3:
                    turn_x(tile + 3, i + (r + 3) // R, (r + 3) % R)
                if left(tile) >= 2:
                    up(tile + 2, r + 2)
                if left(tile) >= 1:
                    turn_h(tile + 1, r + 1)
                down(tile, r)

            for r in range(3):
                turn_x(r, 0, r)
                if r < 2:
                    up(r, r)
            turn_h(0, 0)
            all_tiles(step, pe)

        @block.scalar
        def _(act):
            def take(b, par, is_first):
                act.wait_ge(xnT_made, b + 1)
                if not is_first:
                    act.wait_ge(lg_made, b - 1)
                    if first:
                        act.wait_ge(xT_ready, b - 1)
                nc.scalar.activation(xrT[par][:, :], tr_ps, ACT.Copy).then_inc(xr_ready, 1)

            for par in range(2):
                take(par, par, True)
            with act.Fori(1, PAIRS) as i:
                for par in range(2):
                    take(2 * i + par, par, False)
            act.wait_ge(shifted, 1)
            nc.scalar.activation(pr[:, :, :], pr[:, :, :], ACT.Exp).then_inc(e_ready, 1)
            if first:
                for g in range(GROUPS):
                    if g >= 2:
                        act.wait_ge(sdn_made, g - 1)
                    for c in range(FC):
                        act.wait_ge(sup_made, FC * g + c + 1)
                        nc.scalar.activation(shT[g % 2][:, c, :], sup_ps[c][:, :], ACT.Gelu).then_inc(sh_ready, 1)
                for u in range(U):
                    act.wait_ge(wqk_made, u + 1)
                    nc.scalar.activation(k.wqk[:, G * u:G * u + G, :].rearrange("p h d -> p (h d)"), sup_ps[u][:, :],
                                         ACT.Copy).then_inc(k.wqk_ready, 1)

            def take_x(tile, r):
                act.wait_ge(xt_made, tile + 1)
                if not (isinstance(tile, int) and tile < 2):
                    act.wait_ge(up_made, tile - 1)
                nc.scalar.activation(xt[r % 2][:, :], tr_ps, ACT.Copy).then_inc(xt_ready, 1)

            def hidden(tile, r):
                act.wait_ge(turned, tile + 1)
                if not (isinstance(tile, int) and tile < 2):
                    act.wait_ge(y_made, tile - 1)
                nc.scalar.activation(hT[r % 2][:, :, :].rearrange("p c s -> p (c s)"), turn_ps[r % 2][:, :],
                                     ACT.Gelu if first else ACT.Relu).then_inc(hT_ready, 1)

            def step(tile, i, r, is_first):
                if left(tile) >= 3:
                    take_x(tile + 3, r + 3)
                if left(tile) >= 1:
                    hidden(tile + 1, r + 1)

            for r in range(3):
                take_x(r, r)
            hidden(0, 0)
            all_tiles(step, act)

        @block.gpsimd
        def _(pool):
            pool.wait_ge(var_ready, 1)
            nc.gpsimd.tensor_tensor(k.rstd[:, :], k.var[:, :], k.half[:, :], ALU.pow).then_inc(rstd_ready, 1)
            pool.wait_ge(consts, 16 * NC)
            for p in range(PICKS):
                nc.gpsimd.tensor_copy(rowbuf[p][:, :, D].bitcast(I32), ids[:, p, :]).then_inc(ids_set, 1)
            if first:
                with pool.Fori(0, PAIRS) as i:
                    for par in range(2):
                        pool.wait_ge(xr_ready, 2 * i + par + 1)
                        nc.gpsimd.tensor_copy(xT[:, 2 * i + par, :], xrT[par][:, :]).then_inc(xT_ready, 1)
            pool.wait_ge(ids_set, PICKS)
            pool.wait_ge(k.slots_set, 32)
            for p in range(PICKS):
                pool.wait_ge(slots_ready, p + 1)
                pool.wait_ge(rows_ready, B if p == 0 else B + 1)
                for b in range(B):
                    nc.gpsimd.indirect_dma_start(slots_dram.rearrange("t s c -> (t s) c"),
                                                 bass.IndirectOffsetOnAxis(slot[p][:, b:b + 1], 0),
                                                 rowbuf[p][:, b, :], None).then_inc(scattered, 16)

            def put(tile, i, r, is_first):
                pool.wait_ge(y_ready, tile + 1)
                pool.wait_ge(tile_in[r], 16 * (i + 1))
                pool.sem_inc(puts_begun, 1)
                nc.gpsimd.indirect_dma_start(out_dram.rearrange("b s d -> (b s) d"),
                                             bass.IndirectOffsetOnAxis(xin[r][:, D:D + 1].bitcast(I32), 0),
                                             y[r][:, :], None).then_inc(tile_out[r], 16)

            all_tiles(put, pool)

        @block.vector
        def _(dve):
            V = nc.vector
            norm_stats(nc, dve, k, norm_own, var_ready)
            dve.wait_ge(rstd_ready, 1)

            def norm(i, is_first):
                for par in range(2):
                    b = 2 * i + par
                    if not is_first:
                        dve.wait_ge(xnT_made, b - 1)
                    mean = k.mean[:, b:b + 1] if isinstance(b, int) else k.mean[:, bass.ds(b, 1)]
                    rstd = k.rstd[:, b:b + 1] if isinstance(b, int) else k.rstd[:, bass.ds(b, 1)]
                    V.tensor_scalar(xn[par][:, :], k.x[:, b, :], mean, rstd, ALU.subtract, ALU.mult).then_inc(xn_ready, 1)
                    V.tensor_scalar(rowbuf[0][:, b, 0:D], k.x[:, b, :], mean, rstd, ALU.subtract, ALU.mult).then_inc(rows_ready, 1)

            norm(0, True)
            with dve.Fori(1, PAIRS) as i:
                norm(i, False)
            dve.wait_ge(rows_ready, B)
            if first:
                V.tensor_copy(rowbuf[1][:, :, 0:D], rowbuf[0][:, :, 0:D]).then_inc(rows_ready, 1)
                V.scalar_tensor_tensor(out=k.x[:, :, :], in0=rowbuf[0][:, :, 0:D], scalar=tg, in1=k.x[:, :, :],
                                       op0=ALU.mult, op1=ALU.add).then_inc(norm_own, 1)

            made = [0]

            def step(ins):
                made[0] += 1
                ins.then_inc(own, 1)
                dve.wait_ge(own, made[0])

            dve.wait_ge(lg_made, B)
            dve.wait_ge(consts, 16 * NC)
            it = rows(iota[:, :], B)
            if first:
                step(V.tensor_copy(pr[:, :, :], lg_ps))
            else:
                step(V.tensor_tensor(pr[:, :, :], lg_ps, rows(router_b[:, :], B), ALU.add))
            step(V.tensor_reduce(top[:, :], pr[:, :, :], AX, ALU.max))
            V.tensor_tensor(pr[:, :, :], pr[:, :, :], wide(top[:, :], E), ALU.subtract).then_inc(shifted, 1)
            dve.wait_ge(e_ready, 1)
            step(V.tensor_reduce(total[:, :], pr[:, :, :], AX, ALU.add))
            step(V.reciprocal(total[:, :], total[:, :]))
            step(V.tensor_tensor(pr[:, :, :], pr[:, :, :], wide(total[:, :], E), ALU.mult))

            def pick(prob, m, idx, onehot):
                step(V.tensor_reduce(m[:, :], prob, AX, ALU.max))
                step(V.tensor_tensor(tmp[:, :, :], prob, wide(m[:, :], E), ALU.is_lt))
                step(V.scalar_tensor_tensor(out=tmp[:, :, :], in0=tmp[:, :, :], scalar=float(E), in1=it, op0=ALU.mult, op1=ALU.add))
                step(V.tensor_reduce(idx[:, :], tmp[:, :, :], AX, ALU.min))
                step(V.tensor_tensor(onehot, it, wide(idx[:, :], E), ALU.is_equal))

            pick(pr[:, :, :], m1, i1, o1[:, :, :])
            step(V.scalar_tensor_tensor(out=o2[:, :, :], in0=o1[:, :, :], scalar=-2.0, in1=pr[:, :, :], op0=ALU.mult, op1=ALU.add))
            pick(o2[:, :, :], m2, i2, o2[:, :, :])
            if first:
                V.tensor_tensor(uses[:, :, :], o1[:, :, :], o2[:, :, :], ALU.add).then_inc(uses_ready, 1)
                V.tensor_scalar(rowbuf[0][:, :, D + 1], m1[:, :], tg, None, ALU.mult)
                V.tensor_scalar(rowbuf[1][:, :, D + 1], m2[:, :], tg, None, ALU.mult)
            else:
                step(V.tensor_scalar(i2[:, :], i2[:, :], 1.0, None, ALU.add))
                step(V.tensor_scalar(top[:, :], m2[:, :], 0.0, None, ALU.is_gt))
                step(V.tensor_tensor(i2[:, :], i2[:, :], top[:, :], ALU.mult))
                step(V.scalar_tensor_tensor(out=i1[:, :], in0=i2[:, :], scalar=-1.0, in1=i1[:, :], op0=ALU.add, op1=ALU.max))
                V.tensor_tensor(uses[:, :, :], it, wide(i1[:, :], E), ALU.is_equal).then_inc(uses_ready, 1)
                dve.wait_ge(uses_ready, 1)
                step(V.tensor_tensor(o2[:, :, :], uses[:, :, :], pr[:, :, :], ALU.mult))
                step(V.tensor_reduce(weight[:, :], o2[:, :, :], AX, ALU.add))
                V.tensor_tensor(rowbuf[0][:, :, 0:D], rowbuf[0][:, :, 0:D], wide(weight[:, :], D), ALU.mult)
                V.memset(rowbuf[0][:, :, D + 1], 0.0)

            dve.wait_ge(rank_made, 1)
            step(V.tensor_copy(count[:, :, :], count_ps.rearrange("p (b e) -> p e b", e=E)))
            now = count
            for n, shift in enumerate((1, 2, 4, 8)):
                new = upto[n % 2]
                V.tensor_copy(new[:, :, 0:shift], now[:, :, 0:shift]).then_inc(own, 1)
                made[0] += 1
                step(V.tensor_tensor(new[:, :, shift:B], now[:, :, shift:B], now[:, :, 0:B - shift], ALU.add))
                now = new
            through = now
            step(V.tensor_tensor(at[:, 0:B, :].rearrange("p b e -> p e b"), wide(through[:, :, B - 1], B), rows(edges[:, :], E), ALU.is_gt))
            step(V.tensor_reduce(tiles[:, :], at[:, 0:B, :].rearrange("p b e -> p e b"), AX, ALU.add))
            now = tiles
            for n, shift in enumerate((1, 2, 4)):
                new = tupto[n % 2]
                V.tensor_copy(new[:, 0:shift], now[:, 0:shift]).then_inc(own, 1)
                made[0] += 1
                step(V.tensor_tensor(new[:, shift:E], now[:, shift:E], now[:, 0:E - shift], ALU.add))
                now = new
            ends = now
            spare = tupto[1]
            step(V.tensor_tensor(spare[:, :], ends[:, :], tiles[:, :], ALU.subtract))
            step(V.tensor_tensor(count[:, :, :], through[:, :, :], count[:, :, :], ALU.subtract))
            step(V.scalar_tensor_tensor(out=count[:, :, :], in0=wide(spare[:, :], B), scalar=128.0, in1=count[:, :, :],
                                        op0=ALU.mult, op1=ALU.add))
            step(V.tensor_tensor(tmp[:, :, :], rank_ps.rearrange("p (b e) -> p b e", e=E),
                                 count[:, :, :].rearrange("p e b -> p b e"), ALU.add))
            for p in range(PICKS):
                onehot = (o1 if p == 0 else o2) if first else uses
                step(V.tensor_tensor(pr[:, :, :], onehot[:, :, :], tmp[:, :, :], ALU.mult))
                step(V.tensor_reduce(top[:, :], pr[:, :, :], AX, ALU.add))
                V.tensor_copy(slot[p][:, :], top[:, :]).then_inc(slots_ready, 1)
                dve.wait_ge(slots_ready, p + 1)
            step(V.tensor_tensor(at[:, :, :], rows(ends[:, :], NT), wide(iota_tile[:, :], E), ALU.is_le))
            step(V.tensor_reduce(tile_e[:, :], at[:, :, :], AX, ALU.add))
            V.tensor_scalar(tile_i[:, :], tile_e[:, :], float(E - 1), None, ALU.min).then_inc(plan_ready, 1)

            if first:
                for g in range(GROUPS):
                    dve.wait_ge(sdn_made, g + 1)
                    xg = k.x[:, GB * g:GB * g + GB, :]
                    V.scalar_tensor_tensor(out=xg, in0=sdn_ps[g % 2][:, :].rearrange("p (b d) -> p b d", d=D), scalar=tg,
                                           in1=xg, op0=ALU.mult, op1=ALU.add).then_inc(sdn_taken, 1)
            else:
                dve.wait_ge(plan_ready, 1)
                dve.wait_ge(k.bias_in, 32)

            def expert_of(tile):
                at = tile_i[0:1, tile:tile + 1] if isinstance(tile, int) else tile_i[0:1, bass.ds(tile, 1)]
                return dve.value_load(at, min_val=0, max_val=E - 1)

            def take_h(tile, r):
                if not first:
                    e = expert_of(tile)
                dve.wait_ge(up_made, tile + 1)
                if not (isinstance(tile, int) and tile < 2):
                    dve.wait_ge(turned, tile - 1)
                if first:
                    V.tensor_copy(h[r % 2][:, :], up_ps[r % 2][:, :]).then_inc(h_ready, 1)
                else:
                    V.tensor_tensor(h[r % 2][:, :], up_ps[r % 2][:, :], k.b1[:, e, :], ALU.add).then_inc(h_ready, 1)

            def take_y(tile, i, r, is_first):
                if not first:
                    e = expert_of(tile)
                dve.wait_ge(y_made, tile + 1)
                if not is_first:
                    dve.wait_ge(tile_out[r], 16 * i)
                if first:
                    dve.wait_ge(tile_in[r], 16 * (i + 1))
                    V.tensor_scalar(y[r][:, :], y_ps[r % 2][:, 0:D], xin[r][:, D + 1:D + 2], None, ALU.mult).then_inc(y_ready, 1)
                else:
                    V.tensor_tensor(y[r][:, :], y_ps[r % 2][:, 0:D], k.b2[:, e, :], ALU.add).then_inc(y_ready, 1)

            def tile_step(tile, i, r, is_first):
                if left(tile) >= 2:
                    take_h(tile + 2, r + 2)
                take_y(tile, i, r, is_first)

            take_h(0, 0)
            take_h(1, 1)
            all_tiles(tile_step, dve)
            if first:
                dve.wait_ge(sdn_taken, GROUPS)
            for g in range(GROUPS):
                dve.wait_ge(z_in[g], 16 * PICKS)
                xg = k.x[:, GB * g:GB * g + GB, :]
                if first:
                    V.tensor_tensor(xg, z[:, 0, GB * g:GB * g + GB, :], xg, ALU.add).then_inc(z1_added, 1)
                    dve.wait_ge(z1_added, g + 1)
                    V.tensor_tensor(xg, z[:, 1, GB * g:GB * g + GB, :], xg, ALU.add).then_inc(z_added, 1)
                    dve.wait_ge(z_added, g + 1)
                    for b in range(GB * g, GB * g + GB):
                        V.bn_stats(k.stats[:, b, :], k.x[:, b, :]).then_inc(stats_ready, 1)
                else:
                    V.scalar_tensor_tensor(out=xg, in0=z[:, 0, GB * g:GB * g + GB, :], scalar=tg, in1=xg,
                                           op0=ALU.mult, op1=ALU.add).then_inc(z_added, 1)


class Kept:
    pass


def flamingo(nc, w):
    with ExitStack() as ctx:
        t = Tools(nc, ctx, "kept", [])
        k = Kept()
        k.used = []
        k.x = t.sb("x", [128, B, D])
        k.base = t.sb("base", [128, B, D])
        k.ident = t.sb("ident", [128, 128])
        k.graw = t.sb("graw", [128, 4])
        k.tg = t.sb("tg", [128, 4])
        k.half = t.sb("half", [128, B])
        k.stats = t.sb("stats", [128, B, 6])
        k.mean, k.diff, k.var, k.rstd = (t.sb(n, [128, B]) for n in ("mean", "diff", "var", "rstd"))
        k.wo1, k.bo1 = t.sb("wo1", [128, INNER // 128, D]), t.sb("bo1", [128, D])
        k.wv1 = t.sb("wv1", [128, INNER])
        k.wqk = t.sb("wqk", [128, HEADS, D])
        k.causal = t.sb("causal", [128, S])
        k.hidden = t.sb("hidden", [128, B, S], U8)
        k.att1_in, k.wqk_ready = t.sem("att1_in"), t.sem("wqk_ready")
        k.wup = t.sb("wup", [128, E, F])
        k.wdn = t.sb("wdn", [128, E, FC, D])
        k.b1, k.b2 = t.sb("b1", [128, E, F]), t.sb("b2", [128, E, D])
        k.w_in = [t.sem(f"w_in{i}") for i in range(2)]
        k.bias_in = t.sem("bias_in")
        k.slots = [nc.dram_tensor(f"slots{i}", (NTILES[i], 128, ROW), F32, kind="Internal").ap() for i in range(2)]
        k.outs = [nc.dram_tensor(f"outs{i}", ((2 - i) * B + NTILES[i], S, D), F32, kind="Internal").ap() for i in range(2)]
        k.slots_set = t.sem("slots_set")
        start_phase(nc, k, w)
        for layer in range(2):
            attention_phase(nc, k, w, layer)
            experts_phase(nc, k, w, layer)


def kernel(x, ctx_1024, mask_BxS2_bf0, g_xattn, g_ffn, L0_xattn_Wq, L0_xattn_bq, L0_xattn_Wk, L0_xattn_bk,
           L0_xattn_Wv, L0_xattn_bv, L0_xattn_Wo, L0_xattn_bo, L0_ffn_shared_up, L0_ffn_shared_down,
           L0_ffn_routed_up, L0_ffn_routed_down, L0_ffn_router_w, L1_xattn_Wq, L1_xattn_Wk, L1_xattn_Wv,
           L1_xattn_Wo, L1_xattn_bo, L1_ffn_gate_w, L1_ffn_gate_b, L1_ffn_w1, L1_ffn_b1, L1_ffn_w2, L1_ffn_b2):
    import concourse.bacc as bacc
    from concourse.bass_utils import run_bass_kernel_spmd

    def a(v):
        return np.asarray(v)

    head = np.arange(128) // DK % G
    padding = [np.zeros((n, 128, ROW), np.int32) for n in NTILES]
    for layer in range(2):
        padding[layer][:, :, D] = (2 - layer) * B * S + np.arange(128 * NTILES[layer]).reshape(-1, 128)
    data = {
        "xr": a(x).transpose(1, 0, 2),
        "ctxT": a(ctx_1024).transpose(0, 2, 1),
        "mask": a(mask_BxS2_bf0),
        "g_xattn": a(g_xattn), "g_ffn": a(g_ffn),
        "ident": np.eye(128, dtype=np.float32),
        "headmask": (head[:, None] == np.arange(G)[None]).astype(np.float32),
        "causal": np.where(np.arange(S)[None] > np.arange(S)[:, None], np.float32(-FMAX), np.float32(0)),
        "iota": np.arange(E, dtype=np.float32),
        "wq0": a(L0_xattn_Wq).T, "wk0": a(L0_xattn_Wk).T, "wv0": a(L0_xattn_Wv).T,
        "bqkv0": np.stack([a(L0_xattn_bq), a(L0_xattn_bk), a(L0_xattn_bv)], 1),
        "wo0": a(L0_xattn_Wo).T[:, None], "bo0": a(L0_xattn_bo),
        "wqT1": a(L1_xattn_Wq).reshape(D, HEADS, DH).transpose(2, 1, 0),
        "wkT1": a(L1_xattn_Wk).reshape(D, HEADS, DH).transpose(2, 1, 0),
        "wv1": a(L1_xattn_Wv),
        "wo1": a(L1_xattn_Wo).reshape(INNER // 128, 128, D).transpose(1, 0, 2), "bo1": a(L1_xattn_bo),
        "router0": a(L0_ffn_router_w), "router1": a(L1_ffn_gate_w).T, "router_b1": a(L1_ffn_gate_b),
        "shared_up": a(L0_ffn_shared_up)[0],
        "shared_down": a(L0_ffn_shared_down)[0].reshape(FC, 128, D).transpose(1, 0, 2),
        "up0": a(L0_ffn_routed_up).transpose(1, 0, 2),
        "down0": a(L0_ffn_routed_down).reshape(E, FC, 128, D).transpose(2, 0, 1, 3),
        "up1": a(L1_ffn_w1).transpose(2, 0, 1),
        "down1": a(L1_ffn_w2).transpose(0, 2, 1).reshape(E, FC, 128, D).transpose(2, 0, 1, 3),
        "b1": a(L1_ffn_b1), "b2": a(L1_ffn_b2),
        "iota_tile": np.arange(max(NTILES), dtype=np.float32),
        "edges": 128 * np.arange(B, dtype=np.float32),
        "before": (np.arange(128)[:, None] < np.arange(128)[None]).astype(np.float32),
        "ones": np.ones((128, 128), np.float32),
        "ids": (np.arange(S)[:, None, None] + 128 * (np.arange(2)[None, :, None] * B + np.arange(B)[None, None])).astype(np.int32),
        "padding0": padding[0], "padding1": padding[1],
    }
    nc = bacc.Bacc("TRN2", target_bir_lowering=False, num_devices=1)
    arrays, w = {}, {}
    for name, v in data.items():
        v = np.ascontiguousarray(v)
        arrays[f"in_{name}"] = v
        w[name] = nc.dram_tensor(f"in_{name}", v.shape, mybir.dt.from_np(v.dtype), kind="ExternalInput").ap()
    w["out"] = nc.dram_tensor("out", (S, B, D), F32, kind="ExternalOutput").ap()
    flamingo(nc, w)
    r = run_bass_kernel_spmd(nc, [arrays], core_ids=[0])
    return np.ascontiguousarray(r.results[0]["out"].transpose(1, 0, 2))
```

```python
from contextlib import ExitStack

import numpy as np

import concourse.bass as bass
from concourse import mybir

F32 = mybir.dt.float32
BF16 = mybir.dt.bfloat16
U8 = mybir.dt.uint8
I32 = mybir.dt.int32
ALU = mybir.AluOpType
ACT = mybir.ActivationFunctionType
AX = mybir.AxisListType.X

B, S, D = 16, 128, 128
HEADS = 16
DK = D // HEADS
DH = 64
INNER = HEADS * DH
F = 512
FC = F // 128
E = 8
G = 4
U = HEADS // G
PAIRS = B // 2
EARLY = 3
GROUPS = 4
GB = B // GROUPS
GT = GB * S
R = 8
ROWS = (D + 2, 2 * D + 1)
NTILES = [(uses * B * S + E * 127) // 128 for uses in (2, 1)]
EPS = 1e-5
FMAX = float(np.finfo(np.float32).max)


class Tools:

    def __init__(self, nc, ctx, tag, used):
        self.nc, self.ctx, self.tag, self.used = nc, ctx, tag, used

    def sb(self, name, shape, dt=F32):
        return self.ctx.enter_context(self.nc.sbuf_tensor(f"{self.tag}_{name}", shape, dt))

    def ps(self, name, shape, dt=F32):
        return self.ctx.enter_context(self.nc.psum_tensor(f"{self.tag}_{name}", shape, dt))

    def sem(self, name):
        self.used.append(self.nc.alloc_semaphore(f"{self.tag}_{name}"))
        return self.used[-1]


def wide(ap, n):
    return ap.unsqueeze(2).to_broadcast([ap.shape[0], ap.shape[1], n])


def rows(ap, m):
    return ap.unsqueeze(1).to_broadcast([ap.shape[0], m, ap.shape[1]])


def start_phase(nc, k, w):
    with ExitStack() as ctx:
        t = Tools(nc, ctx, "start", k.used)
        loaded = t.sem("loaded")
        x_loaded = t.sem("x_loaded")
        tanh_done = t.sem("tanh_done")
        block = ctx.enter_context(nc.Block())

        @block.sync
        def _(sp):
            sp.dma_start(k.x[:, :, :], w["xr"]).then_inc(x_loaded, 16)
            sp.dma_start(k.graw[:, 0:2], w["g_xattn"].partition_broadcast(128)).then_inc(loaded, 16)
            sp.dma_start(k.graw[:, 2:4], w["g_ffn"].partition_broadcast(128)).then_inc(loaded, 16)
            sp.dma_start(k.ident[:, :], w["ident"]).then_inc(loaded, 16)
            for dst, src in [(k.wq0[:, :], w["wq0"]), (k.wk0[:, :], w["wk0"]), (k.wv0[:, :], w["wv0"]), (k.bqkv0[:, :], w["bqkv0"]),
                             (k.headmask[:, :], w["headmask"]), (k.wo0[:, :, :], w["wo0"]),
                             (k.bo0[:, :], w["bo0"].partition_broadcast(128))]:
                sp.dma_start(dst, src).then_inc(k.att0_in, 16)

        @block.scalar
        def _(act):
            act.wait_ge(loaded, 48)
            nc.scalar.activation(k.tg[:, :], k.graw[:, :], ACT.Tanh).then_inc(tanh_done, 1)
            act.wait_ge(tanh_done, 1)

        @block.vector
        def _(dve):
            nc.vector.memset(k.half[:, :], -0.5)
            dve.wait_ge(x_loaded, 16)
            with dve.Fori(0, GROUPS) as g:
                for s in range(GB):
                    nc.vector.bn_stats(k.stats[:, GB * g + s, :], k.x[:, GB * g + s, :])


def norm_stats(nc, dve, k, own, ready):
    m0, m1 = k.stats[:, :, 1], k.stats[:, :, 4]
    v0, v1 = k.stats[:, :, 2], k.stats[:, :, 5]
    nc.vector.tensor_tensor(k.mean[:, :], m0, m1, ALU.add).then_inc(own, 1)
    nc.vector.tensor_tensor(k.diff[:, :], m0, m1, ALU.subtract).then_inc(own, 1)
    nc.vector.tensor_tensor(k.var[:, :], v0, v1, ALU.add).then_inc(own, 1)
    dve.wait_ge(own, 3)
    nc.vector.tensor_scalar(k.mean[:, :], k.mean[:, :], 0.5, None, ALU.mult).then_inc(own, 1)
    nc.vector.tensor_tensor(k.diff[:, :], k.diff[:, :], k.diff[:, :], ALU.mult).then_inc(own, 1)
    nc.vector.tensor_scalar(k.var[:, :], k.var[:, :], 1.0 / D, EPS, ALU.mult, ALU.add).then_inc(own, 1)
    dve.wait_ge(own, 6)
    nc.vector.scalar_tensor_tensor(out=k.var[:, :], in0=k.diff[:, :], scalar=0.25, in1=k.var[:, :],
                                   op0=ALU.mult, op1=ALU.add).then_inc(ready, 1)


def invert_std(nc, k, ready):
    for g in range(GROUPS):
        own = slice(GB * g, GB * g + GB)
        nc.gpsimd.tensor_tensor(k.rstd[:, own], k.var[:, own], k.half[:, own], ALU.pow).then_inc(ready, 1)


def attention_phase(nc, k, w, layer):
    first = layer == 0
    scale = float(np.float32(1.0) / np.sqrt(np.float32(DK if first else DH)))
    earlier = list(k.used)
    OC = 1 if first else HEADS * DH // 128
    gate = layer

    with ExitStack() as ctx:
        t = Tools(nc, ctx, f"att{layer}", k.used)
        if first:
            wo, bo, wq, wk, wv, bqkv, headmask = k.wo0, k.bo0, k.wq0, k.wk0, k.wv0, k.bqkv0, k.headmask
            bq = t.sb("bq", [128, 1])
            bv = t.sb("bv", [128, S])
        else:
            wo, bo, wv, wqk, causal, hidden = k.wo1, k.bo1, k.wv1, k.wqk, k.causal, k.hidden
        ctxT = [t.sb(f"ctxT{i}", [128, S]) for i in range(2)]
        xn = [t.sb(f"xn{i}", [128, D]) for i in range(2)]
        xnT = [t.sb(f"xnT{i}", [128, S]) for i in range(2)]
        if first:
            qT = [t.sb(f"qT{i}", [128, U, S]) for i in range(2)]
            kraw = [t.sb(f"kraw{i}", [128, S]) for i in range(2)]
            kT = [t.sb(f"kT{i}", [128, G, S]) for i in range(2)]
            v = [t.sb(f"v{i}", [128, G, U, G, DK]) for i in range(2)]
        else:
            qT = [t.sb(f"qT{i}", [128, HEADS, S]) for i in range(2)]
            v = [t.sb(f"v{i}", [128, INNER]) for i in range(2)]
            bias = [t.sb(f"bias{i}", [128, S]) for i in range(2)]
        oT = [t.sb(f"oT{i}", [128, OC, S]) for i in range(2)]
        probs = [t.sb(f"probs{i}", [128, G, S]) for i in range(2 * U)]
        low = [t.sb(f"low{i}", [128, G]) for i in range(2 * U)]
        total = [t.sb(f"total{i}", [128, G]) for i in range(2 * U)]
        inv = [t.sb(f"inv{i}", [128, G]) for i in range(2 * U)]
        pT = [t.sb(f"pT{i}", [128, G, S]) for i in range(2)]
        sc_ps = [t.ps(f"sc_ps{i}", [128, G, S]) for i in range(4 if first else 2)]
        t_ps = [t.ps(f"t_ps{i}", [128, G, S]) for i in range(1 if first else 2)]
        SB, TB = len(sc_ps), len(t_ps)
        q_ps = t.ps("q_ps", [128, G, S])
        kv_ps = q_ps if first else t.ps("kv_ps", [128, G, S])
        o_ps = t.ps("o_ps", [128, G, S])
        y_ps = t.ps("y_ps", [128, G, S])

        weights = k.att0_in if first else k.att1_in
        ctx_in = [t.sem(f"ctx_in{i}") for i in range(2)]
        norm_own = t.sem("norm_own")
        var_ready = t.sem("var_ready")
        rstd_ready = t.sem("rstd_ready")
        base_own = t.sem("base_own")
        base_ready = t.sem("base_ready")
        xn_ready, xnT_made, xnT_ready = t.sem("xn_ready"), t.sem("xnT_made"), t.sem("xnT_ready")
        q_made, q_ready = t.sem("q_made"), t.sem("q_ready")
        v_made, v_ready = t.sem("v_made"), t.sem("v_ready")
        sc_made, low_ready = t.sem("sc_made"), t.sem("low_ready")
        exp_done, pT_made, pT_ready = t.sem("exp_done"), t.sem("pT_made"), t.sem("pT_ready")
        inv_ready, probs_ready = t.sem("inv_ready"), t.sem("probs_ready")
        o_made, o_ready = t.sem("o_made"), t.sem("o_ready")
        y_made, x_ready, stats_ready = t.sem("y_made"), t.sem("x_ready"), t.sem("stats_ready")
        if first:
            zeros_set, bq_ready = t.sem("zeros_set"), t.sem("bq_ready")
            k_made, kraw_ready, k_ready = t.sem("k_made"), t.sem("kraw_ready"), t.sem("k_ready")
            bv_ready, bv_made, bo_full = t.sem("bv_ready"), t.sem("bv_made"), t.sem("bo_full")
        else:
            bias_ready, masked = t.sem("bias_ready"), t.sem("masked")
        if not first:
            nc.clear_and_free_semaphores(earlier)
        block = ctx.enter_context(nc.Block())

        spread = [q_ps, kv_ps, o_ps, y_ps]
        QE = 1 if first else U
        VE = 1 if first else 2

        def batch(i, par, ahead=0):
            return 2 * i + par + ahead, (par + ahead) % 2

        def turns(i, par, ahead):
            return i + (par + ahead) // 2

        def masked_v(q):
            dst = v[q][:, :, :, :, :].rearrange("p h u c d -> p (h u c d)")
            out = bass.AP(tensor=dst.tensor, offset=dst.offset, ap=[dst.ap[0], [D + DK, G], [G * DK, U], [1, DK]])
            return out, y_ps[:, 0, :].rearrange("p (u h d) -> p h u d", u=U, h=G)

        @block.sync
        def _(sp):
            for par in range(2):
                sp.dma_start(ctxT[par][:, :], w["ctxT"][par]).then_inc(ctx_in[par], 16)
            assert E == PAIRS
            pads = NTILES[layer] // E

            def experts_share(e):
                sp.dma_start(k.wup[:, e, :], w[f"up{layer}"][:, e]).then_inc(k.w_in[layer], 16)
                sp.dma_start(k.wdn[:, e, :, :], w[f"down{layer}"][:, e]).then_inc(k.w_in[layer], 16)
                tiles = slice(pads * e, pads * e + pads) if isinstance(e, int) else bass.ds(pads * e, pads)
                sp.dma_start(k.slots[layer].bitcast(I32)[tiles], w[f"padding{layer}"][tiles]).then_inc(k.slots_set, 16)

            with sp.Fori(1, PAIRS) as i:
                for par in range(2):
                    b, _p = batch(i, par)
                    if first:
                        sp.wait_ge(v_made, b - 1)
                    else:
                        sp.wait_ge(sc_made, U * (b - 1))
                    sp.dma_start(ctxT[par][:, :], w["ctxT"][b]).then_inc(ctx_in[par], 16)
                experts_share(i)
            experts_share(0)
            rest = slice(pads * E, NTILES[layer])
            sp.dma_start(k.slots[layer].bitcast(I32)[rest], w[f"padding{layer}"][rest]).then_inc(k.slots_set, 16)
            if not first:
                sp.dma_start(k.b1[:, :, :], w["b1"]).then_inc(k.bias_in, 16)
                sp.dma_start(k.b2[:, :, :], w["b2"].partition_broadcast(128)).then_inc(k.bias_in, 16)

        NW = 7 if first else 5

        @block.tensor
        def _(pe):
            def x_transpose(i, par, ahead):
                b, q = batch(i, par, ahead)
                pe.wait_ge(xn_ready, b + 1)
                if first:
                    pe.wait_ge(kraw_ready, b + 1)
                elif not (isinstance(b, int) and b == 0):
                    pe.wait_ge(q_ready, QE * b)
                nc.tensor.transpose(q_ps[:, 0, :], xn[q][:, :], k.ident[:, :]).then_inc(xnT_made, 1)

            def project_q(i, par, ahead, g):
                b, q = batch(i, par, ahead)
                pe.wait_ge(xnT_ready, b + 1)
                if first:
                    nc.tensor.matmul(q_ps[:, 0, :], wq[:, :], xnT[q][:, :], start=True, stop=True).then_inc(q_made, 1)
                    return
                if g or not (isinstance(b, int) and b == 0):
                    pe.wait_ge(q_ready, QE * b + g)
                for hh in range(G):
                    mm = nc.tensor.matmul(q_ps[:, hh, :], wqk[:, G * g + hh, :], xnT[q][:, :], start=True, stop=True)
                mm.then_inc(q_made, 1)

            def project_k(i, par, ahead):
                b, q = batch(i, par, ahead)
                pe.wait_ge(ctx_in[q], 16 * (turns(i, par, ahead) + 1))
                if not (isinstance(b, int) and b == 0):
                    pe.wait_ge(q_ready, b)
                nc.tensor.matmul(kv_ps[:, 0, :], wk[:, :], ctxT[q][:, :], start=True, stop=True).then_inc(k_made, 1)

            def project_v(i, par, ahead, half):
                b, q = batch(i, par, ahead)
                if first:
                    if isinstance(b, int) and b < 2:
                        pe.wait_ge(v_ready, 1) if b else pe.wait_ge(bo_full, 1)
                    else:
                        pe.wait_ge(x_ready, b - 1)
                    nc.tensor.matmul(y_ps[:, 0, :], ctxT[q][:, :], wv[:, :], start=True, stop=True).then_inc(v_made, 1)
                    return
                pe.wait_ge(ctx_in[q], 16 * (turns(i, par, ahead) + 1))
                if half or not (isinstance(b, int) and b == EARLY):
                    pe.wait_ge(v_ready, VE * (b - EARLY) + half)
                nc.tensor.matmul(kv_ps[:, :, :].rearrange("p a b -> p (a b)"), ctxT[q][:, :],
                                 wv[:, half * 512:half * 512 + 512], start=True, stop=True).then_inc(v_made, 1)

            def scores(i, par, ahead, g):
                b, q = batch(i, par, ahead)
                if first:
                    pe.wait_ge(q_ready, b + 1)
                    pe.wait_ge(k_ready, b + 1)
                else:
                    pe.wait_ge(q_ready, QE * b + g + 1)
                    pe.wait_ge(ctx_in[q], 16 * (turns(i, par, ahead) + 1))
                if g >= SB or not (isinstance(b, int) and b == 0):
                    pe.wait_ge(exp_done if first else masked, U * b + g - SB + 1)
                if first:
                    nc.tensor.matmul(sc_ps[g % SB][:, :, :].rearrange("p a b -> p (a b)"), qT[q][:, g, :],
                                     kT[q][:, :, :].rearrange("p a b -> p (a b)"), start=True, stop=True).then_inc(sc_made, 1)
                    return
                for hh in range(G):
                    mm = nc.tensor.matmul(sc_ps[g % SB][:, hh, :], qT[q][:, G * g + hh, :], ctxT[q][:, :],
                                          start=True, stop=True)
                mm.then_inc(sc_made, 1)

            def turn_probs(i, par, g):
                b, q = batch(i, par)
                pe.wait_ge(probs_ready, U * b + g + 1)
                if g >= TB or not (isinstance(b, int) and b == 0):
                    pe.wait_ge(pT_ready, U * b + g - TB + 1)
                for hh in range(G):
                    mm = nc.tensor.transpose(t_ps[g % TB][:, hh, :], probs[U * q + g][:, hh, :], k.ident[:, :])
                mm.then_inc(pT_made, 1)

            def values(i, par, ahead, g):
                b, q = batch(i, par, ahead)
                pe.wait_ge(pT_ready, U * b + g + 1)
                early = not first and isinstance(b, int) and b < EARLY
                if first:
                    pe.wait_ge(v_ready, b + 1)
                elif not early:
                    pe.wait_ge(v_ready, VE * (b - EARLY) + VE)
                if first:
                    if g == 0 and not (isinstance(b, int) and b == 0):
                        pe.wait_ge(o_ready, b)
                    for hh in range(G):
                        mm = nc.tensor.matmul(o_ps[32 * g:32 * g + 32, 0, :],
                                              v[q][:, hh, g, :, :].rearrange("p a b -> p (a b)"),
                                              pT[g % 2][:, hh, :], start=(hh == 0), stop=(hh == G - 1))
                else:
                    if g or not (isinstance(b, int) and b == 0):
                        pe.wait_ge(o_ready, U * b + g)
                    for hh in range(G):
                        h = G * g + hh
                        r = 64 * (hh % 2)
                        values_h = k.v1[:, b, DH * h:DH * h + DH] if early else v[q][:, DH * h:DH * h + DH]
                        mm = nc.tensor.matmul(o_ps[r:r + 64, hh // 2, :], values_h,
                                              pT[g % 2][:, hh, :], start=True, stop=True)
                mm.then_inc(o_made, 1)

            def project_out(i, par, ahead):
                b, q = batch(i, par, ahead)
                pe.wait_ge(o_ready, (b + 1) if first else U * (b + 1))
                if first:
                    pe.wait_ge(v_ready, min(b + 2, B) if isinstance(b, int) else b + 2)
                elif not (isinstance(b, int) and b == 0):
                    pe.wait_ge(x_ready, b)
                for c in range(OC):
                    mm = nc.tensor.matmul(y_ps[:, 0, :], oT[q][:, c, :], wo[:, c, :], start=(c == 0), stop=(c == OC - 1))
                mm.then_inc(y_made, 1)

            def pair(i, is_first, is_last):
                for par in range(2):
                    has_before = not (is_first and par == 0)
                    has_next = not (is_last and par == 1)
                    makes_v = has_next and (first or not isinstance(i, int) or 2 * i + par + 1 >= EARLY)
                    for g in range(U):
                        turn_probs(i, par, g)
                        if g:
                            values(i, par, 0, g - 1)
                        elif has_before:
                            values(i, par, -1, U - 1)
                        if g == 1 and has_before:
                            project_out(i, par, -1)
                        if g == (3 if first else 1) and makes_v:
                            project_v(i, par, 1, 0)
                        if g == 2 and makes_v and not first:
                            project_v(i, par, 1, 1)
                        if not is_last:
                            if first:
                                if g == 1:
                                    x_transpose(i, par, 2)
                                if g == 2:
                                    project_q(i, par, 2, 0)
                            else:
                                if g:
                                    project_q(i, par, 2, g - 1)
                        if g < U - 1:
                            if has_next:
                                scores(i, par, 1, g + 1)
                        elif not is_last:
                            scores(i, par, 2, 0)
                            if not first:
                                project_q(i, par, 2, 3)
                        if g == 0 and not is_last:
                            project_k(i, par, 2) if first else x_transpose(i, par, 2)

            pe.wait_ge(weights, 16 * NW)
            if first:
                pe.wait_ge(bv_ready, 1)
                nc.tensor.matmul(y_ps[:, 0, :], bv[:, :], wo[:, 0, :], start=True, stop=True).then_inc(bv_made, 1)
                pe.wait_ge(zeros_set, 3)
                for par in range(2):
                    project_k(0, par, 0)
                    x_transpose(0, par, 0)
                    project_q(0, par, 0, 0)
                    if par == 0:
                        project_v(0, par, 0, 0)
                for g in range(U):
                    scores(0, 0, 0, g)
            else:
                pe.wait_ge(k.wqk_ready, U)
                for par in range(2):
                    pe.wait_ge(xn_ready, par + 1)
                    nc.tensor.transpose(t_ps[par][:, 0, :], xn[par][:, :], k.ident[:, :]).then_inc(xnT_made, 1)

                def first_q(b, g):
                    pe.wait_ge(xnT_ready, b + 1)
                    if b:
                        pe.wait_ge(q_ready, g + 1)
                    for hh in range(G):
                        mm = nc.tensor.matmul(spread[g][:, hh, :], wqk[:, G * g + hh, :], xnT[b][:, :], start=True, stop=True)
                    mm.then_inc(q_made, 1)

                for g in range(U):
                    first_q(0, g)
                for g in range(2):
                    scores(0, 0, 0, g)
                for g in range(U):
                    first_q(1, g)
                    if g < 2:
                        scores(0, 0, 0, g + 2)
            scores(0, 1, 0, 0)
            pair(0, True, False)
            if not first:
                pair(1, False, False)
            with pe.Fori(1 if first else 2, PAIRS - 1) as i:
                pair(i, False, False)
            pair(PAIRS - 1, False, True)
            values(PAIRS, 0, -1, U - 1)
            project_out(PAIRS, 0, -1)

        @block.scalar
        def _(act):
            def take_xnT(i, par, ahead, src=q_ps[:, 0, :]):
                b, q = batch(i, par, ahead)
                act.wait_ge(xnT_made, b + 1)
                if not (isinstance(i, int) and i == 0 and ahead == 0):
                    act.wait_ge(q_made, QE * (b - 1))
                nc.scalar.activation(xnT[q][:, :], src, ACT.Copy).then_inc(xnT_ready, 1)

            def take_k(i, par, ahead):
                b, q = batch(i, par, ahead)
                act.wait_ge(k_made, b + 1)
                if not (isinstance(i, int) and i == 0 and ahead == 0):
                    act.wait_ge(k_ready, b - 1)
                nc.scalar.activation(kraw[q][:, :], kv_ps[:, 0, :], ACT.Identity, bias=bqkv[:, 1:2]).then_inc(kraw_ready, 1)

            def take_v(i, par, ahead, half):
                b, q = batch(i, par, ahead)
                act.wait_ge(v_made, (b if first else VE * (b - EARLY) + half) + 1)
                if not (isinstance(i, int) and i == 0 and par + ahead < 2):
                    act.wait_ge(o_made, U * (b - 1))
                if first:
                    out, src = masked_v(q)
                    nc.scalar.activation(out, src, ACT.Copy).then_inc(v_ready, 1)
                else:
                    nc.scalar.activation(v[q][:, half * 512:half * 512 + 512],
                                         kv_ps[:, :, :].rearrange("p a b -> p (a b)"), ACT.Copy).then_inc(v_ready, 1)

            def take_q(i, par, ahead, g, bank=q_ps):
                b, q = batch(i, par, ahead)
                act.wait_ge(q_made, QE * b + g + 1)
                if first:
                    if not (isinstance(i, int) and i == 0 and ahead == 0):
                        act.wait_ge(sc_made, U * (b - 1))
                    for u in range(U):
                        r = 32 * u
                        last = nc.scalar.activation(qT[q][r:r + 32, u, :], q_ps[r:r + 32, 0, :], ACT.Identity,
                                                    bias=bq[r:r + 32, :], scale=-scale)
                    last.then_inc(q_ready, 1)
                    return
                if not (isinstance(i, int) and i == 0 and ahead == 0):
                    act.wait_ge(sc_made, U * (b - 2) + g + 1)
                nc.scalar.activation(qT[q][:, G * g:G * g + G, :], bank[:, :, :], ACT.Copy).then_inc(q_ready, 1)

            def exponentials(i, par, ahead, g):
                b, q = batch(i, par, ahead)
                n = U * b + g
                act.wait_ge(low_ready, n + 1)
                p = probs[U * q + g]
                if first and not (isinstance(i, int) and i == 0 and par + ahead < 2):
                    act.wait_ge(pT_made, n - 2 * U + 1)
                for hh in range(G):
                    src = sc_ps[g % SB] if first else p
                    last = nc.scalar.activation(p[:, hh, :], src[:, hh, :], ACT.Exp, bias=low[U * q + g][:, hh:hh + 1],
                                                scale=-1.0, accum_out=total[U * q + g][:, hh:hh + 1])
                last.then_inc(exp_done, 1)

            def take_pT(i, par, g):
                b, q = batch(i, par)
                act.wait_ge(pT_made, U * b + g + 1)
                if g >= 2 or not (isinstance(b, int) and b == 0):
                    act.wait_ge(o_made, U * b + g - 1)
                nc.scalar.activation(pT[g % 2][:, :, :], t_ps[g % TB][:, :, :], ACT.Copy).then_inc(pT_ready, 1)

            def pair(i, is_first, is_last):
                for par in range(2):
                    has_next = not (is_last and par == 1)
                    makes_v = has_next and (first or not isinstance(i, int) or 2 * i + par + 1 >= EARLY)
                    for g in range(U):
                        if not first:
                            take_pT(i, par, g)
                        if g == 1 and makes_v and not first:
                            take_v(i, par, 1, 0)
                        if g == 2 and makes_v and not first:
                            take_v(i, par, 1, 1)
                        if not is_last:
                            if first:
                                if g == 1:
                                    take_xnT(i, par, 2)
                                if g == 2:
                                    take_q(i, par, 2, 0)
                            else:
                                if g:
                                    take_q(i, par, 2, g - 1)
                        if has_next:
                            exponentials(i, par, 1, g)
                        if g == 0 and not is_last:
                            take_k(i, par, 2) if first else take_xnT(i, par, 2)
                        if g == 3 and not is_last and not first:
                            take_q(i, par, 2, 3)

            if first:
                act.wait_ge(weights, 16 * NW)
                act.wait_ge(zeros_set, 3)
                act.wait_ge(bq_ready, 1)
                for par in range(2):
                    take_k(0, par, 0)
                    take_xnT(0, par, 0)
                    take_q(0, par, 0, 0)
                    if par == 0:
                        take_v(0, par, 0, 0)
                for g in range(U):
                    exponentials(0, 0, 0, g)
            else:
                for par in range(2):
                    take_xnT(0, par, 0, t_ps[par][:, 0, :])
                for g in range(U):
                    take_q(0, 0, 0, g, spread[g])
                for g in range(U):
                    take_q(0, 1, 0, g, spread[g])
                    exponentials(0, 0, 0, g)
            pair(0, True, False)
            if not first:
                pair(1, False, False)
            with act.Fori(1 if first else 2, PAIRS - 1) as i:
                pair(i, False, False)
            pair(PAIRS - 1, False, True)

        @block.gpsimd
        def _(pool):
            if first:
                for q in range(2):
                    nc.gpsimd.memset(v[q][:, :, :, :, :], 0.0).then_inc(zeros_set, 1)
            pool.wait_ge(var_ready, 1)
            invert_std(nc, k, rstd_ready)
            pool.wait_ge(weights, 16 * NW)
            if first:
                pool.wait_ge(bo_full, 1)
            nc.gpsimd.tensor_scalar(bo[:, :], bo[:, :], k.tg[:, gate:gate + 1], None, ALU.mult).then_inc(base_own, 1)
            pool.wait_ge(base_own, 1)

            def add_base(g):
                own = slice(GB * g, GB * g + GB)
                nc.gpsimd.tensor_tensor(k.base[:, own, :], k.x[:, own, :], rows(bo[:, :], GB), ALU.add).then_inc(base_ready, 1)

            def mask_k(i, par, ahead):
                b, q = batch(i, par, ahead)
                pool.wait_ge(kraw_ready, b + 1)
                if not (isinstance(i, int) and i == 0 and ahead == 0):
                    pool.wait_ge(sc_made, U * (b - 1))
                nc.gpsimd.tensor_tensor(kT[q][:, :, :], rows(kraw[q][:, :], G), wide(headmask[:, :], S),
                                        ALU.mult).then_inc(k_ready, 1)

            def normalize(i, par, ahead, g):
                b, q = batch(i, par, ahead)
                pool.wait_ge(inv_ready, U * b + g + 1)
                p = probs[U * q + g][:, :, :]
                nc.gpsimd.tensor_tensor(p, p, wide(inv[U * q + g][:, :], S), ALU.mult).then_inc(probs_ready, 1)

            def pair(i, is_last):
                for par in range(2):
                    has_next = not (is_last and par == 1)
                    for g in range(U):
                        if g == 0:
                            normalize(i, par, 0, U - 1)
                        elif has_next:
                            normalize(i, par, 1, g - 1)
                        if g == 1 and first and not is_last:
                            mask_k(i, par, 2)

            if first:
                mask_k(0, 0, 0)
                mask_k(0, 1, 0)
            for g in range(GROUPS):
                add_base(g)
                if g < U - 1:
                    normalize(0, 0, 0, g)
            pair(0, False)
            with pool.Fori(1, PAIRS - 1) as i:
                pair(i, False)
            pair(PAIRS - 1, True)

        @block.vector
        def _(dve):
            def norm(i, par, ahead):
                b, q = batch(i, par, ahead)
                if not (isinstance(i, int) and i == 0 and ahead == 0):
                    dve.wait_ge(xnT_made, b - 1)
                if isinstance(b, int):
                    mean, rstd, x = k.mean[:, b:b + 1], k.rstd[:, b:b + 1], k.x[:, b, :]
                else:
                    mean, rstd, x = k.mean[:, bass.ds(b, 1)], k.rstd[:, bass.ds(b, 1)], k.x[:, b, :]
                nc.vector.tensor_scalar(xn[q][:, :], x, mean, rstd, ALU.subtract, ALU.mult).then_inc(xn_ready, 1)

            def make_bias(i, par, ahead):
                b, q = batch(i, par, ahead)
                if not (isinstance(i, int) and i == 0 and ahead == 0):
                    dve.wait_ge(masked, U * (b - 1))
                nc.vector.scalar_tensor_tensor(out=bias[q][:, :], in0=hidden[:, b, :], scalar=FMAX,
                                               in1=causal[:, :], op0=ALU.mult, op1=ALU.max).then_inc(bias_ready, 1)

            def find_low(i, par, ahead, g):
                b, q = batch(i, par, ahead)
                n = U * b + g
                p = probs[U * q + g][:, :, :]
                dve.wait_ge(sc_made, n + 1)
                if not (isinstance(i, int) and i == 0 and par + ahead < 2):
                    dve.wait_ge(pT_made, n - 2 * U + 1)
                if first:
                    nc.vector.tensor_reduce(low[U * q + g][:, :], sc_ps[g % SB][:, :, :], AX, ALU.min).then_inc(low_ready, 1)
                else:
                    dve.wait_ge(bias_ready, b + 1)
                    nc.vector.scalar_tensor_tensor(out=p, in0=sc_ps[g % SB][:, :, :], scalar=-scale, in1=rows(bias[q][:, :], G),
                                                   op0=ALU.mult, op1=ALU.add).then_inc(masked, 1)
                    dve.wait_ge(masked, n + 1)
                    nc.vector.tensor_reduce(low[U * q + g][:, :], p, AX, ALU.min).then_inc(low_ready, 1)

            def take_v(i, par, ahead):
                b, q = batch(i, par, ahead)
                dve.wait_ge(v_made, b + 1)
                if not (isinstance(i, int) and i == 0 and par + ahead < 2):
                    dve.wait_ge(o_made, U * (b - 1))
                out, src = masked_v(q)
                nc.vector.tensor_copy(out, src).then_inc(v_ready, 1)

            def take_pT(i, par, g):
                b, q = batch(i, par)
                dve.wait_ge(pT_made, U * b + g + 1)
                if g >= 2 or not (isinstance(b, int) and b == 0):
                    dve.wait_ge(o_made, U * b + g - 1)
                nc.vector.tensor_copy(pT[g % 2][:, :, :], t_ps[g % TB][:, :, :]).then_inc(pT_ready, 1)

            def invert(i, par, ahead, g):
                b, q = batch(i, par, ahead)
                dve.wait_ge(exp_done, U * b + g + 1)
                nc.vector.reciprocal(inv[U * q + g][:, :], total[U * q + g][:, :]).then_inc(inv_ready, 1)

            def take_o(i, par, ahead, g):
                b, q = batch(i, par, ahead)
                dve.wait_ge(o_made, U * b + g + 1)
                if not (isinstance(i, int) and i == 0 and par + ahead < 2):
                    dve.wait_ge(y_made, b - 1)
                if first:
                    nc.vector.tensor_copy(oT[q][:, 0, :], o_ps[:, 0, :]).then_inc(o_ready, 1)
                else:
                    nc.vector.tensor_copy(oT[q][:, 2 * g:2 * g + 2, :], o_ps[:, 0:2, :]).then_inc(o_ready, 1)

            def finish(i, par, ahead):
                b, q = batch(i, par, ahead)
                if isinstance(b, int) and b == 0:
                    dve.wait_ge(base_ready, GROUPS)
                dve.wait_ge(y_made, b + 1)
                nc.vector.scalar_tensor_tensor(out=k.x[:, b, :], in0=y_ps[:, 0, :], scalar=k.tg[:, gate:gate + 1],
                                               in1=k.base[:, b, :], op0=ALU.mult, op1=ALU.add).then_inc(x_ready, 1)

            def row_stats(i, par, ahead):
                b, q = batch(i, par, ahead)
                dve.wait_ge(x_ready, b + 1)
                nc.vector.bn_stats(k.stats[:, b, :], k.x[:, b, :]).then_inc(stats_ready, 1)

            def pair(i, is_first, is_last):
                for par in range(2):
                    has_before = not (is_first and par == 0)
                    has_next = not (is_last and par == 1)
                    for g in range(U):
                        if has_next:
                            find_low(i, par, 1, g)
                        if first:
                            take_pT(i, par, g)
                        if first and g == 3 and has_next:
                            take_v(i, par, 1)
                        if g == 0 and not is_last:
                            norm(i, par, 2)
                        if g == 0:
                            invert(i, par, 0, U - 1)
                        elif has_next:
                            invert(i, par, 1, g - 1)
                        if first:
                            if g == 0 and has_before:
                                take_o(i, par, -1, U - 1)
                        else:
                            if g:
                                take_o(i, par, 0, g - 1)
                            elif has_before:
                                take_o(i, par, -1, U - 1)
                            if g == 3 and not is_last:
                                make_bias(i, par, 2)
                        if g == 1 and has_before:
                            finish(i, par, -1)
                        if g == 2 and has_before:
                            row_stats(i, par, -1)

            norm_stats(nc, dve, k, norm_own, var_ready)
            if first:
                for q in range(2):
                    last = nc.vector.memset(qT[q][:, :, :], 0.0)
                last.then_inc(zeros_set, 1)
                dve.wait_ge(weights, 16 * NW)
                nc.vector.tensor_scalar(bv[:, :], k.ident[:, :], 0.0, bqkv[:, 2:3], ALU.mult, ALU.add).then_inc(bv_ready, 1)
                nc.vector.tensor_scalar(bq[:, :], bqkv[:, 0:1], -scale, None, ALU.mult).then_inc(bq_ready, 1)
                dve.wait_ge(bv_made, 1)
                nc.vector.tensor_tensor(bo[:, :], y_ps[:, 0, :], bo[:, :], ALU.add).then_inc(bo_full, 1)
            dve.wait_ge(weights, 16 * NW)
            if first:
                dve.wait_ge(zeros_set, 3)
            dve.wait_ge(rstd_ready, 1)
            for par in range(2):
                norm(0, par, 0)
                if not first:
                    make_bias(0, par, 0)
            dve.wait_ge(rstd_ready, GROUPS)
            for g in range(U):
                find_low(0, 0, 0, g)
                if g:
                    invert(0, 0, 0, g - 1)
            pair(0, True, False)
            with dve.Fori(1, PAIRS - 1) as i:
                pair(i, False, False)
            pair(PAIRS - 1, False, True)
            take_o(PAIRS, 0, -1, U - 1)
            finish(PAIRS, 0, -1)
            row_stats(PAIRS, 0, -1)
            dve.wait_ge(stats_ready, B)


def experts_phase(nc, k, w, layer):
    first = layer == 0
    gate = 2 + layer
    PICKS = 2 if first else 1
    ROW = ROWS[layer]
    NT = NTILES[layer]
    tg = k.tg[:, gate:gate + 1]
    slots_dram, out_dram = k.slots[layer], k.outs[layer]

    with ExitStack() as ctx:
        t = Tools(nc, ctx, f"ffn{layer}", k.used)
        router = t.sb("router", [128, E])
        iota = t.sb("iota", [128, E])
        iota_tile = t.sb("iota_tile", [128, NT])
        edges = t.sb("edges", [128, B])
        earlier = t.sb("earlier", [128, E, E])
        before = t.sb("before", [128, 128])
        before16, ones16 = t.sb("before16", [128, 128], BF16), t.sb("ones16", [128, 128], BF16)
        ids = t.sb("ids", [128, PICKS, B], I32)
        rowbuf = [t.sb(f"rowbuf{p}", [128, B, ROW]) for p in range(PICKS)]
        xT = t.sb("xT", [128, B, S])
        if first:
            sup, sdown = t.sb("sup", [128, F]), t.sb("sdown", [128, FC, D])
            shT = [t.sb(f"shT{i}", [128, FC, GT]) for i in range(2)]
            wqT, wkT = t.sb("wqT", [DH, HEADS, D]), t.sb("wkT", [DH, HEADS, D])
            ctxT = t.sb("ctxT", [128, EARLY, S])
        else:
            router_b = t.sb("router_b", [128, E])
            weight = t.sb("weight", [128, B])
        pr, o1, o2, tmp = (t.sb(n, [128, B, E]) for n in ("pr", "o1", "o2", "tmp"))
        top, total, m1, i1, m2, i2 = (t.sb(n, [128, B]) for n in ("top", "total", "m1", "i1", "m2", "i2"))
        uses = t.sb("uses", [128, B, E], BF16)
        tiles, uses_of, starts, ends = (t.sb(n, [128, E]) for n in ("tiles", "uses_of", "starts", "ends"))
        tiles_before = t.sb("tiles_before", [128, E, E])
        slot = [t.sb(f"slot{p}", [128, B], I32) for p in range(PICKS)]
        at = t.sb("at", [128, NT, E])
        tile_e = t.sb("tile_e", [128, NT])
        tile_i = t.sb("tile_i", [128, NT], I32)
        xin = [t.sb(f"xin{i}", [128, ROW]) for i in range(R)]
        xt = [t.sb(f"xt{i}", [128, 128]) for i in range(2)]
        upw = [t.sb(f"upw{i}", [128, F]) for i in range(4)]
        upb = [t.sb(f"upb{i}", [128, FC]) for i in range(4)]
        hT = [t.sb(f"hT{i}", [128, FC, 128]) for i in range(2)]
        y = [t.sb(f"y{i}", [128, D]) for i in range(R)]
        if first:
            z = t.sb("z", [128, PICKS, B, D])
        else:
            yb = [t.sb(f"yb{i}", [128, D]) for i in range(2)]

        bank = [t.ps(f"bank{i}", [128, 512]) for i in range(8)]
        tr_ps = bank[6][:, 0:128]
        lg_ps = bank[7][:, 0:B * E].rearrange("p (b e) -> p b e", e=E)
        first_tr_ps = [bank[6], bank[4]]
        rank_ps, count_ps = bank[5][:, 0:B * E], bank[6][:, 0:B * E]
        sup_ps, sdn_ps = bank[0:4], bank[4:6]
        up_ps, y_ps = bank[0:4], bank[4:6]

        consts, shared_in = t.sem("consts"), t.sem("shared_in")
        norm_own, var_ready, rstd_ready = t.sem("norm_own"), t.sem("var_ready"), t.sem("rstd_ready")
        xnT_made, xT_ready = t.sem("xnT_made"), t.sem("xT_ready")
        counts16_ready, counted, copied, tails_ready = (t.sem(n) for n in ("counts16_ready", "counted", "copied", "tails_ready"))
        rows_ready, lg_made, shifted, e_ready, own = (t.sem(n) for n in ("rows_ready", "lg_made", "shifted", "e_ready", "own"))
        uses_ready, rank_made, slots_ready, ids_set, scattered, plan_ready = (
            t.sem(n) for n in ("uses_ready", "rank_made", "slots_ready", "ids_set", "scattered", "plan_ready"))
        if not first:
            weight_ready, weighted = t.sem("weight_ready"), t.sem("weighted")
        if first:
            qk_in, wqk_made, ctx_in, v1_made = t.sem("qk_in"), t.sem("wqk_made"), t.sem("ctx_in"), t.sem("v1_made")
            sup_made, sh_ready, sdn_made, sdn_taken = (t.sem(n) for n in ("sup_made", "sh_ready", "sdn_made", "sdn_taken"))
        tile_in = [t.sem(f"tile_in{i}") for i in range(R)]
        puts_begun = t.sem("puts_begun")
        tile_out = [t.sem(f"tile_out{i}") for i in range(R)]
        xt_made, xt_ready, upb_ready, upw_ready, up_made, hT_ready, y_made, y_ready = (
            t.sem(n) for n in ("xt_made", "xt_ready", "upb_ready", "upw_ready", "up_made", "hT_ready", "y_made", "y_ready"))
        if first:
            z_in = [t.sem(f"z_in{g}") for g in range(GROUPS)]
            z_summed, z_added, stats_ready = t.sem("z_summed"), t.sem("z_added"), t.sem("stats_ready")
        else:
            yb_ready = t.sem("yb_ready")
        block = ctx.enter_context(nc.Block())
        NC = 7 if first else 8

        def all_tiles(step, engine):
            for r in range(R):
                step(r, 0, r, True)
            with engine.Fori(1, NT // R) as i:
                for r in range(R):
                    step(R * i + r, i, r, False)
            for r in range(NT % R):
                step(NT - NT % R + r, NT // R, r, False)

        def left(tile):
            return NT - 1 - tile if isinstance(tile, int) else 3

        @block.sync
        def _(sp):
            loads = [(router[:, :], w[f"router{layer}"]), (iota[:, :], w["iota"].partition_broadcast(128)),
                     (iota_tile[:, :], w["iota_tile"][0:NT].partition_broadcast(128)),
                     (edges[:, :], w["edges"].partition_broadcast(128)), (before[:, :], w["before"]),
                     (earlier[:, :, :], w["earlier"].partition_broadcast(128)), (ids[:, :, :], w["ids"][:, 0:PICKS, :])]
            if not first:
                loads += [(router_b[:, :], w["router_b1"].partition_broadcast(128))]
            for dst, src in loads:
                sp.dma_start(dst, src).then_inc(consts, 16)
            if first:
                sp.dma_start(sup[:, :], w["shared_up"]).then_inc(shared_in, 16)
                sp.dma_start(sdown[:, :, :], w["shared_down"]).then_inc(shared_in, 16)
                for dst, src in [(wqT[:, :, :], w["wqT1"]), (wkT[:, :, :], w["wkT1"])]:
                    sp.dma_start(dst, src).then_inc(qk_in, 16)
                sp.dma_start(ctxT[:, :, :], w["ctxT"][0:EARLY].rearrange("b d s -> d b s")).then_inc(ctx_in, 16)
                for dst, src in [(k.wv1[:, :], w["wv1"]), (k.wo1[:, :, :], w["wo1"]),
                                 (k.bo1[:, :], w["bo1"].partition_broadcast(128)), (k.causal[:, :], w["causal"]),
                                 (k.hidden[:, :, :], w["mask"].partition_broadcast(128))]:
                    sp.dma_start(dst, src).then_inc(k.att1_in, 16)
            sp.wait_ge(scattered, 16 * PICKS * B)

            def load(tile, i, r, is_first):
                if not is_first:
                    sp.wait_ge(tile_out[r], 16 * i)
                sp.dma_start(xin[r][:, :], slots_dram[tile]).then_inc(tile_in[r], 16)

            all_tiles(load, sp)
            for r in range(R):
                sp.wait_ge(tile_out[r], 16 * len(range(r, NT, R)))
            if first:
                for g in range(GROUPS):
                    for p in range(PICKS):
                        src = out_dram[p * B + GB * g:p * B + GB * g + GB].rearrange("b s d -> s b d")
                        sp.dma_start(z[:, p, GB * g:GB * g + GB, :], src).then_inc(z_in[g], 16)

        @block.tensor
        def _(pe):
            def turn_group(g):
                if g >= 2:
                    pe.wait_ge(xT_ready, g - 1)
                for s in range(GB):
                    b = GB * g + s
                    pe.wait_ge(rows_ready, b + 1)
                    mm = nc.tensor.transpose(first_tr_ps[g % 2][:, S * s:S * s + S], rowbuf[0][:, b, 0:D], k.ident[:, :])
                mm.then_inc(xnT_made, 1)

            def logits(g):
                pe.wait_ge(xT_ready, g + 1)
                for b in range(GB * g, GB * g + GB):
                    mm = nc.tensor.matmul(lg_ps[:, b, :], xT[:, b, :], router[:, :], start=True, stop=True)
                mm.then_inc(lg_made, 1)

            pe.wait_ge(consts, 16 * NC)
            turn_group(0)
            for g in range(GROUPS):
                if g + 1 < GROUPS:
                    turn_group(g + 1)
                logits(g)

            def shared_up(g, chunks=range(FC)):
                pe.wait_ge(xT_ready, g + 1)
                for c in chunks:
                    if g:
                        pe.wait_ge(sh_ready, FC * (g - 1) + c + 1)
                    nc.tensor.matmul(sup_ps[c][:, :], sup[:, 128 * c:128 * c + 128],
                                     xT[:, GB * g:GB * g + GB, :].rearrange("p a b -> p (a b)"),
                                     start=True, stop=True).then_inc(sup_made, 1)

            def shared_down(g):
                pe.wait_ge(sh_ready, FC * (g + 1))
                if g >= 2:
                    pe.wait_ge(sdn_taken, g - 1)
                for s in range(GB):
                    for c in range(FC):
                        mm = nc.tensor.matmul(sdn_ps[g % 2][:, 128 * s:128 * s + 128], shT[g % 2][:, c, S * s:S * s + S],
                                              sdown[:, c, :], start=(c == 0), stop=(c == FC - 1))
                mm.then_inc(sdn_made, 1)

            def ranks():
                pe.wait_ge(uses_ready, 1)
                pe.wait_ge(counts16_ready, 2)
                u = uses[:, :, :].rearrange("p b e -> p (b e)")
                nc.tensor.matmul(count_ps, ones16[:, :], u, start=True, stop=True).then_inc(counted, 1)
                nc.tensor.matmul(rank_ps, before16[:, :], u, start=True, stop=False)
                for back in range(1, B):
                    mm = nc.tensor.matmul(rank_ps[:, back * E:], ones16[:, :], u[:, 0:(B - back) * E], start=False, stop=(back == B - 1))
                mm.then_inc(rank_made, 1)

            if first:
                pe.wait_ge(shared_in, 32)
                shared_up(0)
                shared_up(1, range(FC // 2))
                ranks()
                shared_up(1, range(FC // 2, FC))
                shared_down(0)
                pe.wait_ge(slots_ready, PICKS)
                for g in range(1, GROUPS):
                    if g + 1 < GROUPS:
                        shared_up(g + 1)
                    shared_down(g)
                pe.wait_ge(qk_in, 32)
                for u in range(U):
                    for hh in range(G):
                        mm = nc.tensor.matmul(sup_ps[u][:, D * hh:D * hh + D], wqT[:, G * u + hh, :], wkT[:, G * u + hh, :],
                                              start=True, stop=True)
                    mm.then_inc(wqk_made, 1)
                pe.wait_ge(ctx_in, 16)
                pe.wait_ge(k.att1_in, 16 * 5)
                for n in range(2 * EARLY):
                    b, half = divmod(n, 2)
                    pe.wait_ge(k.wqk_ready, n + 1) if n < U else pe.wait_ge(k.v1_ready, n - U + 1)
                    nc.tensor.matmul(sup_ps[n % U][:, :], ctxT[:, b, :], k.wv1[:, 512 * half:512 * half + 512],
                                     start=True, stop=True).then_inc(v1_made, 1)
                pe.wait_ge(k.v1_ready, 2 * EARLY)
                pe.wait_ge(sdn_taken, GROUPS)
            else:
                ranks()
            pe.wait_ge(plan_ready, 1)
            pe.wait_ge(k.w_in[layer], 32 * E)

            def turn_x(tile, i, r):
                pe.wait_ge(tile_in[r], 16 * (i + 1))
                if not (isinstance(tile, int) and tile == 0):
                    pe.wait_ge(xt_ready, tile)
                nc.tensor.transpose(tr_ps, xin[r][:, 0:D], k.ident[:, :]).then_inc(xt_made, 1)

            def expert_of(tile):
                at = tile_i[0:1, tile:tile + 1] if isinstance(tile, int) else tile_i[0:1, bass.ds(tile, 1)]
                return pe.value_load(at, min_val=0, max_val=E - 1)

            def up(tile, r):
                pe.wait_ge(xt_ready, tile + 1)
                pe.wait_ge(upw_ready, tile + 1)
                if not (isinstance(tile, int) and tile < 4):
                    pe.wait_ge(hT_ready, tile - 3)
                for c in range(FC):
                    mm = nc.tensor.matmul(up_ps[r % 4][:, 128 * c:128 * c + 128], upw[r % 4][:, 128 * c:128 * c + 128],
                                          xt[r % 2][:, :], start=True, stop=True)
                mm.then_inc(up_made, 1)

            def down(tile, r):
                e = expert_of(tile)
                pe.wait_ge(hT_ready, tile + 1)
                if not (isinstance(tile, int) and tile < 2):
                    pe.wait_ge(y_ready, tile - 1)
                for c in range(FC):
                    mm = nc.tensor.matmul(y_ps[r % 2][:, 0:D], hT[r % 2][:, c, :], k.wdn[:, e, c, :], start=(c == 0), stop=(c == FC - 1))
                mm.then_inc(y_made, 1)

            def step(tile, i, r, is_first):
                if left(tile) >= 3:
                    turn_x(tile + 3, i + (r + 3) // R, (r + 3) % R)
                if left(tile) >= 2:
                    up(tile + 2, r + 2)
                down(tile, r)

            for r in range(3):
                turn_x(r, 0, r)
                if r < 2:
                    up(r, r)
            all_tiles(step, pe)

        @block.scalar
        def _(act):
            if not first:
                nc.scalar.activation(rowbuf[0][:, :, D + 1:], k.x[:, :, :], ACT.Copy).then_inc(tails_ready, 1)
            for g in range(GROUPS):
                act.wait_ge(xnT_made, g + 1)
                nc.scalar.activation(xT[:, GB * g:GB * g + GB, :].rearrange("p b s -> p (b s)"), first_tr_ps[g % 2][:, :],
                                     ACT.Copy).then_inc(xT_ready, 1)
            if first:
                act.wait_ge(rows_ready, B)
                nc.scalar.activation(rowbuf[1][:, :, 0:D], rowbuf[0][:, :, 0:D], ACT.Copy).then_inc(copied, 1)
            act.wait_ge(shifted, 1)
            nc.scalar.activation(pr[:, :, :], pr[:, :, :], ACT.Exp).then_inc(e_ready, 1)
            if not first:
                act.wait_ge(weight_ready, 1)
                for b in range(B):
                    nc.scalar.activation(rowbuf[0][:, b, 0:D], rowbuf[0][:, b, 0:D], ACT.Copy,
                                         scale=weight[:, b:b + 1]).then_inc(weighted, 1)
            if first:
                for g in range(GROUPS):
                    if g >= 2:
                        act.wait_ge(sdn_made, g - 1)
                    for c in range(FC):
                        act.wait_ge(sup_made, FC * g + c + 1)
                        nc.scalar.activation(shT[g % 2][:, c, :], sup_ps[c][:, :], ACT.Gelu).then_inc(sh_ready, 1)
                for u in range(U):
                    act.wait_ge(wqk_made, u + 1)
                    nc.scalar.activation(k.wqk[:, G * u:G * u + G, :].rearrange("p h d -> p (h d)"), sup_ps[u][:, :],
                                         ACT.Copy).then_inc(k.wqk_ready, 1)
                for n in range(2 * EARLY):
                    b, half = divmod(n, 2)
                    act.wait_ge(v1_made, n + 1)
                    nc.scalar.activation(k.v1[:, b, 512 * half:512 * half + 512], sup_ps[n % U][:, :],
                                         ACT.Copy).then_inc(k.v1_ready, 1)

            def take_x(tile, r):
                act.wait_ge(xt_made, tile + 1)
                if not (isinstance(tile, int) and tile < 2):
                    act.wait_ge(up_made, tile - 1)
                nc.scalar.activation(xt[r % 2][:, :], tr_ps, ACT.Copy).then_inc(xt_ready, 1)

            def hidden(tile, r):
                if not first:
                    act.wait_ge(upb_ready, tile + 1)
                act.wait_ge(up_made, tile + 1)
                if not (isinstance(tile, int) and tile < 2):
                    act.wait_ge(y_made, tile - 1)
                if first:
                    nc.scalar.activation(hT[r % 2][:, :, :].rearrange("p c s -> p (c s)"), up_ps[r % 4][:, :],
                                         ACT.Gelu).then_inc(hT_ready, 1)
                    return
                for c in range(FC):
                    last = nc.scalar.activation(hT[r % 2][:, c, :], up_ps[r % 4][:, 128 * c:128 * c + 128], ACT.Relu,
                                                bias=upb[r % 4][:, c:c + 1])
                last.then_inc(hT_ready, 1)

            def step(tile, i, r, is_first):
                if left(tile) >= 3:
                    take_x(tile + 3, r + 3)
                if left(tile) >= 1:
                    hidden(tile + 1, r + 1)

            for r in range(3):
                take_x(r, r)
            hidden(0, 0)
            all_tiles(step, act)

        @block.gpsimd
        def _(pool):
            pool.wait_ge(var_ready, 1)
            invert_std(nc, k, rstd_ready)
            pool.wait_ge(consts, 16 * NC)
            for p in range(PICKS):
                nc.gpsimd.tensor_copy(rowbuf[p][:, :, D].bitcast(I32), ids[:, p, :]).then_inc(ids_set, 1)
            nc.gpsimd.memset(ones16[:, :], 1.0).then_inc(counts16_ready, 1)
            nc.gpsimd.tensor_copy(before16[:, :], before[:, :]).then_inc(counts16_ready, 1)
            pool.wait_ge(ids_set, PICKS)
            pool.wait_ge(k.slots_set, 16 * (E + 1) * (layer + 1))
            for p in range(PICKS):
                pool.wait_ge(slots_ready, p + 1)
                pool.wait_ge(tails_ready, 1)
                if first:
                    pool.wait_ge(copied, p) if p else pool.wait_ge(rows_ready, B)
                for b in range(B):
                    if not first:
                        pool.wait_ge(weighted, b + 1)
                    nc.gpsimd.indirect_dma_start(slots_dram.rearrange("t s c -> (t s) c"),
                                                 bass.IndirectOffsetOnAxis(slot[p][:, b:b + 1], 0),
                                                 rowbuf[p][:, b, :], None).then_inc(scattered, 16)

            def put(tile, i, r, is_first):
                pool.wait_ge(y_ready, tile + 1)
                pool.wait_ge(tile_in[r], 16 * (i + 1))
                pool.sem_inc(puts_begun, 1)
                nc.gpsimd.indirect_dma_start(out_dram.rearrange("b s d -> (b s) d"),
                                             bass.IndirectOffsetOnAxis(xin[r][:, D:D + 1].bitcast(I32), 0),
                                             y[r][:, :], None).then_inc(tile_out[r], 16)

            all_tiles(put, pool)
            if first:
                for g in range(GROUPS):
                    pool.wait_ge(z_in[g], 32)
                    own = slice(GB * g, GB * g + GB)
                    nc.gpsimd.tensor_tensor(z[:, 0, own, :], z[:, 0, own, :], z[:, 1, own, :], ALU.add).then_inc(z_summed, 1)

        @block.vector
        def _(dve):
            V = nc.vector
            norm_stats(nc, dve, k, norm_own, var_ready)
            with dve.Fori(0, GROUPS) as g:
                dve.wait_ge(rstd_ready, g + 1)
                for s in range(GB):
                    b = GB * g + s
                    V.tensor_scalar(rowbuf[0][:, b, 0:D], k.x[:, b, :], k.mean[:, bass.ds(b, 1)], k.rstd[:, bass.ds(b, 1)],
                                    ALU.subtract, ALU.mult).then_inc(rows_ready, 1)

            made = [0]

            def step(ins):
                made[0] += 1
                ins.then_inc(own, 1)
                dve.wait_ge(own, made[0])

            dve.wait_ge(lg_made, GROUPS)
            dve.wait_ge(consts, 16 * NC)
            it = rows(iota[:, :], B)
            lg = lg_ps
            if not first:
                step(V.tensor_tensor(pr[:, :, :], lg_ps, rows(router_b[:, :], B), ALU.add))
                lg = pr[:, :, :]
            step(V.tensor_reduce(top[:, :], lg, AX, ALU.max))
            V.tensor_tensor(pr[:, :, :], lg, wide(top[:, :], E), ALU.subtract).then_inc(shifted, 1)
            dve.wait_ge(e_ready, 1)
            step(V.tensor_reduce(total[:, :], pr[:, :, :], AX, ALU.add))
            step(V.reciprocal(total[:, :], total[:, :]))
            step(V.tensor_tensor(pr[:, :, :], pr[:, :, :], wide(total[:, :], E), ALU.mult))

            def pick(prob, m, idx, onehot):
                step(V.tensor_reduce(m[:, :], prob, AX, ALU.max))
                step(V.tensor_tensor(tmp[:, :, :], prob, wide(m[:, :], E), ALU.is_lt))
                step(V.scalar_tensor_tensor(out=tmp[:, :, :], in0=tmp[:, :, :], scalar=float(E), in1=it, op0=ALU.mult, op1=ALU.add))
                step(V.tensor_reduce(idx[:, :], tmp[:, :, :], AX, ALU.min))
                step(V.tensor_tensor(onehot, it, wide(idx[:, :], E), ALU.is_equal))

            pick(pr[:, :, :], m1, i1, o1[:, :, :])
            step(V.scalar_tensor_tensor(out=o2[:, :, :], in0=o1[:, :, :], scalar=-2.0, in1=pr[:, :, :], op0=ALU.mult, op1=ALU.add))
            pick(o2[:, :, :], m2, i2, o2[:, :, :])
            if first:
                V.tensor_tensor(uses[:, :, :], o1[:, :, :], o2[:, :, :], ALU.add).then_inc(uses_ready, 1)
                V.tensor_scalar(rowbuf[0][:, :, D + 1], m1[:, :], tg, None, ALU.mult)
                V.tensor_scalar(rowbuf[1][:, :, D + 1], m2[:, :], tg, None, ALU.mult).then_inc(tails_ready, 1)
            else:
                step(V.tensor_scalar(i2[:, :], i2[:, :], 1.0, None, ALU.add))
                step(V.tensor_scalar(top[:, :], m2[:, :], 0.0, None, ALU.is_gt))
                step(V.tensor_tensor(i2[:, :], i2[:, :], top[:, :], ALU.mult))
                step(V.scalar_tensor_tensor(out=i1[:, :], in0=i2[:, :], scalar=-1.0, in1=i1[:, :], op0=ALU.add, op1=ALU.max))
                V.tensor_tensor(uses[:, :, :], it, wide(i1[:, :], E), ALU.is_equal).then_inc(uses_ready, 1)
                dve.wait_ge(uses_ready, 1)
                step(V.tensor_tensor(o2[:, :, :], uses[:, :, :], pr[:, :, :], ALU.mult))
                V.tensor_reduce(weight[:, :], o2[:, :, :], AX, ALU.add).then_inc(weight_ready, 1)

            dve.wait_ge(counted, 1)
            step(V.tensor_reduce(uses_of[:, :], count_ps.rearrange("p (b e) -> p e b", e=E), AX, ALU.add))
            step(V.tensor_tensor(tmp[:, :, :].rearrange("p b e -> p e b"), wide(uses_of[:, :], B), rows(edges[:, :], E), ALU.is_gt))
            step(V.tensor_reduce(tiles[:, :], tmp[:, :, :].rearrange("p b e -> p e b"), AX, ALU.add))
            step(V.tensor_tensor(tiles_before[:, :, :], rows(tiles[:, :], E), earlier[:, :, :], ALU.mult))
            step(V.tensor_reduce(starts[:, :], tiles_before[:, :, :], AX, ALU.add))
            dve.wait_ge(rank_made, 1)
            step(V.scalar_tensor_tensor(out=tmp[:, :, :], in0=rows(starts[:, :], B), scalar=128.0,
                                        in1=rank_ps.rearrange("p (b e) -> p b e", e=E), op0=ALU.mult, op1=ALU.add))
            for p in range(PICKS):
                onehot = (o1 if p == 0 else o2) if first else uses
                step(V.tensor_tensor(pr[:, :, :], onehot[:, :, :], tmp[:, :, :], ALU.mult))
                step(V.tensor_reduce(top[:, :], pr[:, :, :], AX, ALU.add))
                V.tensor_copy(slot[p][:, :], top[:, :]).then_inc(slots_ready, 1)
                dve.wait_ge(slots_ready, p + 1)
            step(V.tensor_tensor(ends[:, :], starts[:, :], tiles[:, :], ALU.add))
            step(V.tensor_tensor(at[:, :, :], rows(ends[:, :], NT), wide(iota_tile[:, :], E), ALU.is_le))
            step(V.tensor_reduce(tile_e[:, :], at[:, :, :], AX, ALU.add))
            V.tensor_scalar(tile_i[:, :], tile_e[:, :], float(E - 1), None, ALU.min).then_inc(plan_ready, 1)

            if first:
                V.scalar_tensor_tensor(out=k.x[:, :, :], in0=rowbuf[0][:, :, 0:D], scalar=tg, in1=k.x[:, :, :],
                                       op0=ALU.mult, op1=ALU.add).then_inc(norm_own, 1)
                dve.wait_ge(norm_own, 7)
                for g in range(GROUPS):
                    dve.wait_ge(sdn_made, g + 1)
                    xg = k.x[:, GB * g:GB * g + GB, :]
                    V.scalar_tensor_tensor(out=xg, in0=sdn_ps[g % 2][:, :].rearrange("p (b d) -> p b d", d=D), scalar=tg,
                                           in1=xg, op0=ALU.mult, op1=ALU.add).then_inc(sdn_taken, 1)
            dve.wait_ge(plan_ready, 1)
            dve.wait_ge(k.w_in[layer], 32 * E)
            if not first:
                dve.wait_ge(k.bias_in, 32)

            def expert_of(tile):
                at = tile_i[0:1, tile:tile + 1] if isinstance(tile, int) else tile_i[0:1, bass.ds(tile, 1)]
                return dve.value_load(at, min_val=0, max_val=E - 1)

            def fetch(tile, r):
                e = expert_of(tile)
                if not (isinstance(tile, int) and tile < 4):
                    dve.wait_ge(hT_ready, tile - 3)
                if not first:
                    V.tensor_scalar(upb[r % 4][:, :], k.b1[:, e, :], 1.0, None, ALU.mult).then_inc(upb_ready, 1)
                V.tensor_scalar(upw[r % 4][:, :], k.wup[:, e, :], 1.0, None, ALU.mult).then_inc(upw_ready, 1)

            def take_y(tile, i, r, is_first):
                if not first:
                    e = expert_of(tile)
                dve.wait_ge(y_made, tile + 1)
                if not is_first:
                    dve.wait_ge(tile_out[r], 16 * i)
                if first:
                    dve.wait_ge(tile_in[r], 16 * (i + 1))
                    V.tensor_scalar(y[r][:, :], y_ps[r % 2][:, 0:D], xin[r][:, D + 1:D + 2], None, ALU.mult).then_inc(y_ready, 1)
                else:
                    V.tensor_tensor(yb[r % 2][:, :], y_ps[r % 2][:, 0:D], k.b2[:, e, :], ALU.add).then_inc(yb_ready, 1)
                    dve.wait_ge(yb_ready, tile + 1)
                    dve.wait_ge(tile_in[r], 16 * (i + 1))
                    V.scalar_tensor_tensor(out=y[r][:, :], in0=yb[r % 2][:, :], scalar=tg, in1=xin[r][:, D + 1:],
                                           op0=ALU.mult, op1=ALU.add).then_inc(y_ready, 1)

            def tile_step(tile, i, r, is_first):
                if left(tile) >= 3:
                    fetch(tile + 3, r + 3)
                take_y(tile, i, r, is_first)

            for r in range(3):
                fetch(r, r)
            all_tiles(tile_step, dve)
            if first:
                dve.wait_ge(sdn_taken, GROUPS)
                for g in range(GROUPS):
                    xg = k.x[:, GB * g:GB * g + GB, :]
                    dve.wait_ge(z_summed, g + 1)
                    V.tensor_tensor(xg, z[:, 0, GB * g:GB * g + GB, :], xg, ALU.add).then_inc(z_added, 1)
                    dve.wait_ge(z_added, g + 1)
                    for b in range(GB * g, GB * g + GB):
                        V.bn_stats(k.stats[:, b, :], k.x[:, b, :]).then_inc(stats_ready, 1)


class Kept:
    pass


def flamingo(nc, w):
    with ExitStack() as ctx:
        t = Tools(nc, ctx, "kept", [])
        k = Kept()
        k.used = []
        k.x = t.sb("x", [128, B, D])
        k.base = t.sb("base", [128, B, D])
        k.ident = t.sb("ident", [128, 128])
        k.graw = t.sb("graw", [128, 4])
        k.tg = t.sb("tg", [128, 4])
        k.half = t.sb("half", [128, B])
        k.stats = t.sb("stats", [128, B, 6])
        k.mean, k.diff, k.var, k.rstd = (t.sb(n, [128, B]) for n in ("mean", "diff", "var", "rstd"))
        k.wq0, k.wk0, k.wv0, k.bo0 = (t.sb(n, [128, D]) for n in ("wq0", "wk0", "wv0", "bo0"))
        k.wo0 = t.sb("wo0", [128, 1, D])
        k.bqkv0, k.headmask = t.sb("bqkv0", [128, 3]), t.sb("headmask", [128, G])
        k.att0_in = t.sem("att0_in")
        k.wo1, k.bo1 = t.sb("wo1", [128, INNER // 128, D]), t.sb("bo1", [128, D])
        k.wv1 = t.sb("wv1", [128, INNER])
        k.wqk = t.sb("wqk", [128, HEADS, D])
        k.causal = t.sb("causal", [128, S])
        k.hidden = t.sb("hidden", [128, B, S], U8)
        k.v1 = t.sb("v1", [128, EARLY, INNER])
        k.att1_in, k.wqk_ready, k.v1_ready = t.sem("att1_in"), t.sem("wqk_ready"), t.sem("v1_ready")
        k.wup = t.sb("wup", [128, E, F])
        k.wdn = t.sb("wdn", [128, E, FC, D])
        k.b1, k.b2 = t.sb("b1", [128, E, FC]), t.sb("b2", [128, E, D])
        k.w_in = [t.sem(f"w_in{i}") for i in range(2)]
        k.bias_in = t.sem("bias_in")
        k.slots = [nc.dram_tensor(f"slots{i}", (NTILES[i], 128, ROWS[i]), F32, kind="Internal").ap() for i in range(2)]
        k.outs = [nc.dram_tensor("outs0", (2 * B + NTILES[0], S, D), F32, kind="Internal").ap(), w["out"]]
        k.slots_set = t.sem("slots_set")
        start_phase(nc, k, w)
        for layer in range(2):
            attention_phase(nc, k, w, layer)
            experts_phase(nc, k, w, layer)


def kernel(x, ctx_1024, mask_BxS2_bf0, g_xattn, g_ffn, L0_xattn_Wq, L0_xattn_bq, L0_xattn_Wk, L0_xattn_bk,
           L0_xattn_Wv, L0_xattn_bv, L0_xattn_Wo, L0_xattn_bo, L0_ffn_shared_up, L0_ffn_shared_down,
           L0_ffn_routed_up, L0_ffn_routed_down, L0_ffn_router_w, L1_xattn_Wq, L1_xattn_Wk, L1_xattn_Wv,
           L1_xattn_Wo, L1_xattn_bo, L1_ffn_gate_w, L1_ffn_gate_b, L1_ffn_w1, L1_ffn_b1, L1_ffn_w2, L1_ffn_b2):
    import concourse.bacc as bacc
    from concourse.bass_utils import run_bass_kernel_spmd

    def a(v):
        return np.asarray(v)

    head = np.arange(128) // DK % G
    padding = [np.zeros((n, 128, row), np.int32) for n, row in zip(NTILES, ROWS)]
    for layer in range(2):
        padding[layer][:, :, D] = (2 - layer) * B * S + np.arange(128 * NTILES[layer]).reshape(-1, 128)
    data = {
        "xr": a(x).transpose(1, 0, 2),
        "ctxT": a(ctx_1024).transpose(0, 2, 1),
        "mask": a(mask_BxS2_bf0),
        "g_xattn": a(g_xattn), "g_ffn": a(g_ffn),
        "ident": np.eye(128, dtype=np.float32),
        "headmask": (head[:, None] == np.arange(G)[None]).astype(np.float32),
        "causal": np.where(np.arange(S)[None] > np.arange(S)[:, None], np.float32(FMAX), np.float32(0)),
        "iota": np.arange(E, dtype=np.float32),
        "wq0": a(L0_xattn_Wq).T, "wk0": a(L0_xattn_Wk).T, "wv0": a(L0_xattn_Wv).T,
        "bqkv0": np.stack([a(L0_xattn_bq), a(L0_xattn_bk), a(L0_xattn_bv)], 1),
        "wo0": a(L0_xattn_Wo).T[:, None], "bo0": a(L0_xattn_bo),
        "wqT1": a(L1_xattn_Wq).reshape(D, HEADS, DH).transpose(2, 1, 0),
        "wkT1": a(L1_xattn_Wk).reshape(D, HEADS, DH).transpose(2, 1, 0),
        "wv1": a(L1_xattn_Wv),
        "wo1": a(L1_xattn_Wo).reshape(INNER // 128, 128, D).transpose(1, 0, 2), "bo1": a(L1_xattn_bo),
        "router0": a(L0_ffn_router_w), "router1": a(L1_ffn_gate_w).T, "router_b1": a(L1_ffn_gate_b),
        "shared_up": a(L0_ffn_shared_up)[0],
        "shared_down": a(L0_ffn_shared_down)[0].reshape(FC, 128, D).transpose(1, 0, 2),
        "up0": a(L0_ffn_routed_up).transpose(1, 0, 2),
        "down0": a(L0_ffn_routed_down).reshape(E, FC, 128, D).transpose(2, 0, 1, 3),
        "up1": a(L1_ffn_w1).transpose(2, 0, 1),
        "down1": a(L1_ffn_w2).transpose(0, 2, 1).reshape(E, FC, 128, D).transpose(2, 0, 1, 3),
        "b1": a(L1_ffn_b1).reshape(E, FC, 128).transpose(2, 0, 1), "b2": a(L1_ffn_b2),
        "iota_tile": np.arange(max(NTILES), dtype=np.float32),
        "edges": 128 * np.arange(B, dtype=np.float32),
        "before": (np.arange(128)[:, None] < np.arange(128)[None]).astype(np.float32),
        "earlier": (np.arange(E)[None] < np.arange(E)[:, None]).astype(np.float32),
        "ids": (np.arange(S)[:, None, None] + 128 * (np.arange(2)[None, :, None] * B + np.arange(B)[None, None])).astype(np.int32),
        "padding0": padding[0], "padding1": padding[1],
    }
    nc = bacc.Bacc("TRN2", target_bir_lowering=False, num_devices=1)
    arrays, w = {}, {}
    for name, v in data.items():
        v = np.ascontiguousarray(v)
        arrays[f"in_{name}"] = v
        w[name] = nc.dram_tensor(f"in_{name}", v.shape, mybir.dt.from_np(v.dtype), kind="ExternalInput").ap()
    w["out"] = nc.dram_tensor("out", (B + NTILES[1], S, D), F32, kind="ExternalOutput").ap()
    flamingo(nc, w)
    r = run_bass_kernel_spmd(nc, [arrays], core_ids=[0])
    return np.ascontiguousarray(r.results[0]["out"][:B])
```
